# Optimizing a Trainium2 kernel written in Bass

```python
import numpy as np
import jax
import jax.numpy as jnp

def _softmax(x, axis=-1):
    return jax.nn.softmax(x, axis=axis)

def _gelu(x):
    return jax.nn.gelu(x, approximate=True)

def _silu(x):
    return jax.nn.silu(x)

def _sigmoid(x):
    return jax.nn.sigmoid(x)

def _layernorm(x, axis=-1, eps=1e-05):
    m = jnp.mean(x, axis=axis, keepdims=True)
    v = jnp.var(x, axis=axis, keepdims=True)
    return (x - m) / jnp.sqrt(v + eps)

def _scatter_add(tgt, idx, src, axis=0):
    return tgt.at[idx].add(src)

def _segment_sum(src, seg, n):
    return jax.ops.segment_sum(src, seg, n)
kernel_name = 'mk_decoder_postln_d1_seqx_r8_f50fb1'

def setup_inputs(seed: int=0):
    np.random.seed(seed)
    _w = jnp.asarray

    def _rec_inputs():
        import jax
        import jax.numpy as jnp
        _rk = jax.random.key(seed)
        x = 7.22e-05 + 1 * jax.random.normal(jax.random.fold_in(_rk, 1), (32, 64, 256), jnp.float32)
        _lenS = 64 - jax.random.randint(jax.random.fold_in(_rk, 7), (32,), 0, max(1, 64 // 4) + 1, jnp.int32)
        _lenS2 = 64 - jax.random.randint(jax.random.fold_in(_rk, 8), (32,), 0, max(1, 64 // 4) + 1, jnp.int32)
        _ctx_512P = jax.random.normal(jax.random.fold_in(_rk, 11), (32, 16, 64), jnp.float32)
        _ctx_512c = jax.random.dirichlet(jax.random.fold_in(_rk, 511), 0.3 * jnp.ones((16,), jnp.float32), (32, 64))
        _ctx_512t = jnp.einsum('bsk,bkd->bsd', _ctx_512c, _ctx_512P)
        _ctx_512t = _ctx_512t * jax.lax.rsqrt(jnp.mean(jnp.square(_ctx_512t)) + 1e-12) * 0.953939
        ctx_512 = -0.000514642 + 1.00011 * (_ctx_512t + 0.3 * jax.random.normal(jax.random.fold_in(_rk, 611), (32, 64, 64), jnp.float32))
        return (x, ctx_512)
    x, ctx_512 = _rec_inputs()

    def _L0_attn_setup():
        import jax, jax.numpy as jnp
        import numpy as np
        D_MODEL = 256
        N_HEADS = 16
        D_K = D_MODEL // N_HEADS
        EPS = 1e-06
        key = jax.random.key(seed)
        ks = jax.random.split(key, 9)
        s = 1.0 / np.sqrt(D_MODEL)
        return {'x': jax.random.normal(ks[0], (4, 512, D_MODEL), dtype=jnp.float32), 'Wq': jax.random.normal(ks[1], (D_MODEL, D_MODEL), dtype=jnp.float32) * s, 'bq': jnp.zeros((D_MODEL,), dtype=jnp.float32), 'Wk': jax.random.normal(ks[2], (D_MODEL, D_MODEL), dtype=jnp.float32) * s, 'bk': jnp.zeros((D_MODEL,), dtype=jnp.float32), 'Wv': jax.random.normal(ks[3], (D_MODEL, D_MODEL), dtype=jnp.float32) * s, 'bv': jnp.zeros((D_MODEL,), dtype=jnp.float32), 'Wo': jax.random.normal(ks[4], (D_MODEL, D_MODEL), dtype=jnp.float32) * s, 'bo': jnp.zeros((D_MODEL,), dtype=jnp.float32)}
    _L0_attn_all = _L0_attn_setup()
    _L0_attn_in = {k: v for k, v in _L0_attn_all.items() if k in ('Wq', 'bq', 'Wk', 'bk', 'Wv', 'bv', 'Wo', 'bo')}
    del _L0_attn_all

    def _L0_xattn_setup():
        import jax, jax.numpy as jnp
        import numpy as np
        import math
        D_MODEL = 256
        N_HEADS = 16
        N_GROUPS = 4
        HEADS_PER_GROUP = N_HEADS // N_GROUPS
        HEAD_DIM = D_MODEL // N_HEADS
        B, S = (2, 256)
        key = jax.random.key(seed)
        k1, k2, k3, k4, k5 = jax.random.split(key, 5)
        q = jax.random.normal(k1, (B, S, D_MODEL), dtype=jnp.float32)
        k = jax.random.normal(k2, (B, S, N_GROUPS * HEAD_DIM), dtype=jnp.float32)
        v = jax.random.normal(k3, (B, S, N_GROUPS * HEAD_DIM), dtype=jnp.float32)
        lim = 1.0 / math.sqrt(D_MODEL)
        Wc = jax.random.uniform(k4, (D_MODEL, D_MODEL), minval=-lim, maxval=lim, dtype=jnp.float32)
        bc = jax.random.uniform(k5, (D_MODEL,), minval=-lim, maxval=lim, dtype=jnp.float32)
        return {'q': q, 'k': k, 'v': v, 'Wc': Wc, 'bc': bc}
    _L0_xattn_all = _L0_xattn_setup()
    _L0_xattn_in = {k: v for k, v in _L0_xattn_all.items() if k in ('Wc', 'bc')}
    del _L0_xattn_all

    def _L0_ffn_setup():
        import jax, jax.numpy as jnp
        import numpy as np
        B, S, H = (2, 256, 256)
        E, K = (16, 4)
        I_MOE, I_SH = (176, 704)
        key = jax.random.key(seed)
        ks = jax.random.split(key, 9)

        def w(k, shape, fan_in):
            return jax.random.normal(k, shape, jnp.float32) * fan_in ** (-0.5)
        return {'hidden_states': jax.random.normal(ks[0], (B, S, H), jnp.float32), 'router_w': w(ks[1], (E, H), H), 'w_gate': w(ks[2], (E, H, I_MOE), H), 'w_up': w(ks[3], (E, H, I_MOE), H), 'w_down': w(ks[4], (E, I_MOE, H), I_MOE), 'sh_gate': w(ks[5], (H, I_SH), H), 'sh_up': w(ks[6], (H, I_SH), H), 'sh_down': w(ks[7], (I_SH, H), I_SH), 'sh_gate_w': w(ks[8], (H, 1), H)}
    _L0_ffn_all = _L0_ffn_setup()
    _L0_ffn_in = {k: v for k, v in _L0_ffn_all.items() if k in ('router_w', 'w_gate', 'w_up', 'w_down', 'sh_gate', 'sh_up', 'sh_down', 'sh_gate_w')}
    del _L0_ffn_all
    return {'x': x, 'ctx_512': ctx_512, 'L0_attn_Wq': _L0_attn_in['Wq'], 'L0_attn_bq': _L0_attn_in['bq'], 'L0_attn_Wk': _L0_attn_in['Wk'], 'L0_attn_bk': _L0_attn_in['bk'], 'L0_attn_Wv': _L0_attn_in['Wv'], 'L0_attn_bv': _L0_attn_in['bv'], 'L0_attn_Wo': _L0_attn_in['Wo'], 'L0_attn_bo': _L0_attn_in['bo'], 'L0_xattn_Wc': _L0_xattn_in['Wc'], 'L0_xattn_bc': _L0_xattn_in['bc'], 'L0_ffn_router_w': _L0_ffn_in['router_w'], 'L0_ffn_w_gate': _L0_ffn_in['w_gate'], 'L0_ffn_w_up': _L0_ffn_in['w_up'], 'L0_ffn_w_down': _L0_ffn_in['w_down'], 'L0_ffn_sh_gate': _L0_ffn_in['sh_gate'], 'L0_ffn_sh_up': _L0_ffn_in['sh_up'], 'L0_ffn_sh_down': _L0_ffn_in['sh_down'], 'L0_ffn_sh_gate_w': _L0_ffn_in['sh_gate_w']}

def reference(x, ctx_512, L0_attn_Wq, L0_attn_bq, L0_attn_Wk, L0_attn_bk, L0_attn_Wv, L0_attn_bv, L0_attn_Wo, L0_attn_bo, L0_xattn_Wc, L0_xattn_bc, L0_ffn_router_w, L0_ffn_w_gate, L0_ffn_w_up, L0_ffn_w_down, L0_ffn_sh_gate, L0_ffn_sh_up, L0_ffn_sh_down, L0_ffn_sh_gate_w):
    import jax
    import jax.numpy as jnp

    def _L0_attn_ref(x, Wq, bq, Wk, bk, Wv, bv, Wo, bo):
        import jax, jax.numpy as jnp
        import numpy as np
        D_MODEL = 256
        N_HEADS = 16
        D_K = D_MODEL // N_HEADS
        EPS = 1e-06
        b, n, _ = x.shape
        h, d = (N_HEADS, D_K)

        def proj(W, bias):
            y = jnp.einsum('bnm,dm->bnd', x, W) + bias
            return y.reshape(b, n, h, d).transpose(0, 2, 1, 3)
        Q = jax.nn.relu(proj(Wq, bq))
        K = jax.nn.relu(proj(Wk, bk))
        V = proj(Wv, bv)
        pos = jnp.arange(n, dtype=x.dtype)
        decay = jnp.exp(-pos / n)[None, None, :, None]
        Q = Q * decay
        K = K * decay
        KV = jnp.einsum('bhnd,bhne->bhde', K, V)
        Ksum = K.sum(axis=2)
        Z = 1.0 / (jnp.einsum('bhnd,bhd->bhn', Q, Ksum)[..., None] + EPS)
        out = jnp.einsum('bhnd,bhde->bhne', Q, KV) * Z
        out = out.transpose(0, 2, 1, 3).reshape(b, n, h * d)
        return jnp.einsum('bnm,dm->bnd', out, Wo) + bo

    def _L0_xattn_ref(q, k, v, Wc, bc):
        import jax, jax.numpy as jnp
        import numpy as np
        import math
        D_MODEL = 256
        N_HEADS = 16
        N_GROUPS = 4
        HEADS_PER_GROUP = N_HEADS // N_GROUPS
        HEAD_DIM = D_MODEL // N_HEADS
        B, S = (2, 256)
        b, s, _ = q.shape
        qh = q.reshape(b, s, N_GROUPS, HEADS_PER_GROUP, HEAD_DIM).transpose(0, 2, 3, 1, 4)
        kh = k.reshape(b, s, N_GROUPS, HEAD_DIM).transpose(0, 2, 1, 3)
        vh = v.reshape(b, s, N_GROUPS, HEAD_DIM).transpose(0, 2, 1, 3)
        scale = 1.0 / math.sqrt(HEAD_DIM)
        scores = jnp.einsum('bghsd,bgtd->bghst', qh, kh) * scale
        probs = jax.nn.softmax(scores, axis=-1)
        out = jnp.einsum('bghst,bgtd->bghsd', probs, vh)
        out = out.transpose(0, 3, 1, 2, 4).reshape(b, s, D_MODEL)
        return out @ Wc.T + bc

    def _L0_ffn_ref(hidden_states, router_w, w_gate, w_up, w_down, sh_gate, sh_up, sh_down, sh_gate_w):
        import jax, jax.numpy as jnp
        import numpy as np
        B, S, H = (2, 256, 256)
        E, K = (16, 4)
        I_MOE, I_SH = (176, 704)
        orig = hidden_states.shape
        h = hidden_states.reshape(-1, orig[-1])
        N = h.shape[0]
        logits = h @ router_w.T
        probs = jax.nn.softmax(logits.astype(jnp.float32), axis=-1)
        top_vals, top_idx = jax.lax.top_k(probs, K)
        top_vals = top_vals / jnp.maximum(top_vals.sum(-1, keepdims=True), 1e-09)
        top_vals = top_vals.astype(h.dtype)
        comb = jnp.zeros((N, E), h.dtype).at[jnp.arange(N)[:, None], top_idx].add(top_vals)
        g = jnp.einsum('nh,ehi->eni', h, w_gate)
        u = jnp.einsum('nh,ehi->eni', h, w_up)
        y = jnp.einsum('eni,eih->enh', jax.nn.silu(g) * u, w_down)
        routed = jnp.einsum('enh,ne->nh', y, comb)
        shared = jax.nn.silu(h @ sh_gate) * (h @ sh_up) @ sh_down
        sg = jax.nn.sigmoid(h @ sh_gate_w)
        return (routed + sg * shared).reshape(orig)
    x = _layernorm(x + _L0_attn_ref(x, L0_attn_Wq, L0_attn_bq, L0_attn_Wk, L0_attn_bk, L0_attn_Wv, L0_attn_bv, L0_attn_Wo, L0_attn_bo), axis=-1)
    x = _layernorm(x + _L0_xattn_ref(x, ctx_512, ctx_512, L0_xattn_Wc, L0_xattn_bc), axis=-1)
    x = _layernorm(x + _L0_ffn_ref(x, L0_ffn_router_w, L0_ffn_w_gate, L0_ffn_w_up, L0_ffn_w_down, L0_ffn_sh_gate, L0_ffn_sh_up, L0_ffn_sh_down, L0_ffn_sh_gate_w), axis=-1)
    return x

_drawn_inputs = setup_inputs


def setup_inputs(seed=0):
    import zlib

    import numpy as np

    out = dict(_drawn_inputs(seed))
    spreads = {'L0_attn_bq': (0.0, 0.41),
     'L0_attn_bk': (0.0, 0.535),
     'L0_attn_bv': (0.0, 0.1),
     'L0_attn_bo': (0.0, 0.1)}
    factors = {}
    for name, (base, spread) in spreads.items():
        noise = np.random.default_rng([zlib.crc32(name.encode()), seed]).standard_normal(out[name].shape)
        drawn = base * np.exp(spread * noise) if base else spread * noise
        out[name] = jnp.asarray(drawn.astype(out[name].dtype))
    for name, factor in factors.items():
        out[name] = (out[name] * factor).astype(out[name].dtype)
    return out
```

```python
from contextlib import ExitStack

import concourse.bass as bass
from concourse import mybir

F32, F16 = mybir.dt.float32, mybir.dt.float16
U32, I32 = mybir.dt.uint32, mybir.dt.int32
ALU = mybir.AluOpType
ACT = mybir.ActivationFunctionType
AX = mybir.AxisListType.X

P = 128
B, S, D = 32, 64, 256
N = B * S
KC = D // P
HD = 16
NG, HPG = 4, 4
C = NG * HD
VW = 2 * (HD + 1)
E, TOPK = 16, 4
IM, IS = 176, 704
IC = -(-IS // P)
W_SCALE = 64.0
W_BACK = 1.0 / W_SCALE
ATTN_EPS, LN_EPS, TOP_MIN = 1e-6, 1e-5, 1e-9

GROUPS = 4
GT = N // GROUPS
TQ = GT // P
GB = GT // S
EPG = E // GROUPS

ROW = D + E + 1
REGION = N + P
DUMP = E * REGION
NO_TOKEN = 1 << 20

W_PARTS = dict(q=KC * D, kv=KC * 2 * D, o=KC * D, c=KC * D, r=KC * (E + 1), gu=KC * 2 * IS, dn=IC * D)
W_AT, _n = {}, 0
for _name, _cols in W_PARTS.items():
    W_AT[_name] = _n
    _n += _cols
W_COLS = _n
W_PIECES = [(0, W_AT["o"]), (W_AT["o"], W_AT["gu"]), (W_AT["gu"], W_COLS)]
EG = KC * 2 * IM
EW = EG + KC * D

CF_PARTS = dict(ident=P, head_mask=P, decay_row=S, decay_col=1, slot=1, token=TQ, eps=1, iota=E,
                region=E, steps=E, upto=E * E, evens=P // 2)
CF_AT, _n = {}, 0
for _name, _cols in CF_PARTS.items():
    CF_AT[_name] = _n
    _n += _cols
CF_COLS = _n
RSQRT_STEPS = 3
RSQRT = 2 + 2 * RSQRT_STEPS
R_CHAIN = 31

PER = dict(
    ld_xT=16, ld_x=16, ld_ctx=16, ctx_in=16 * 2 * NG, ld_v=16 * NG, ld_exp=16 * EPG, st_acc=16,
    scattered=16 * TQ * TOPK,
    xT_hi=1, xT_lo=1, ctx_hi=1, ctx_lo=1, v_hi=1, v_lo=1, x_bo=1,
    q_proj=KC, q_relu=KC, q_decay=KC, kv_proj=TQ, kv_read=2 * TQ, k_relu=TQ,
    kv_state=GB, kv_masked=2 * GB, attn_nd=GB, attn_den=TQ, attn_rec=TQ, attn_div=TQ, attn_hi=TQ, attn_lo=TQ,
    wo_done=TQ, ln1_sum=TQ, ln1_stat=TQ, ln1_mv=TQ, ln1_rstd=TQ * RSQRT, x1_norm=TQ, x1_bc=TQ,
    x1T=TQ, x1T_hi=TQ, x1T_lo=TQ, s_done=GB, s_max=GB, m_T=GB, m_copied=GB, st_done=GB,
    exp_done=GB, e_hi=GB, e_lo=GB, pv_done=GB, pv_rec=GB, pv_norm=GB, aT=TQ, aT_hi=TQ, aT_lo=TQ,
    wc_done=TQ, ln2_sum=TQ, ln2_stat=TQ, ln2_mv=TQ, ln2_rstd=TQ * RSQRT, x2_norm=TQ,
    row_hi=TQ, row_lo=TQ, x2T=TQ, x2T_read=TQ, router=1, r_chain=R_CHAIN, r_exp=2, rank=1,
    g_done=IC, u_done=IC, silu=IC, h_mul=IC, h_hi=IC, h_lo=IC, down=TQ, acc_row=TQ,
    w_hi=EPG, w_lo=EPG,
)
SLOT_SEMS = ("xg_in", "xg_T", "xg_read", "meta", "e_gu", "e_silu", "e_mul", "e_hT", "e_hhi", "e_hlo",
             "e_y", "e_yw", "e_id", "e_add")
LAST_SEMS = ("f_in", "f_sum", "f_stat", "f_mv", "f_rstd", "f_out", "f_st")
ONCE_SEMS = ("ld_const", "ld_w0", "ld_w1", "ld_w2", "ld_ind", "setup", "ws_hi", "ws_lo", "st_zero", "t_chain", "t_rows",
             "t_tab", "st_pad", "waits_apart")
SETUP = 9

THREE = ((0, 0), (1, 0), (0, 1))


def chunk_rows(c):
    return min(P, IS - c * P)


def decoder_layer_program(nc, t, out):
    xs = nc.dram_tensor("xs_rows", [DUMP + P, ROW], F32, kind="Internal").ap()
    acc = [nc.dram_tensor(f"acc{p}", [N, D], F32, kind="Internal").ap() for p in range(2)]

    with ExitStack() as ctx:
        def sb(name, shape, dt=F32):
            return ctx.enter_context(nc.sbuf_tensor(name, shape, dt))

        def over(buffer, shape, dt=F32, at=0):
            cols = 1
            for n in shape[1:]:
                cols *= n
            cols = cols if dt != F16 else cols // 2
            view = buffer[0:shape[0], at:at + cols]
            if dt != F32:
                view = view.bitcast(dt)
            names = "abcde"[:len(shape) - 1]
            return view.rearrange(f"p ({' '.join(names)}) -> p {' '.join(names)}", **dict(zip(names, shape[1:])))

        w_stage = sb("w_stage", [P, W_COLS])
        w16 = sb("w16", [P, 2, W_COLS], F16)
        e_stage = sb("e_stage", [P, EW])
        e_w16 = sb("e_w16", [P, E, 2, EW], F16)
        cf = sb("cf", [P, CF_COLS])
        ch = sb("ch", [P, 3 * P], F16)
        bq_col = sb("bq_col", [P, KC])
        bias_rows = sb("bias_rows", [P, 4, D])
        bk_row, bv_row, bo_row, bc_row = (bias_rows[:, n, :] for n in range(4))

        def const(name):
            return cf[:, CF_AT[name]:CF_AT[name] + CF_PARTS[name]]

        ident, head_mask, decay_row = const("ident"), const("head_mask"), const("decay_row")
        id16, tri16, ones16 = ch[:, 0:P], ch[:, P:2 * P], ch[:, 2 * P:3 * P]

        def weight(name, part, chunk, lo, n):
            width = {"q": D, "kv": 2 * D, "o": D, "c": D, "r": E + 1, "gu": 2 * IS, "dn": D}[name]
            a = W_AT[name] + chunk * width + lo
            return w16[:, part, a:a + n]

        xT = sb("xT", [P, KC, GT])
        x_in = sb("x_in", [P, TQ, D])
        c_stage = sb("c_stage", [C, GB, S])
        c_parts = sb("c_parts", [C, 2, GB, S], F16)
        c16 = sb("c16", [C + NG, 2, GB, NG * S], F16)
        v_stage = sb("v_stage", [P, GB, 2, VW])
        v16 = sb("v16", [P, 2, GB, 2, VW], F16)
        vb = sb("vb", [P, TQ, KC, P + 1])
        x1 = sb("x1", [P, TQ, D])
        x2 = sb("x2", [P, TQ, D])
        row = sb("row", [P, TQ, ROW])
        row16 = row[:, :, 0:D].bitcast(F16)
        queries_then_x2T = sb("queries_then_x2T", [P, KC * GT])
        qd = over(queries_then_x2T, [P, KC, GT])
        x2T16 = over(queries_then_x2T, [P, 2, KC, GT], F16)
        xT_then_x1T = sb("xT_then_x1T", [P, 2 * TQ * HPG * S])
        xT16 = over(xT_then_x1T, [P, 2, KC, GT], F16)
        xh = over(xT_then_x1T, [C + NG, 2, TQ, 2, HPG * S], F16)
        state_then_rows = sb("state_then_rows", [P, 4 * D])
        kv_m = over(state_then_rows, [P, 2, KC, P])
        k_sum = over(state_then_rows, [P, 2, KC, P], at=2 * D)
        aT16 = over(state_then_rows, [P, 2, 2, 2, P], F16)
        onehot = over(state_then_rows, [P, TQ, TOPK, E], at=2 * D)
        pos_sel = over(state_then_rows, [P, TQ, TOPK, E], at=3 * D)
        kb = over(w_stage, [P, TQ, D])
        e32 = over(w_stage, [P, 2, 2, HPG * S])
        gate = over(w_stage, [P, 2, GT])
        h32 = over(w_stage, [P, 2, GT], at=2 * GT)
        a2 = over(w_stage, [P, GB, P], at=4 * GT)
        after = 4 * GT + GB * P
        h16 = over(w_stage, [P, 2, IC, GT], F16, at=after)
        a32 = over(w_stage, [P, 2, D], at=after)
        a16 = over(w_stage, [P, 2, 2, KC, P], F16, at=after + 2 * D)
        e16 = over(w_stage, [P, 2, 2, 2, HPG * S], F16, at=after + 4 * D)
        den = over(w_stage, [P, 2, D], at=after + IC * GT)
        m16 = sb("m16", [P, 2, 2 * NG], F16)
        stat1 = sb("stat1", [P, TQ, 6])
        mv1 = sb("mv1", [P, TQ, 2])
        rstd1 = sb("rstd1", [P, TQ])
        half1 = sb("half1", [P, TQ])
        rec = sb("rec", [P, 2, 2 * NG])
        stat2 = sb("stat2", [P, TQ, 6])
        mv2 = sb("mv2", [P, TQ, 2])
        rstd2 = sb("rstd2", [P, TQ])
        half2 = sb("half2", [P, TQ])
        lg = sb("lg", [P, TQ, E + 1])
        lg_max = sb("lg_max", [P, TQ])
        shifted = sb("shifted", [P, TQ, E])
        ex = sb("ex", [P, TQ, E])
        sg_e = sb("sg_e", [P, TQ])
        sg_d = sb("sg_d", [P, TQ])
        sg = sb("sg", [P, TQ])
        ex_sum = sb("ex_sum", [P, TQ])
        ex_rec = sb("ex_rec", [P, TQ])
        prob = sb("prob", [P, TQ, E])
        top_v = sb("top_v", [P, TQ, 8])
        top_i = sb("top_i", [P, TQ, 8], U32)
        top_f = sb("top_f", [P, TQ, TOPK])
        mask16 = sb("mask16", [P, TQ + 1, E], F16)
        chosen = sb("chosen", [P, TQ, E])
        w_sum = sb("w_sum", [P, TQ])
        w_clip = sb("w_clip", [P, TQ])
        w_rec = sb("w_rec", [P, TQ])
        count = sb("count", [P, E])
        pos = sb("pos", [P, TQ, E])
        pos_f = sb("pos_f", [P, TQ * TOPK])
        pos_u = sb("pos_u", [P, TQ * TOPK], U32)
        token = sb("token", [P, TQ])
        zeros = sb("zeros", [P, D])
        pad_row = sb("pad_row", [P, ROW])
        newton = sb("newton", [P, 1])
        more = over(queries_then_x2T, [P, E, E])
        tiles = sb("tiles", [P, E])
        tiles_to = over(queries_then_x2T, [P, E, E], at=E * E)
        cum = sb("cum", [P, E])
        evens_below = over(queries_then_x2T, [P, P // 2], at=2 * E * E)
        passed = sb("passed", [P, E])
        passed_t = sb("passed_t", [P, E])
        slot_f = sb("slot_f", [P, 8])
        TAB_ROW, TAB_PAD, TAB_LAPS = P, 2 * P, 2 * P + E
        tab = sb("tab", [1, TAB_LAPS + 1], I32)
        xg = over(xT[:, :, :].rearrange("p k n -> p (k n)"), [P, 2, ROW])
        xg16 = xg[:, :, 0:D].bitcast(F16)
        xgT = over(xT_then_x1T, [P, 2, 2 * KC, P], F16)
        ehT = over(xT_then_x1T, [P, 2, 2, KC, P], F16, at=2 * D)
        eh = over(queries_then_x2T, [P, 2, KC * P])
        ye = over(queries_then_x2T, [P, 2, D], at=2 * D)
        e_gate = over(w_stage, [P, 2, IM])
        meta = sb("meta", [P, 2, E + 1])
        ids = sb("ids", [P, 2], U32)
        fa = over(x1[:, :, :].rearrange("p q d -> p (q d)"), [P, 2, 2, D])
        fo = over(x_in[:, :, :].rearrange("p q d -> p (q d)"), [P, 2, D])
        fsum = over(x_in[:, :, :].rearrange("p q d -> p (q d)"), [P, 2, D], at=2 * D)
        fstat = sb("fstat", [P, 2, 6])
        fmv = sb("fmv", [P, 2, 2])
        frstd = sb("frstd", [P, 2])
        fhalf = sb("fhalf", [P, 2])

        bank = [ctx.enter_context(nc.psum_tensor(f"bank{k}", [P, 512], F32)) for k in range(8)]
        bP, bK, bN, bW, bT, bE = bank[0:2], bank[2:4], bank[4], bank[5], bank[6], bank[7]

        def half(b):
            return b[:, :].bitcast(F16)

        sems = {k: ctx.enter_context(nc.semaphore("s_" + k)) for k in (*PER, *ONCE_SEMS)}
        slot_sem = {k: [ctx.enter_context(nc.semaphore(f"s_{k}{p}")) for p in range(2)]
                    for k in (*SLOT_SEMS, *LAST_SEMS)}

        def need(eng, name, i, n=None):
            eng.wait_ge(sems[name], i * PER[name] + (PER[name] if n is None else n))

        def apart(eng, sem, value):
            eng.wait_ge(sem, value)
            eng.sem_inc(sems["waits_apart"], 1)

        def bc(ap, shape):
            return ap.broadcast_to(list(shape))

        block = ctx.enter_context(nc.Block())

        @block.sync
        def _(sp):
            def load_group(i, later):
                if later:
                    need(sp, "xT_hi", i, 0)
                    need(sp, "xT_lo", i, 0)
                sp.dma_start(xT[:, :, :], t["xT"][:, :, bass.ts(i, GT)].rearrange("k p n -> p k n")
                             ).then_inc(sems["ld_xT"], 16)
                if later:
                    apart(sp, sems["ctx_hi"], i * PER["ctx_hi"])
                    apart(sp, sems["ctx_lo"], i * PER["ctx_lo"])
                sp.dma_start(c_stage[:, :, :], t["ctxT"][:, bass.ts(i, GB), :]).then_inc(sems["ld_ctx"], 16)
                if later:
                    need(sp, "v_hi", i, 0)
                    need(sp, "v_lo", i, 0)
                for g in range(NG):
                    r, w = (g % 2) * S, (g % 2) * (HD + 1)
                    sp.dma_start(v_stage[r:r + S, :, g // 2, w:w + HD],
                                 t["ctx"][bass.ts(i, GB), :, g * HD:(g + 1) * HD].rearrange("b t d -> t b d")
                                 ).then_inc(sems["ld_v"], 16)
                if later:
                    need(sp, "ln2_sum", i, 0)
                sp.dma_start(x_in[:, :, :], t["x"][bass.ts(i, GT), :].rearrange("(q p) d -> p q d", p=P)
                             ).then_inc(sems["ld_x"], 16)

            def place_context(i):
                apart(sp, sems["ctx_hi"], (i + 1) * PER["ctx_hi"])
                apart(sp, sems["ctx_lo"], (i + 1) * PER["ctx_lo"])
                need(sp, "st_done", i, 0)
                for part in range(2):
                    for g in range(NG):
                        sp.dma_start(c16[g * HD:(g + 1) * HD, part, :, g * S:(g + 1) * S],
                                     c_parts[g * HD:(g + 1) * HD, part, :, :]).then_inc(sems["ctx_in"], 16)

            def load_experts(i):
                for n in range(EPG):
                    need(sp, "w_hi", i, n)
                    need(sp, "w_lo", i, n)
                    sp.dma_start(e_stage[:, :], t["e_w"][bass.ds(i * EPG + n, 1)].rearrange("a p c -> p (a c)")
                                 ).then_inc(sems["ld_exp"], 16)

            def store_group(i):
                need(sp, "acc_row", i)
                sp.dma_start(acc[0][bass.ts(i, GT), :].rearrange("(q p) d -> p q d", p=P), x2[:, :, :]
                             ).then_inc(sems["st_acc"], 16)

            sp.dma_start(cf[:, :], t["cf"]).then_inc(sems["ld_const"], 16)
            sp.dma_start(ch[:, :], t["ch"]).then_inc(sems["ld_const"], 16)
            sp.dma_start(bq_col[:, :], t["bq"]).then_inc(sems["ld_const"], 16)
            sp.dma_start(bias_rows[:, :, :].rearrange("p n d -> p (n d)"), t["biases"].partition_broadcast(P)
                         ).then_inc(sems["ld_const"], 16)
            def load_weights(n):
                a, b = W_PIECES[n]
                sp.dma_start(w_stage[:, a:b], t["w"][:, a:b]).then_inc(sems[f"ld_w{n}"], 16)

            load_weights(0)
            sp.wait_ge(sems["setup"], SETUP)
            load_group(0, False)
            for n in range(1, len(W_PIECES)):
                load_weights(n)
            sp.dma_start(c16[C:C + NG, 0, :, :], t["pick"]).then_inc(sems["ld_ind"], 16)
            sp.dma_start(acc[1].rearrange("(n p) d -> p n d", p=P),
                         bc(zeros[:, :].unsqueeze(1), [P, N // P, D])).then_inc(sems["st_zero"], 16)
            with sp.Fori(0, GROUPS - 1) as i:
                place_context(i)
                load_experts(i)
                load_group(i + 1, True)
                store_group(i)
            place_context(GROUPS - 1)
            load_experts(GROUPS - 1)
            store_group(GROUPS - 1)

            sp.wait_ge(sems["t_tab"], 1)
            sp.dma_start(xs[DUMP:DUMP + P, :], pad_row[:, :]).then_inc(sems["st_pad"], 16)
            for e in range(E):
                after = sp.value_load(tab[0:1, TAB_PAD + e:TAB_PAD + e + 1], min_val=0, max_val=DUMP - P)
                sp.dma_start(xs[bass.ds(after, P), :], pad_row[:, :]).then_inc(sems["st_pad"], 16)
            sp.wait_ge(sems["st_pad"], 16 * (E + 1))
            need(sp, "scattered", GROUPS - 1)
            laps = sp.value_load(tab[0:1, TAB_LAPS:TAB_LAPS + 1], min_val=0, max_val=P // 2 - 1)
            with sp.Fori(0, laps + 1) as j:
                for p in range(2):
                    first = sp.value_load(tab[0:1, bass.ds(TAB_ROW + 2 * j + p, 1)], min_val=0, max_val=DUMP)
                    sp.wait_ge(slot_sem["xg_T"][p], j)
                    sp.wait_ge(slot_sem["meta"][p], j)
                    sp.dma_start(xg[:, p, :], xs[bass.ds(first, P), :]).then_inc(slot_sem["xg_in"][p], 16)
            for p in range(2):
                apart(sp, slot_sem["e_add"][p], laps * 16 + 16)
            with sp.Fori(0, N // P // 2) as j:
                for p in range(2):
                    sp.wait_ge(slot_sem["f_sum"][p], j)
                    for a in range(2):
                        sp.dma_start(fa[:, p, a, :], acc[a][bass.ds(j * 2 * P + p * P, P), :]
                                     ).then_inc(slot_sem["f_in"][p], 16)
            for p in range(2):
                sp.wait_ge(slot_sem["f_st"][p], 16 * (N // P // 2))

        @block.tensor
        def _(pe):
            def three(out, lhs, rhs, chunks):
                steps = [(w, d, k) for k in range(chunks) for w, d in THREE]
                for n, (w, d, k) in enumerate(steps):
                    last = pe.matmul(out, lhs(w, d, k), rhs(w, d, k), start=n == 0, stop=n == len(steps) - 1)
                return last

            def q_projection(i):
                need(pe, "xT_hi", i)
                need(pe, "xT_lo", i)
                for c in range(KC):
                    if c == 0:
                        need(pe, "r_chain", i, 0)
                    else:
                        need(pe, "h_mul", i, 0)
                    three(bP[c][:, :], lambda w, d, k: weight("q", w, k, c * P, P),
                          lambda w, d, k: xT16[:, d, k, :], KC).then_inc(sems["q_proj"], 1)

            def kv_projection(i, q):
                if q < 2:
                    need(pe, "q_relu", i, q + 1)
                else:
                    need(pe, "kv_read", i, 2 * (q - 1))
                three(bP[q % 2][:, :], lambda w, d, k: xT16[:, d, k, q * P:(q + 1) * P],
                      lambda w, d, k: weight("kv", w, k, 0, 2 * D), KC).then_inc(sems["kv_proj"], 1)

            def kv_state(i, b):
                q, r = b // 2, (b % 2) * S
                need(pe, "k_relu", i, q + 1)
                need(pe, "kv_read", i, 2 * (q + 1))
                if b < 2:
                    need(pe, "h_mul", i, 0)
                else:
                    need(pe, "kv_masked", i, 2 * (b - 1))
                for c in range(KC):
                    last = pe.matmul(bK[b % 2][:, c * (P + 1):(c + 1) * (P + 1)], kb[r:r + S, q, c * P:(c + 1) * P],
                                     vb[r:r + S, q, c, :], start=True, stop=True)
                last.then_inc(sems["kv_state"], 1)

            def attention(i, b):
                need(pe, "kv_masked", i, 2 * (b + 1))
                if b == 0:
                    need(pe, "q_decay", i)
                    need(pe, "h_mul", i, 0)
                if b % 2 == 0 and b:
                    need(pe, "attn_div", i, b // 2)
                for m, state in enumerate((kv_m, k_sum)):
                    for c in range(KC):
                        a = m * D + c * P + (b % 2) * S
                        last = pe.matmul(bN[:, a:a + S], state[:, b % 2, c, :], qd[:, c, b * S:(b + 1) * S],
                                         start=True, stop=True)
                last.then_inc(sems["attn_nd"], 1)

            def attention_out(i, q):
                need(pe, "attn_hi", i, q + 1)
                need(pe, "attn_lo", i, q + 1)
                if q == 0:
                    need(pe, "acc_row", i, 0)
                else:
                    need(pe, "ln1_sum", i, q)
                three(bW[:, 0:D], lambda w, d, k: a16[:, q % 2, d, k, :],
                      lambda w, d, k: weight("o", w, k, 0, D), KC).then_inc(sems["wo_done"], 1)

            def x1_transposes(i, q):
                if q == 0:
                    need(pe, "acc_row", i, 0)
                else:
                    need(pe, "x1T_lo", i, q)
                apart(pe, sems["x1_norm"], i * PER["x1_norm"] + q + 1)
                for h in range(HPG):
                    last = pe.transpose(bT[0:C, h * P:(h + 1) * P], x1[:, q, h * C:(h + 1) * C], ident)
                last.then_inc(sems["x1T"], 1)

            def scores(i, b):
                q = b // 2
                need(pe, "x1T_hi", i, q + 1)
                if b == 0:
                    need(pe, "ctx_in", i)
                if b < 2:
                    need(pe, "kv_masked", i)
                else:
                    need(pe, "s_max", i, b - 1)
                for hp in range(2):
                    last = pe.matmul(bK[b % 2][:, hp * NG * S:(hp + 1) * NG * S],
                                     xh[0:C, 0, q, b % 2, hp * P:(hp + 1) * P], c16[0:C, 0, b, :],
                                     start=True, stop=True)
                last.then_inc(sems["s_done"], 1)

            def max_transposes(i, b):
                need(pe, "s_max", i, b + 1)
                if b == 0:
                    need(pe, "kv_read", i)
                else:
                    need(pe, "m_copied", i, b)
                for hp in range(2):
                    last = pe.transpose(half(bP[0])[0:NG, hp * P:(hp + 1) * P], m16[:, b % 2, hp * NG:(hp + 1) * NG], id16)
                last.then_inc(sems["m_T"], 1)

            def scores_T(i, b):
                q = b // 2
                need(pe, "m_copied", i, b + 1)
                need(pe, "x1T_lo", i, q + 1)
                if b == 0:
                    pe.wait_ge(sems["ld_ind"], 16)
                    need(pe, "r_chain", i, 0)
                else:
                    need(pe, "exp_done", i, b)
                for gp in range(2):
                    last = three(bE[:, gp * HPG * S:(gp + 1) * HPG * S],
                                 lambda w, d, k: c16[0:C if w or d else C + NG, w, b, gp * P:(gp + 1) * P],
                                 lambda w, d, k: xh[0:C if w or d else C + NG, d, q, b % 2, :], 1)
                last.then_inc(sems["st_done"], 1)

            def values(i, b):
                need(pe, "e_hi", i, b + 1)
                need(pe, "e_lo", i, b + 1)
                if b == 0:
                    need(pe, "v_hi", i)
                    need(pe, "v_lo", i)
                    need(pe, "attn_div", i)
                if b == 1:
                    need(pe, "kv_read", i)
                if b >= 2:
                    need(pe, "pv_norm", i, b - 1)
                for hp in range(2):
                    for gp in range(2):
                        a = (hp * 2 + gp) * VW
                        last = three((bN, bP[1])[b % 2][:, a:a + VW],
                                     lambda w, d, k: e16[:, b % 2, d, gp, hp * P:(hp + 1) * P],
                                     lambda w, d, k: v16[:, w, b, gp, :], 1)
                last.then_inc(sems["pv_done"], 1)

            def a_transposes(i, q):
                need(pe, "pv_norm", i, 2 * (q + 1))
                if q == 0:
                    need(pe, "x1T_lo", i)
                else:
                    need(pe, "aT_lo", i, q)
                for b in range(2):
                    last = pe.transpose(bT[:, b * P:(b + 1) * P], a2[:, 2 * q + b, :], ident)
                last.then_inc(sems["aT"], 1)

            def cross_out(i, q):
                need(pe, "aT_hi", i, q + 1)
                need(pe, "aT_lo", i, q + 1)
                if q == 0:
                    need(pe, "ln1_sum", i)
                else:
                    need(pe, "ln2_sum", i, q)
                three(bW[:, 0:D], lambda w, d, k: aT16[:, q % 2, d, k, :],
                      lambda w, d, k: weight("c", w, k, 0, D), KC).then_inc(sems["wc_done"], 1)

            def x2_transposes(i, q):
                need(pe, "row_hi", i, q + 1)
                need(pe, "row_lo", i, q + 1)
                if q == 0:
                    need(pe, "aT_lo", i)
                else:
                    need(pe, "x2T_read", i, q)
                for a in range(2 * KC):
                    last = pe.transpose(half(bT)[:, a * P:(a + 1) * P], row16[:, q, a * P:(a + 1) * P], id16)
                last.then_inc(sems["x2T"], 1)

            def router(i):
                need(pe, "m_copied", i)
                need(pe, "x2T_read", i)
                for q in range(TQ):
                    last = three(bP[0][:, q * (E + 1):(q + 1) * (E + 1)],
                                 lambda w, d, k: x2T16[:, d, k, q * P:(q + 1) * P],
                                 lambda w, d, k: weight("r", w, k, 0, E + 1), KC)
                last.then_inc(sems["router"], 1)

            def ranks(i):
                need(pe, "r_chain", i, R_MASK)
                need(pe, "exp_done", i)
                flat = mask16[:, :, :].rearrange("p q e -> p (q e)")
                pe.matmul(bE[:, 0:(TQ + 1) * E], tri16, flat, start=True, stop=False, skip_group_check=True)
                for q in range(TQ):
                    last = pe.matmul(bE[:, (q + 1) * E:(TQ + 1) * E].rearrange("p (q e) -> p q e", e=E), ones16,
                                     bc(mask16[:, q:q + 1, :], [P, TQ - q, E]), start=False, stop=q == TQ - 1,
                                     skip_group_check=True)
                last.then_inc(sems["rank"], 1)

            def shared_up(i, c):
                n, (bg, bu) = chunk_rows(c), ((bK[0], bK[1]), (bP[1], bN))[c % 2]
                if c < 2:
                    need(pe, "s_max", i)
                    need(pe, "pv_norm", i)
                else:
                    need(pe, "h_mul", i, c - 1)
                for half_, b_, name in ((0, bg, "g_done"), (1, bu, "u_done")):
                    three(b_[0:n, :], lambda w, d, k: weight("gu", w, k, half_ * IS + c * P, n),
                          lambda w, d, k: x2T16[:, d, k, :], KC).then_inc(sems[name], 1)

            def shared_down(i, q):
                if q == 0:
                    need(pe, "h_hi", i)
                    need(pe, "h_lo", i)
                    need(pe, "ln2_sum", i)
                    need(pe, "x2T_read", i)
                if q >= 2:
                    need(pe, "acc_row", i, q - 1)
                steps = [(w, d, c) for c in range(IC) for w, d in THREE]
                for n, (w, d, c) in enumerate(steps):
                    r = chunk_rows(c)
                    last = pe.matmul((bW, bT)[q % 2][:, 0:D], h16[0:r, d, c, q * P:(q + 1) * P],
                                     weight("dn", w, c, 0, D)[0:r], start=n == 0, stop=n == len(steps) - 1)
                last.then_inc(sems["down"], 1)

            pe.wait_ge(sems["ld_const"], 64)
            pe.wait_ge(sems["ws_hi"], len(W_PIECES))
            pe.wait_ge(sems["ws_lo"], len(W_PIECES))
            pe.wait_ge(sems["setup"], SETUP)
            with pe.Fori(0, GROUPS) as i:
                q_projection(i)
                for q in range(TQ):
                    kv_projection(i, q)
                for b in range(GB + 1):
                    if b < GB:
                        kv_state(i, b)
                    if b >= 1:
                        attention(i, b - 1)
                    if b >= 3 and b % 2:
                        attention_out(i, (b - 3) // 2)
                attention_out(i, TQ - 1)
                x1_transposes(i, 0)
                for step in range(GB + 6):
                    if step % 2 == 0 and step // 2 + 1 < TQ:
                        x1_transposes(i, step // 2 + 1)
                    if step < GB:
                        scores(i, step)
                    if 1 <= step <= GB:
                        max_transposes(i, step - 1)
                    if 2 <= step < GB + 2:
                        scores_T(i, step - 2)
                    if 3 <= step < GB + 3:
                        values(i, step - 3)
                    if step >= 5 and step % 2 and step < GB + 5:
                        a_transposes(i, (step - 5) // 2)
                    if step >= 6 and step % 2 == 0 and step < GB + 6:
                        cross_out(i, (step - 6) // 2)
                for q in range(TQ):
                    x2_transposes(i, q)
                router(i)
                for c in range(IC):
                    shared_up(i, c)
                    if c == 2:
                        ranks(i)
                for q in range(TQ):
                    shared_down(i, q)

            pe.wait_ge(sems["t_chain"], T_CHAIN)
            for n in range(2):
                last = pe.transpose(bP[0][0:1, n * P:(n + 1) * P], slot_f[:, n:n + 1], ident)
            last.then_inc(sems["t_rows"], 1)

            def slot_transposes(j, p):
                pe.wait_ge(slot_sem["xg_in"][p], 16 * (j + 1))
                pe.wait_ge(slot_sem["xg_read"][p], j)
                for a in range(2 * KC):
                    last = pe.transpose(half((bT, bE)[p])[:, a * P:(a + 1) * P], xg16[:, p, a * P:(a + 1) * P], id16)
                last.then_inc(slot_sem["xg_T"][p], 1)

            def slot_up(j, p):
                e = pe.value_load(tab[0:1, bass.ds(2 * j + p, 1)], min_val=0, max_val=E - 1)
                pe.wait_ge(slot_sem["xg_read"][p], j + 1)
                pe.wait_ge(slot_sem["e_mul"][p], j)
                three(bP[p][:, 0:2 * IM], lambda w, d, k: xgT[:, p, d * KC + k, :],
                      lambda w, d, k: e_w16[:, bass.ds(e, 1), w, k * 2 * IM:(k + 1) * 2 * IM].rearrange("p a n -> p (a n)"),
                      KC).then_inc(slot_sem["e_gu"][p], 1)

            def slot_h_transposes(j, p):
                pe.wait_ge(slot_sem["e_mul"][p], j + 1)
                pe.wait_ge(slot_sem["e_hlo"][p], j)
                for k in range(KC):
                    last = pe.transpose(bK[p][:, k * P:(k + 1) * P], eh[:, p, k * P:(k + 1) * P], ident)
                last.then_inc(slot_sem["e_hT"][p], 1)

            def slot_down(j, p):
                e = pe.value_load(tab[0:1, bass.ds(2 * j + p, 1)], min_val=0, max_val=E - 1)
                pe.wait_ge(slot_sem["e_hhi"][p], j + 1)
                pe.wait_ge(slot_sem["e_hlo"][p], j + 1)
                pe.wait_ge(slot_sem["e_yw"][p], j)
                three((bN, bW)[p][:, 0:D], lambda w, d, k: ehT[:, p, d, k, :],
                      lambda w, d, k: e_w16[:, bass.ds(e, 1), w, EG + k * D:EG + (k + 1) * D].rearrange("p a n -> p (a n)"),
                      KC).then_inc(slot_sem["e_y"][p], 1)

            pe.wait_ge(sems["t_tab"], 1)
            need(pe, "acc_row", GROUPS - 1)
            need(pe, "w_hi", GROUPS - 1)
            need(pe, "w_lo", GROUPS - 1)
            laps = pe.value_load(tab[0:1, TAB_LAPS:TAB_LAPS + 1], min_val=0, max_val=P // 2 - 1)
            slot_transposes(0, 0)
            slot_up(0, 0)
            slot_transposes(0, 1)
            slot_up(0, 1)
            slot_h_transposes(0, 0)
            with pe.Fori(0, laps) as j:
                slot_transposes(j + 1, 0)
                slot_down(j, 0)
                slot_up(j + 1, 0)
                slot_h_transposes(j, 1)
                slot_transposes(j + 1, 1)
                slot_down(j, 1)
                slot_up(j + 1, 1)
                slot_h_transposes(j + 1, 0)
            slot_down(laps, 0)
            slot_h_transposes(laps, 1)
            slot_down(laps, 1)

        @block.scalar
        def _(act):
            def split_expert(i, n):
                act.wait_ge(sems["ld_exp"], i * PER["ld_exp"] + 16 * (n + 1))
                act.activation(e_w16[:, bass.ds(i * EPG + n, 1), 0, :].rearrange("p a c -> p (a c)"),
                               e_stage[:, :], ACT.Copy, scale=W_SCALE).then_inc(sems["w_hi"], 1)

            act.wait_ge(sems["ld_const"], 64)
            for n, (a, b) in enumerate(W_PIECES):
                act.wait_ge(sems[f"ld_w{n}"], 16)
                act.activation(w16[:, 0, a:b], w_stage[:, a:b], ACT.Copy, scale=W_SCALE).then_inc(sems["ws_hi"], 1)
            with act.Fori(0, GROUPS) as i:
                need(act, "ld_xT", i)
                need(act, "kv_proj", i, 0)
                act.activation(xT16[:, 0, :, :], xT[:, :, :], ACT.Copy).then_inc(sems["xT_hi"], 1)
                for c in range(KC):
                    need(act, "q_proj", i, c + 1)
                    if c == 0:
                        need(act, "attn_nd", i, 0)
                    act.activation(qd[:, c, :], bP[c][:, :], ACT.Relu, bias=bq_col[:, c:c + 1], scale=W_BACK
                                   ).then_inc(sems["q_relu"], 1)
                need(act, "ld_ctx", i)
                need(act, "ctx_in", i, 0)
                act.activation(c_parts[:, 0, :, :], c_stage[:, :, :], ACT.Copy).then_inc(sems["ctx_hi"], 1)
                need(act, "ld_v", i)
                need(act, "pv_done", i, 0)
                act.activation(v16[:, 0, :, :, :], v_stage[:, :, :, :], ACT.Copy).then_inc(sems["v_hi"], 1)
                for q in range(TQ):
                    need(act, "kv_read", i, 2 * q + 1)
                    act.activation(kb[:, q, :], kb[:, q, :], ACT.Relu, scale=const("decay_col")
                                   ).then_inc(sems["k_relu"], 1)
                for q in range(TQ):
                    need(act, "attn_nd", i, 2 * (q + 1))
                    if q >= 2:
                        need(act, "attn_div", i, q - 1)
                    act.activation(den[:, q % 2, :], bN[:, D:2 * D], ACT.Identity, bias=const("eps")
                                   ).then_inc(sems["attn_den"], 1)
                    need(act, "attn_div", i, q + 1)
                    if q >= 2:
                        need(act, "wo_done", i, q - 1)
                    else:
                        need(act, "wo_done", i, 0)
                    act.activation(a16[:, q % 2, 0, :, :], a32[:, q % 2, :].rearrange("p (c n) -> p c n", c=KC), ACT.Copy
                                   ).then_inc(sems["attn_hi"], 1)
                    split_expert(i, q)

                def x1T_hi(q):
                    need(act, "x1T", i, q + 1)
                    if q == 0:
                        need(act, "st_done", i, 0)
                    act.activation(xh[0:C, 0, q, :, :].rearrange("p b (h s) -> p h b s", h=HPG),
                                   bT[0:C, :].rearrange("p (h b s) -> p h b s", h=HPG, b=2), ACT.Copy
                                   ).then_inc(sems["x1T_hi"], 1)

                x1T_hi(0)
                for step in range(GB + 6):
                    if step % 2 == 0 and step // 2 + 1 < TQ:
                        x1T_hi(step // 2 + 1)
                    if 1 <= step <= GB:
                        b = step - 1
                        need(act, "m_T", i, b + 1)
                        act.activation(xh[C:C + NG, 0, b // 2, b % 2, :], half(bP[0])[0:NG, 0:HPG * S], ACT.Copy,
                                       scale=-1.0).then_inc(sems["m_copied"], 1)
                    if 2 <= step < GB + 2:
                        b = step - 2
                        need(act, "st_done", i, b + 1)
                        if b >= 2:
                            need(act, "e_hi", i, b - 1)
                            need(act, "e_lo", i, b - 1)
                        act.activation(e32[:, b % 2, :, :], bE[:, :].rearrange("p (g n) -> p g n", g=2), ACT.Exp,
                                       scale=HD ** -0.5).then_inc(sems["exp_done"], 1)
                    if step >= 5 and step % 2 and step < GB + 5:
                        q = (step - 5) // 2
                        need(act, "aT", i, q + 1)
                        need(act, "wc_done", i, max(q - 1, 0))
                        act.activation(aT16[:, q % 2, 0, :, :].rearrange("p e (b s) -> p b e s", b=2),
                                       bT[:, 0:D].rearrange("p (b e s) -> p b e s", b=2, e=2), ACT.Copy
                                       ).then_inc(sems["aT_hi"], 1)
                for q in range(TQ):
                    need(act, "x2_norm", i, q + 1)
                    if q == 0:
                        need(act, "scattered", i, 0)
                        need(act, "x2T", i, 0)
                    act.activation(row16[:, q, 0:D], x2[:, q, :], ACT.Copy).then_inc(sems["row_hi"], 1)
                need(act, "r_chain", i, R_SHIFT)
                act.activation(ex[:, :, :], shifted[:, :, :], ACT.Exp).then_inc(sems["r_exp"], 1)
                act.activation(sg_e[:, :], lg[:, :, E], ACT.Exp, scale=-1.0).then_inc(sems["r_exp"], 1)
                for c in range(IC + 1):
                    if c < IC:
                        n = chunk_rows(c)
                        need(act, "g_done", i, c + 1)
                        if c == 0:
                            need(act, "e_hi", i)
                            need(act, "e_lo", i)
                        if c >= 2:
                            need(act, "h_mul", i, c - 1)
                        act.activation(gate[0:n, c % 2, :], (bK[0], bP[1])[c % 2][0:n, :], ACT.Silu, scale=W_BACK
                                       ).then_inc(sems["silu"], 1)
                    if c >= 1:
                        n = chunk_rows(c - 1)
                        need(act, "h_mul", i, c)
                        if c == 1:
                            need(act, "down", i, 0)
                        act.activation(h16[0:n, 0, c - 1, :], h32[0:n, (c - 1) % 2, :], ACT.Copy
                                       ).then_inc(sems["h_hi"], 1)

            def slot_silu(j, p):
                act.wait_ge(slot_sem["e_gu"][p], j + 1)
                act.wait_ge(slot_sem["e_mul"][p], j)
                act.activation(e_gate[:, p, :], bP[p][:, 0:IM], ACT.Silu, scale=W_BACK).then_inc(slot_sem["e_silu"][p], 1)

            def slot_h_hi(j, p):
                act.wait_ge(slot_sem["e_hT"][p], j + 1)
                act.wait_ge(slot_sem["e_y"][p], j)
                act.activation(ehT[:, p, 0, :, :], bK[p][:, 0:KC * P].rearrange("p (k n) -> p k n", k=KC), ACT.Copy
                               ).then_inc(slot_sem["e_hhi"][p], 1)

            def slot_weighted(j, p):
                e = act.value_load(tab[0:1, bass.ds(2 * j + p, 1)], min_val=0, max_val=E - 1)
                act.wait_ge(slot_sem["e_y"][p], j + 1)
                act.wait_ge(slot_sem["meta"][p], j + 1)
                act.wait_ge(slot_sem["e_add"][p], 16 * j)
                act.activation(ye[:, p, :], (bN, bW)[p][:, 0:D], ACT.Copy, scale=meta[:, p, bass.ds(e, 1)]
                               ).then_inc(slot_sem["e_yw"][p], 1)

            act.wait_ge(sems["t_tab"], 1)
            laps = act.value_load(tab[0:1, TAB_LAPS:TAB_LAPS + 1], min_val=0, max_val=P // 2 - 1)
            slot_silu(0, 0)
            slot_silu(0, 1)
            slot_h_hi(0, 0)
            with act.Fori(0, laps) as j:
                slot_weighted(j, 0)
                slot_silu(j + 1, 0)
                slot_h_hi(j, 1)
                slot_weighted(j, 1)
                slot_silu(j + 1, 1)
                slot_h_hi(j + 1, 0)
            slot_weighted(laps, 0)
            slot_h_hi(laps, 1)
            slot_weighted(laps, 1)
            with act.Fori(0, N // P // 2) as j:
                for p in range(2):
                    act.wait_ge(slot_sem["f_out"][p], j + 1)
                    act.dma_start(out[bass.ds(j * 2 * P + p * P, P), :], fo[:, p, :]).then_inc(slot_sem["f_st"][p], 16)

        @block.vector
        def _(dve):
            dve.memset(vb[:, :, :, P:P + 1], 1.0).then_inc(sems["setup"], 1)
            dve.memset(mask16[:, TQ, :], 0.0).then_inc(sems["setup"], 1)
            dve.wait_ge(sems["ld_const"], 64)
            dve.tensor_copy(token[:, :], const("token")).then_inc(sems["setup"], 1)
            dve.tensor_copy(count[:, :], const("region")).then_inc(sems["setup"], 1)
            dve.wait_ge(sems["setup"], SETUP)
            for n, (a, b) in enumerate(W_PIECES):
                dve.wait_ge(sems["ws_hi"], n + 1)
                dve.scalar_tensor_tensor(w16[:, 1, a:b], w_stage[:, a:b], W_SCALE, w16[:, 0, a:b], ALU.mult,
                                         ALU.subtract).then_inc(sems["ws_lo"], 1)

            def split_expert(i, n):
                need(dve, "w_hi", i, n + 1)
                w = e_w16[:, bass.ds(i * EPG + n, 1), :, :].rearrange("p a s c -> p (a s) c")
                dve.scalar_tensor_tensor(w[:, 1, :], e_stage[:, :], W_SCALE, w[:, 0, :], ALU.mult,
                                         ALU.subtract).then_inc(sems["w_lo"], 1)

            def norm_stats(i, q, ln, total, stat, mv):
                need(dve, f"{ln}_sum", i, q + 1)
                dve.bn_stats(stat[:, q, :], total[:, q, :]).then_inc(sems[f"{ln}_stat"], 1)
                apart(dve, sems[f"{ln}_stat"], i * PER[f"{ln}_stat"] + q + 1)
                dve.bn_aggr(mv[:, q, :], stat[:, q, :]).then_inc(sems[f"{ln}_mv"], 1)

            with dve.Fori(0, GROUPS) as i:
                need(dve, "xT_hi", i)
                need(dve, "kv_proj", i, 0)
                dve.tensor_tensor(xT16[:, 1, :, :], xT[:, :, :], xT16[:, 0, :, :], ALU.subtract).then_inc(sems["xT_lo"], 1)
                for q in range(TQ):
                    need(dve, "kv_proj", i, q + 1)
                    if q == 0:
                        need(dve, "kv_state", i, 0)
                    keys, vals = bP[q % 2][:, 0:D], bP[q % 2][:, D:2 * D]
                    dve.scalar_tensor_tensor(kb[:, q, :], keys, W_BACK, bk_row, ALU.mult, ALU.add
                                             ).then_inc(sems["kv_read"], 1)
                    dve.scalar_tensor_tensor(vb[:, q, :, 0:P], vals.rearrange("p (c n) -> p c n", c=KC), W_BACK,
                                             bv_row.rearrange("p (c n) -> p c n", c=KC), ALU.mult, ALU.add
                                             ).then_inc(sems["kv_read"], 1)

                def state_masks(b):
                    need(dve, "kv_state", i, b + 1)
                    if b >= 2:
                        need(dve, "attn_nd", i, b - 1)
                    st = bK[b % 2][:, 0:KC * (P + 1)].rearrange("p (c n) -> p c n", c=KC)
                    blocks = bc(head_mask.unsqueeze(1), [P, KC, P])
                    dve.tensor_tensor(kv_m[:, b % 2, :, :], st[:, :, 0:P], blocks, ALU.mult).then_inc(sems["kv_masked"], 1)
                    dve.tensor_tensor(k_sum[:, b % 2, :, :], bc(st[:, :, P:P + 1], [P, KC, P]), blocks, ALU.mult
                                      ).then_inc(sems["kv_masked"], 1)

                def attention_rows(q):
                    need(dve, "attn_den", i, q + 1)
                    if q >= 2:
                        need(dve, "attn_hi", i, q - 1)
                        need(dve, "attn_lo", i, q - 1)
                    dve.reciprocal(den[:, q % 2, :], den[:, q % 2, :]).then_inc(sems["attn_rec"], 1)
                    need(dve, "attn_rec", i, q + 1)
                    dve.tensor_tensor(a32[:, q % 2, :], bN[:, 0:D], den[:, q % 2, :], ALU.mult).then_inc(sems["attn_div"], 1)
                    need(dve, "attn_hi", i, q + 1)
                    need(dve, "attn_div", i, q + 1)
                    if q >= 2:
                        need(dve, "wo_done", i, q - 1)
                    dve.tensor_tensor(a16[:, q % 2, 1, :, :], a32[:, q % 2, :].rearrange("p (c n) -> p c n", c=KC),
                                      a16[:, q % 2, 0, :, :], ALU.subtract).then_inc(sems["attn_lo"], 1)

                def first_norm(q):
                    need(dve, "wo_done", i, q + 1)
                    if q == 0:
                        need(dve, "x_bo", i)
                        need(dve, "x1T", i, 0)
                        need(dve, "x1_bc", i, 0)
                    dve.scalar_tensor_tensor(x1[:, q, :], bW[:, 0:D], W_BACK, x_in[:, q, :], ALU.mult, ALU.add
                                             ).then_inc(sems["ln1_sum"], 1)
                    norm_stats(i, q, "ln1", x1, stat1, mv1)

                def first_normed(q):
                    need(dve, "ln1_rstd", i, RSQRT * (q + 1))
                    need(dve, "ln1_mv", i, q + 1)
                    dve.tensor_scalar(x1[:, q, :], x1[:, q, :], mv1[:, q, 0:1], rstd1[:, q:q + 1], ALU.subtract,
                                      ALU.mult).then_inc(sems["x1_norm"], 1)

                for b in range(GB + 1):
                    if b < GB:
                        state_masks(b)
                    if b >= 2 and b % 2 == 0:
                        q = b // 2 - 1
                        attention_rows(q)
                        if q >= 1:
                            first_norm(q - 1)
                            split_expert(i, q - 1)
                        if q >= 2:
                            first_normed(q - 2)
                first_norm(TQ - 1)
                first_normed(TQ - 2)
                first_normed(TQ - 1)
                split_expert(i, TQ - 1)

                def x1T_lo(q):
                    need(dve, "x1T_hi", i, q + 1)
                    if q == 0:
                        need(dve, "st_done", i, 0)
                    dve.tensor_tensor(xh[0:C, 1, q, :, :].rearrange("p b (h s) -> p h b s", h=HPG),
                                      bT[0:C, :].rearrange("p (h b s) -> p h b s", h=HPG, b=2),
                                      xh[0:C, 0, q, :, :].rearrange("p b (h s) -> p h b s", h=HPG), ALU.subtract
                                      ).then_inc(sems["x1T_lo"], 1)

                def second_norm(q):
                    need(dve, "wc_done", i, q + 1)
                    need(dve, "x1_bc", i, q + 1)
                    if q == 0:
                        need(dve, "row_hi", i, 0)
                        need(dve, "row_lo", i, 0)
                        need(dve, "st_acc", i, 0)
                    dve.scalar_tensor_tensor(x2[:, q, :], bW[:, 0:D], W_BACK, x_in[:, q, :], ALU.mult, ALU.add
                                             ).then_inc(sems["ln2_sum"], 1)
                    norm_stats(i, q, "ln2", x2, stat2, mv2)

                def second_normed(q):
                    need(dve, "ln2_rstd", i, RSQRT * (q + 1))
                    need(dve, "ln2_mv", i, q + 1)
                    dve.tensor_scalar(x2[:, q, :], x2[:, q, :], mv2[:, q, 0:1], rstd2[:, q:q + 1], ALU.subtract,
                                      ALU.mult).then_inc(sems["x2_norm"], 1)

                x1T_lo(0)
                for step in range(GB + 6):
                    if step % 2 == 0 and step // 2 + 1 < TQ:
                        x1T_lo(step // 2 + 1)
                    if step < GB:
                        need(dve, "s_done", i, step + 1)
                        if step >= 2:
                            need(dve, "m_T", i, step - 1)
                        with nc.allow_low_precision("any value near the maximum guards the softmax"):
                            dve.tensor_reduce(m16[:, step % 2, :], bK[step % 2][:, :].rearrange("p (a t) -> p a t", t=S),
                                              AX, ALU.max).then_inc(sems["s_max"], 1)
                    if 2 <= step < GB + 2:
                        b = step - 2
                        need(dve, "exp_done", i, b + 1)
                        if b >= 2:
                            need(dve, "pv_done", i, b - 1)
                        dve.tensor_copy(e16[:, b % 2, 0, :, :], e32[:, b % 2, :, :]).then_inc(sems["e_hi"], 1)
                    if 3 <= step < GB + 3:
                        b = step - 3
                        o = (bN, bP[1])[b % 2][:, 0:2 * NG * (HD + 1)].rearrange("p (a n) -> p a n", n=HD + 1)
                        need(dve, "pv_done", i, b + 1)
                        if b >= 2:
                            need(dve, "pv_norm", i, b - 1)
                        if b == 0:
                            need(dve, "aT", i, 0)
                        dve.reciprocal(rec[:, b % 2, :], o[:, :, HD]).then_inc(sems["pv_rec"], 1)
                        need(dve, "pv_rec", i, b + 1)
                        dve.tensor_tensor(a2[:, b, :].rearrange("p (a d) -> p a d", d=HD), o[:, :, 0:HD],
                                          bc(rec[:, b % 2, :].unsqueeze(2), [P, 2 * NG, HD]), ALU.mult
                                          ).then_inc(sems["pv_norm"], 1)
                    if step >= 5 and step % 2 and step < GB + 5:
                        q = (step - 5) // 2
                        need(dve, "aT_hi", i, q + 1)
                        if q >= 2:
                            need(dve, "wc_done", i, q - 1)
                        dve.tensor_tensor(aT16[:, q % 2, 1, :, :].rearrange("p e (b s) -> p b e s", b=2),
                                          bT[:, 0:D].rearrange("p (b e s) -> p b e s", b=2, e=2),
                                          aT16[:, q % 2, 0, :, :].rearrange("p e (b s) -> p b e s", b=2), ALU.subtract
                                          ).then_inc(sems["aT_lo"], 1)
                    if step >= 6 and step % 2 == 0:
                        q = (step - 6) // 2
                        second_norm(q)
                        if q >= 1:
                            second_normed(q - 1)
                second_normed(TQ - 1)

                for q in range(TQ):
                    need(dve, "x2T", i, q + 1)
                    if q == 0:
                        need(dve, "u_done", i, 0)
                    dve.tensor_copy(x2T16[:, :, :, q * P:(q + 1) * P].rearrange("p s k n -> p (s k) n"),
                                    half(bT)[:, 0:2 * KC * P].rearrange("p (a n) -> p a n", n=P)
                                    ).then_inc(sems["x2T_read"], 1)

                done = [0]

                def link(instruction):
                    done[0] += 1
                    instruction.then_inc(sems["r_chain"], 1)
                    apart(dve, sems["r_chain"], i * PER["r_chain"] + done[0])

                need(dve, "router", i)
                link(dve.tensor_scalar(lg[:, :, :], bP[0][:, 0:TQ * (E + 1)].rearrange("p (q e) -> p q e", e=E + 1),
                                       W_BACK, None, ALU.mult))
                logits = lg[:, :, 0:E]
                link(dve.tensor_reduce(lg_max[:, :], logits, AX, ALU.max))
                link(dve.tensor_tensor(shifted[:, :, :], logits, bc(lg_max[:, :].unsqueeze(2), [P, TQ, E]), ALU.subtract))
                assert done[0] == R_SHIFT
                need(dve, "r_exp", i, 1)
                link(dve.tensor_reduce(ex_sum[:, :], ex[:, :, :], AX, ALU.add))
                link(dve.reciprocal(ex_rec[:, :], ex_sum[:, :]))
                link(dve.tensor_tensor(prob[:, :, :], ex[:, :, :], bc(ex_rec[:, :].unsqueeze(2), [P, TQ, E]), ALU.mult))
                for q in range(TQ):
                    link(dve.max(top_v[:, q, :], prob[:, q, :]))
                for q in range(TQ):
                    link(dve.max_index(top_i[:, q, :], top_v[:, q, :], prob[:, q, :]))
                link(dve.tensor_copy(top_f[:, :, :], top_i[:, :, 0:TOPK]))
                link(dve.tensor_tensor(onehot[:, :, :, :].rearrange("p q j e -> p (q j) e"),
                                       bc(top_f[:, :, :].rearrange("p q j -> p (q j)").unsqueeze(2), [P, TQ * TOPK, E]),
                                       bc(const("iota").unsqueeze(1), [P, TQ * TOPK, E]), ALU.is_equal))
                with nc.allow_low_precision("zeros and ones"):
                    link(dve.tensor_reduce(mask16[:, 0:TQ, :], onehot[:, :, :, :].rearrange("p q j e -> p q e j"),
                                           AX, ALU.add))
                assert done[0] == R_MASK
                link(dve.tensor_reduce(w_sum[:, :], top_v[:, :, 0:TOPK], AX, ALU.add))
                link(dve.tensor_scalar(w_clip[:, :], w_sum[:, :], TOP_MIN, None, ALU.max))
                link(dve.reciprocal(w_rec[:, :], w_clip[:, :]))
                link(dve.tensor_tensor(chosen[:, :, :], mask16[:, 0:TQ, :], prob[:, :, :], ALU.mult))
                need(dve, "scattered", i, 0)
                link(dve.scalar_tensor_tensor(row[:, :, D:D + E], chosen[:, :, :], W_BACK,
                                              bc(w_rec[:, :].unsqueeze(2), [P, TQ, E]), ALU.mult, ALU.mult))
                link(dve.tensor_copy(row[:, :, ROW - 1:ROW].bitcast(U32), token[:, :].unsqueeze(2)))
                link(dve.tensor_scalar(token[:, :], token[:, :], float(GT), None, ALU.add))
                need(dve, "r_exp", i)
                link(dve.tensor_scalar(sg_d[:, :], sg_e[:, :], 1.0, W_SCALE, ALU.add, ALU.mult))
                link(dve.reciprocal(sg[:, :], sg_d[:, :]))

                for c in range(IC):
                    n, bu = chunk_rows(c), (bK[1], bN)[c % 2]
                    need(dve, "u_done", i, c + 1)
                    need(dve, "silu", i, c + 1)
                    if c >= 2:
                        need(dve, "h_hi", i, c - 1)
                        need(dve, "h_lo", i, c - 1)
                    dve.scalar_tensor_tensor(h32[0:n, c % 2, :], bu[0:n, :], W_BACK, gate[0:n, c % 2, :], ALU.mult,
                                             ALU.mult).then_inc(sems["h_mul"], 1)
                    need(dve, "h_hi", i, c + 1)
                    need(dve, "h_mul", i, c + 1)
                    if c == 0:
                        need(dve, "down", i, 0)
                    dve.tensor_tensor(h16[0:n, 1, c, :], h32[0:n, c % 2, :], h16[0:n, 0, c, :], ALU.subtract
                                      ).then_inc(sems["h_lo"], 1)
                    if c == 3:
                        need(dve, "rank", i)
                        link(dve.tensor_tensor(pos[:, :, :], bE[:, 0:TQ * E].rearrange("p (q e) -> p q e", e=E),
                                               bc(count[:, :].unsqueeze(1), [P, TQ, E]), ALU.add))
                        link(dve.tensor_tensor(count[:, :], count[:, :], bE[:, TQ * E:(TQ + 1) * E], ALU.add))
                        link(dve.tensor_tensor(pos_sel[:, :, :, :], onehot[:, :, :, :],
                                               bc(pos[:, :, :].unsqueeze(2), [P, TQ, TOPK, E]), ALU.mult))
                        link(dve.tensor_reduce(pos_f[:, :], pos_sel[:, :, :, :].rearrange("p q j e -> p (q j) e"),
                                               AX, ALU.add))
                        link(dve.tensor_copy(pos_u[:, :], pos_f[:, :]))
                assert done[0] == R_CHAIN, done[0]

                for q in range(TQ):
                    need(dve, "down", i, q + 1)
                    dve.scalar_tensor_tensor(x2[:, q, :], (bW, bT)[q % 2][:, 0:D], sg[:, q:q + 1], x2[:, q, :],
                                             ALU.mult, ALU.add).then_inc(sems["acc_row"], 1)

            tdone = [0]

            def tlink(instruction):
                tdone[0] += 1
                instruction.then_inc(sems["t_chain"], 1)
                dve.wait_ge(sems["t_chain"], tdone[0])

            tlink(dve.tensor_tensor(passed[:, :], count[:, :], const("region"), ALU.subtract))
            tlink(dve.tensor_tensor(more[:, :, :], bc(passed[:, :].unsqueeze(2), [P, E, E]),
                                    bc(const("steps").unsqueeze(1), [P, E, E]), ALU.is_gt))
            tlink(dve.tensor_reduce(tiles[:, :], more[:, :, :], AX, ALU.add))
            tlink(dve.tensor_tensor(tiles_to[:, :, :], bc(tiles[:, :].unsqueeze(1), [P, E, E]),
                                    const("upto").rearrange("p (a b) -> p a b", a=E), ALU.mult))
            tlink(dve.tensor_reduce(cum[:, :], tiles_to[:, :, :], AX, ALU.add))
            tlink(dve.tensor_scalar(passed[:, :], cum[:, :], const("slot"), None, ALU.is_le))
            tlink(dve.tensor_tensor(passed_t[:, :], passed[:, :], tiles[:, :], ALU.mult))
            tlink(dve.tensor_reduce(slot_f[:, 2:3], passed[:, :], AX, ALU.add))
            tlink(dve.tensor_reduce(slot_f[:, 3:4], passed_t[:, :], AX, ALU.add))
            tlink(dve.tensor_scalar(slot_f[:, 0:1], slot_f[:, 2:3], float(E - 1), None, ALU.min))
            tlink(dve.tensor_tensor(slot_f[:, 4:5], const("slot"), slot_f[:, 3:4], ALU.subtract))
            tlink(dve.tensor_scalar(slot_f[:, 5:6], slot_f[:, 4:5], float(P), None, ALU.mult))
            tlink(dve.scalar_tensor_tensor(slot_f[:, 1:2], slot_f[:, 2:3], float(REGION), slot_f[:, 5:6], ALU.mult,
                                           ALU.add))
            tlink(dve.tensor_scalar(evens_below[:, :], const("evens"), cum[:, E - 1:E], None, ALU.is_lt))
            tlink(dve.tensor_reduce(slot_f[:, 7:8], evens_below[:, :], AX, ALU.add))
            tlink(dve.tensor_copy(tab[0:1, TAB_PAD:TAB_PAD + E], count[0:1, :]))
            tlink(dve.tensor_copy(tab[0:1, TAB_LAPS:TAB_LAPS + 1], slot_f[0:1, 7:8]))
            tlink(dve.memset(eh[:, :, :], 0.0))
            assert tdone[0] == T_CHAIN
            dve.wait_ge(sems["t_rows"], 1)
            dve.tensor_copy(tab[0:1, 0:2 * P], bP[0][0:1, 0:2 * P]).then_inc(sems["t_tab"], 1)

            def slot_read(j, p):
                dve.wait_ge(slot_sem["xg_T"][p], j + 1)
                dve.wait_ge(slot_sem["e_gu"][p], j)
                dve.tensor_copy(xgT[:, p, :, :], half((bT, bE)[p])[:, 0:2 * KC * P].rearrange("p (a n) -> p a n", n=P)
                                ).then_inc(slot_sem["xg_read"][p], 1)

            def slot_product(j, p):
                dve.wait_ge(slot_sem["e_yw"][p], j)
                dve.wait_ge(slot_sem["e_id"][p], j)
                dve.tensor_copy(meta[:, p, :].bitcast(U32), xg[:, p, D:ROW].bitcast(U32)).then_inc(slot_sem["meta"][p], 1)
                dve.wait_ge(slot_sem["e_silu"][p], j + 1)
                dve.wait_ge(slot_sem["e_hT"][p], j)
                dve.scalar_tensor_tensor(eh[:, p, 0:IM], bP[p][:, IM:2 * IM], W_BACK, e_gate[:, p, :], ALU.mult, ALU.mult
                                         ).then_inc(slot_sem["e_mul"][p], 1)

            def slot_h_lo(j, p):
                dve.wait_ge(slot_sem["e_hhi"][p], j + 1)
                dve.tensor_tensor(ehT[:, p, 1, :, :], bK[p][:, 0:KC * P].rearrange("p (k n) -> p k n", k=KC),
                                  ehT[:, p, 0, :, :], ALU.subtract).then_inc(slot_sem["e_hlo"][p], 1)

            dve.wait_ge(sems["t_tab"], 1)
            laps = dve.value_load(tab[0:1, TAB_LAPS:TAB_LAPS + 1], min_val=0, max_val=P // 2 - 1)
            slot_read(0, 0)
            slot_product(0, 0)
            slot_read(0, 1)
            slot_product(0, 1)
            slot_h_lo(0, 0)
            with dve.Fori(0, laps) as j:
                slot_read(j + 1, 0)
                slot_product(j + 1, 0)
                slot_h_lo(j, 1)
                slot_read(j + 1, 1)
                slot_product(j + 1, 1)
                slot_h_lo(j + 1, 0)
            slot_h_lo(laps, 1)

            with dve.Fori(0, N // P // 2) as j:
                for p in range(2):
                    dve.wait_ge(slot_sem["f_in"][p], 32 * (j + 1))
                    dve.wait_ge(slot_sem["f_out"][p], j)
                    dve.tensor_tensor(fsum[:, p, :], fa[:, p, 0, :], fa[:, p, 1, :], ALU.add).then_inc(slot_sem["f_sum"][p], 1)
                    dve.wait_ge(slot_sem["f_sum"][p], j + 1)
                    dve.bn_stats(fstat[:, p, :], fsum[:, p, :]).then_inc(slot_sem["f_stat"][p], 1)
                    apart(dve, slot_sem["f_stat"][p], j + 1)
                    dve.bn_aggr(fmv[:, p, :], fstat[:, p, :]).then_inc(slot_sem["f_mv"][p], 1)
                for p in range(2):
                    dve.wait_ge(slot_sem["f_rstd"][p], RSQRT * (j + 1))
                    dve.wait_ge(slot_sem["f_st"][p], 16 * j)
                    dve.tensor_scalar(fo[:, p, :], fsum[:, p, :], fmv[:, p, 0:1], frstd[:, p:p + 1], ALU.subtract,
                                      ALU.mult).then_inc(slot_sem["f_out"][p], 1)

        @block.gpsimd
        def _(pool):
            def inverse_root(root, variance, minus_half, chain, before, ready, value):
                apart(pool, ready, value)
                pool.tensor_scalar(minus_half, variance, LN_EPS, -0.5, ALU.add, ALU.mult).then_inc(chain, 1)
                apart(pool, chain, before + 1)
                pool.tensor_scalar(root.bitcast(I32), minus_half.bitcast(I32), -0.5, ROOT_GUESS, ALU.mult, ALU.add
                                   ).then_inc(chain, 1)
                for n in range(RSQRT_STEPS):
                    apart(pool, chain, before + 2 + 2 * n)
                    pool.tensor_scalar(newton[:, :], root, root, minus_half, ALU.mult, ALU.mult).then_inc(chain, 1)
                    apart(pool, chain, before + 3 + 2 * n)
                    pool.tensor_scalar(root, newton[:, :], 1.5, root, ALU.add, ALU.mult).then_inc(chain, 1)

            pool.memset(c16[0:C, :, :, :], 0.0).then_inc(sems["setup"], 1)
            pool.memset(v_stage[:, :, :, :], 0.0).then_inc(sems["setup"], 1)
            pool.memset(zeros[:, :], 0.0).then_inc(sems["setup"], 1)
            pool.memset(pad_row[:, 0:ROW - 1], 0.0)
            pool.memset(pad_row[:, ROW - 1:ROW].bitcast(U32), NO_TOKEN).then_inc(sems["setup"], 1)
            for g in range(2):
                pool.wait_ge(sems["setup"], SETUP - 1)
                w = g * (HD + 1) + HD
                ones = pool.memset(v_stage[g * S:(g + 1) * S, :, :, w:w + 1], 1.0)
            ones.then_inc(sems["setup"], 1)

            with pool.Fori(0, GROUPS) as i:
                need(pool, "ld_x", i)
                pool.tensor_tensor(x_in[:, :, :], x_in[:, :, :], bc(bo_row.unsqueeze(1), [P, TQ, D]), ALU.add
                                   ).then_inc(sems["x_bo"], 1)
                for c in range(KC):
                    need(pool, "q_relu", i, c + 1)
                    queries = qd[:, c, :].rearrange("p (b s) -> p b s", s=S)
                    pool.tensor_tensor(queries, queries, bc(decay_row.unsqueeze(1), [P, GB, S]), ALU.mult
                                       ).then_inc(sems["q_decay"], 1)
                need(pool, "ctx_hi", i)
                need(pool, "ctx_in", i, 0)
                pool.tensor_tensor(c_parts[:, 1, :, :], c_stage[:, :, :], c_parts[:, 0, :, :], ALU.subtract
                                   ).then_inc(sems["ctx_lo"], 1)
                need(pool, "v_hi", i)
                need(pool, "pv_done", i, 0)
                pool.tensor_tensor(v16[:, 1, :, :, :].rearrange("p b g n -> p (b g n)"),
                                   v_stage[:, :, :, :].rearrange("p b g n -> p (b g n)"),
                                   v16[:, 0, :, :, :].rearrange("p b g n -> p (b g n)"), ALU.subtract
                                   ).then_inc(sems["v_lo"], 1)
                for q in range(TQ):
                    if q == 0:
                        need(pool, "x1_norm", i, 0)
                    inverse_root(rstd1[:, q:q + 1], mv1[:, q, 1:2], half1[:, q:q + 1], sems["ln1_rstd"],
                                 i * TQ * RSQRT + q * RSQRT, sems["ln1_mv"], i * TQ + q + 1)
                for q in range(TQ):
                    need(pool, "x1_norm", i, q + 1)
                    need(pool, "ln1_sum", i, q + 1)
                    pool.tensor_tensor(x_in[:, q, :], x1[:, q, :], bc_row, ALU.add).then_inc(sems["x1_bc"], 1)
                for step in range(2, GB + 7):
                    if step < GB + 2:
                        b = step - 2
                        need(pool, "e_hi", i, b + 1)
                        need(pool, "exp_done", i, b + 1)
                        if b >= 2:
                            need(pool, "pv_done", i, b - 1)
                        pool.tensor_tensor(e16[:, b % 2, 1, :, :], e32[:, b % 2, :, :], e16[:, b % 2, 0, :, :],
                                           ALU.subtract).then_inc(sems["e_lo"], 1)
                    if step >= 6 and step % 2 == 0 and step < GB + 6:
                        q = (step - 6) // 2
                        if q == 0:
                            need(pool, "x2_norm", i, 0)
                        inverse_root(rstd2[:, q:q + 1], mv2[:, q, 1:2], half2[:, q:q + 1], sems["ln2_rstd"],
                                     i * TQ * RSQRT + q * RSQRT, sems["ln2_mv"], i * TQ + q + 1)
                for q in range(TQ):
                    need(pool, "row_hi", i, q + 1)
                    pool.tensor_tensor(row16[:, q, D:2 * D], x2[:, q, :], row16[:, q, 0:D], ALU.subtract
                                       ).then_inc(sems["row_lo"], 1)
                need(pool, "r_chain", i)
                apart(pool, sems["row_lo"], (i + 1) * PER["row_lo"])
                for q in range(TQ):
                    for k in range(TOPK):
                        a = q * TOPK + k
                        pool.indirect_dma_start(xs, bass.IndirectOffsetOnAxis(ap=pos_u[:, a:a + 1], axis=0),
                                                row[:, q, :], None).then_inc(sems["scattered"], 16)

            need(pool, "st_acc", GROUPS - 1)
            pool.wait_ge(sems["st_zero"], 16)
            pool.wait_ge(sems["t_tab"], 1)
            laps = pool.value_load(tab[0:1, TAB_LAPS:TAB_LAPS + 1], min_val=0, max_val=P // 2 - 1)
            with pool.Fori(0, laps + 1) as j:
                for p in range(2):
                    apart(pool, slot_sem["e_add"][p], 16 * j)
                    apart(pool, slot_sem["meta"][p], j + 1)
                    pool.tensor_copy(ids[:, p:p + 1], meta[:, p, E:E + 1].bitcast(U32)).then_inc(slot_sem["e_id"][p], 1)
                    apart(pool, slot_sem["e_yw"][p], j + 1)
                    apart(pool, slot_sem["e_id"][p], j + 1)
                    pool.indirect_dma_start(acc[p], bass.IndirectOffsetOnAxis(ap=ids[:, p:p + 1], axis=0), ye[:, p, :],
                                            None, bounds_check=N - 1, oob_is_err=False, compute_op=ALU.add
                                            ).then_inc(slot_sem["e_add"][p], 16)
            with pool.Fori(0, N // P // 2) as j:
                for p in range(2):
                    pool.wait_ge(slot_sem["f_out"][p], j)
                    inverse_root(frstd[:, p:p + 1], fmv[:, p, 1:2], fhalf[:, p:p + 1], slot_sem["f_rstd"][p],
                                 j * RSQRT, slot_sem["f_mv"][p], j + 1)


ROOT_GUESS = float(0x5f3759df - (1 << 30) - (1 << 22))
R_SHIFT, R_MASK = 3, 17
T_CHAIN = 18


def constants():
    import numpy as np
    cf = {
        "ident": np.eye(P), "head_mask": np.kron(np.eye(P // HD), np.ones((HD, HD))),
        "decay_row": np.broadcast_to(np.exp(-np.arange(S, dtype=np.float32) / np.float32(S)), (P, S)),
        "decay_col": np.exp(-(np.arange(P, dtype=np.float32) % S) / np.float32(S))[:, None],
        "slot": np.arange(P)[:, None], "token": np.arange(P)[:, None] + P * np.arange(TQ),
        "eps": np.full((P, 1), ATTN_EPS), "iota": np.broadcast_to(np.arange(E), (P, E)),
        "region": np.broadcast_to(REGION * np.arange(E), (P, E)),
        "steps": np.broadcast_to(P * np.arange(E), (P, E)),
        "evens": np.broadcast_to(2 + 2 * np.arange(P // 2), (P, P // 2)),
        "upto": np.broadcast_to(np.tri(E).reshape(-1), (P, E * E)),
    }
    cf = np.concatenate([cf[name].astype(np.float32) for name in CF_PARTS], axis=1)
    ch = np.concatenate([np.eye(P), np.tri(P, k=-1).T, np.ones((P, P))], axis=1).astype(np.float16)
    pick = np.kron(np.eye(NG), np.ones(S)).astype(np.float16)
    return {"cf": cf, "ch": ch, "pick": np.ascontiguousarray(np.broadcast_to(pick[:, None, :], (NG, GB, NG * S)))}


def kernel(**inputs):
    import numpy as np
    import concourse.bacc as bacc
    from concourse.bass_utils import run_bass_kernel_spmd

    a = {k: np.asarray(v) for k, v in inputs.items()}
    pre = "L0_"

    def chunks(w):
        n = -(-w.shape[0] // P)
        full = np.zeros((n * P, w.shape[1]), w.dtype)
        full[:w.shape[0]] = w
        return full.reshape(n, P, w.shape[1]).transpose(1, 0, 2).reshape(P, -1)

    def by_head(w, axis=-1):
        w = np.moveaxis(w, axis, 0)
        return np.moveaxis(w.reshape(NG, HPG, HD, -1).swapaxes(0, 1).reshape(w.shape), 0, axis)

    wc = by_head(a[pre + "xattn_Wc"].T).reshape(NG, 2, 2, HD, D)
    wc = wc.transpose(2, 1, 0, 3, 4).reshape(D, D)
    w = [
        chunks(a[pre + "attn_Wq"].T),
        chunks(np.concatenate([a[pre + "attn_Wk"].T, a[pre + "attn_Wv"].T], axis=1)),
        chunks(by_head(a[pre + "attn_Wo"].T)), chunks(wc),
        chunks(by_head(np.concatenate([a[pre + "ffn_router_w"].T, a[pre + "ffn_sh_gate_w"]], axis=1), 0)),
        chunks(by_head(np.concatenate([a[pre + "ffn_sh_gate"], a[pre + "ffn_sh_up"]], axis=1), 0)),
        chunks(by_head(a[pre + "ffn_sh_down"])),
    ]
    gu = by_head(np.concatenate([a[pre + "ffn_w_gate"], a[pre + "ffn_w_up"]], axis=2), 1)
    down = by_head(a[pre + "ffn_w_down"])
    x = a["x"].reshape(N, D)
    data = {
        "x": by_head(x), "xT": np.ascontiguousarray(x.T).reshape(KC, P, N),
        "ctx": a["ctx_512"], "ctxT": np.ascontiguousarray(a["ctx_512"].transpose(2, 0, 1)),
        "bq": np.ascontiguousarray(a[pre + "attn_bq"].reshape(KC, P).T),
        "biases": np.concatenate([a[pre + "attn_bk"], a[pre + "attn_bv"], by_head(a[pre + "attn_bo"]),
                                  by_head(a[pre + "xattn_bc"])]),
        "w": np.concatenate(w, axis=1),
        "e_w": np.stack([np.concatenate([chunks(gu[e]), chunks(down[e])], axis=1) for e in range(E)]),
        **constants(),
    }
    nc = bacc.Bacc("TRN2", target_bir_lowering=False, num_devices=1)
    args = {k: nc.dram_tensor(f"in_{k}", v.shape, mybir.dt.from_np(v.dtype), kind="ExternalInput").ap()
            for k, v in data.items()}
    out = nc.dram_tensor("out_0", (N, D), F32, kind="ExternalOutput").ap()
    decoder_layer_program(nc, args, out)
    r = run_bass_kernel_spmd(nc, [{f"in_{k}": v for k, v in data.items()}], core_ids=[0])
    by_group = r.results[0]["out_0"].reshape(N, HPG, NG, HD).swapaxes(1, 2)
    return np.ascontiguousarray(by_group).reshape(B, S, D)
```

```python
from contextlib import ExitStack

import concourse.bass as bass
from concourse import mybir

F32, F16 = mybir.dt.float32, mybir.dt.float16
U32, I32 = mybir.dt.uint32, mybir.dt.int32
ALU = mybir.AluOpType
ACT = mybir.ActivationFunctionType
AX = mybir.AxisListType.X

P = 128
B, S, D = 32, 64, 256
N = B * S
KC = D // P
HD = 16
NG, HPG = 4, 4
C = NG * HD
AW = P + P // HD
VW = 2 * (HD + 1)
E, TOPK = 16, 4
IM, IS = 176, 704
IC = -(-IS // P)
W_SCALE = 64.0
W_BACK = 1.0 / W_SCALE
ATTN_EPS, LN_EPS, TOP_MIN = 1e-6, 1e-5, 1e-9

GROUPS = 4
GT = N // GROUPS
TQ = GT // P
GB = GT // S
EPG = E // GROUPS

ROW = D + E + 1
REGION = N + P
DUMP = E * REGION
NO_TOKEN = 1 << 20

W_PARTS = dict(q=KC * D, kv=KC * 2 * D, o=KC * D, c=KC * D, r=KC * (E + 1), gu=KC * 2 * IS, dn=IC * D)
W_AT, _n = {}, 0
for _name, _cols in W_PARTS.items():
    W_AT[_name] = _n
    _n += _cols
W_COLS = _n
W_PIECES = [(0, W_AT["o"]), (W_AT["o"], W_AT["gu"]), (W_AT["gu"], W_COLS)]
EG = KC * 2 * IM
EW = EG + KC * D

CF_PARTS = dict(ident=P, head_mask=P, head_pick=P // HD, attn_eps=1, decay_col=1, slot=1, token=TQ, ln_eps=1, iota=E,
                region=E, steps=E, upto=E * E, evens=P // 2)
CF_AT, _n = {}, 0
for _name, _cols in CF_PARTS.items():
    CF_AT[_name] = _n
    _n += _cols
CF_COLS = _n
R_CHAIN = 31

PER = dict(
    ld_xT=16, ld_x=16, ld_ctx=16, ctx_in=16 * 2 * NG, ld_v=16 * NG, ld_exp=16 * EPG, st_acc=16,
    scattered=16 * TQ * TOPK,
    xT_hi=1, xT_lo=1, ctx_hi=1, ctx_lo=1, v_hi=1, v_lo=1, x_bo=1,
    q_proj=KC, q_relu=KC, kv_proj=TQ, kv_read=2 * TQ, k_relu=TQ,
    kv_state=GB, kv_masked=2 * GB, attn_nd=GB, attn_den=TQ, attn_rec=TQ, attn_div=TQ, attn_T=TQ, attn_hi=TQ, attn_lo=TQ,
    wo_done=TQ, ln1_sum=TQ, ln1_stat=TQ, ln1_mv=TQ, ln1_std=TQ, ln1_rstd=TQ, x1_norm=TQ, x1_bc=TQ,
    x1T=TQ, x1T_hi=TQ, x1T_lo=TQ, s_done=GB, s_max=GB, m_T=GB, m_copied=GB, st_done=GB,
    exp_done=GB, e_hi=GB, e_lo=GB, pv_done=GB, pv_rec=GB, pv_norm=GB, aT=TQ, aT_hi=TQ, aT_lo=TQ,
    wc_done=TQ, ln2_sum=TQ, ln2_stat=TQ, ln2_mv=TQ, ln2_std=1, ln2_rstd=1, x2_norm=TQ,
    row_hi=TQ, row_lo=TQ, x2T=TQ, x2T_read=TQ, router=1, r_chain=R_CHAIN, r_exp=2, rank=1,
    g_done=IC, u_done=IC, silu=IC, h_mul=IC, h_hi=IC, h_lo=IC, down=TQ, acc_row=TQ,
    w_hi=EPG, w_lo=EPG,
)
SLOT_SEMS = ("xg_in", "xg_T", "xg_read", "meta", "e_gu", "e_silu", "e_mul", "e_hT", "e_hhi", "e_hlo",
             "e_y", "e_yw", "e_id", "e_add")
LAST_SEMS = ("f_in", "f_sum", "f_stat", "f_mv", "f_std", "f_rstd", "f_out", "f_st")
ONCE_SEMS = ("ld_const", "ld_w0", "ld_w1", "ld_w2", "ld_ind", "setup", "ws_hi", "ws_lo", "st_zero", "t_chain", "t_rows",
             "t_four", "t_tab", "st_pad", "waits_apart")
SETUP = 9

THREE = ((0, 0), (1, 0), (0, 1))


def chunk_rows(c):
    return min(P, IS - c * P)


def decoder_layer_program(nc, t, out):
    xs = nc.dram_tensor("xs_rows", [DUMP + P, ROW], F32, kind="Internal").ap()
    acc = [nc.dram_tensor(f"acc{p}", [N, D], F32, kind="Internal").ap() for p in range(2)]

    with ExitStack() as ctx:
        def sb(name, shape, dt=F32):
            return ctx.enter_context(nc.sbuf_tensor(name, shape, dt))

        def over(buffer, shape, dt=F32, at=0):
            cols = 1
            for n in shape[1:]:
                cols *= n
            cols = cols if dt != F16 else cols // 2
            view = buffer[0:shape[0], at:at + cols]
            if dt != F32:
                view = view.bitcast(dt)
            names = "abcde"[:len(shape) - 1]
            return view.rearrange(f"p ({' '.join(names)}) -> p {' '.join(names)}", **dict(zip(names, shape[1:])))

        w_stage = sb("w_stage", [P, W_COLS])
        w16 = sb("w16", [P, 2, W_COLS], F16)
        e_stage = sb("e_stage", [P, EW])
        e_w16 = sb("e_w16", [P, E, 2, EW], F16)
        cf = sb("cf", [P, CF_COLS])
        ch = sb("ch", [P, 3 * P], F16)
        bq_col = sb("bq_col", [P, KC])
        bias_rows = sb("bias_rows", [P, 4, D])
        bk_row, bv_row, bo_row, bc_row = (bias_rows[:, n, :] for n in range(4))

        def const(name):
            return cf[:, CF_AT[name]:CF_AT[name] + CF_PARTS[name]]

        ident, head_mask = const("ident"), const("head_mask")
        id16, tri16, ones16 = ch[:, 0:P], ch[:, P:2 * P], ch[:, 2 * P:3 * P]

        def weight(name, part, chunk, lo, n):
            width = {"q": D, "kv": 2 * D, "o": D, "c": D, "r": E + 1, "gu": 2 * IS, "dn": D}[name]
            a = W_AT[name] + chunk * width + lo
            return w16[:, part, a:a + n]

        xT = sb("xT", [P, KC, GT])
        x_in = sb("x_in", [P, TQ, D])
        c_stage = sb("c_stage", [C, GB, S])
        c_parts = sb("c_parts", [C, 2, GB, S], F16)
        c16 = sb("c16", [C + NG, 2, GB, NG * S], F16)
        v_stage = sb("v_stage", [P, GB, 2, VW])
        v16 = sb("v16", [P, 2, GB, 2, VW], F16)
        vb = sb("vb", [P, TQ, KC, P + 1])
        x1 = sb("x1", [P, TQ, D])
        x2 = sb("x2", [P, TQ, D])
        row = sb("row", [P, TQ, ROW])
        row16 = row[:, :, 0:D].bitcast(F16)
        queries_then_x2T = sb("queries_then_x2T", [P, KC * GT])
        qd = over(queries_then_x2T, [P, KC, GT])
        x2T16 = over(queries_then_x2T, [P, 2, KC, GT], F16)
        xT_then_x1T = sb("xT_then_x1T", [P, 2 * TQ * HPG * S])
        xT16 = over(xT_then_x1T, [P, 2, KC, GT], F16)
        xh = over(xT_then_x1T, [C + NG, 2, TQ, 2, HPG * S], F16)
        state_then_rows = sb("state_then_rows", [P, 4 * D])
        kv_m = over(state_then_rows, [P, 2, KC, AW])
        aT16 = over(state_then_rows, [P, 2, 2, 2, P], F16)
        onehot = over(state_then_rows, [P, TQ, TOPK, E], at=2 * D)
        pos_sel = over(state_then_rows, [P, TQ, TOPK, E], at=3 * D)
        kb = over(w_stage, [P, TQ, D])
        e32 = over(w_stage, [P, 2, 2, HPG * S])
        gate = over(w_stage, [P, 2, GT])
        h32 = over(w_stage, [P, 2, GT], at=2 * GT)
        a2 = over(w_stage, [P, GB, P], at=4 * GT)
        after = 4 * GT + GB * P
        h16 = over(w_stage, [P, 2, IC, GT], F16, at=after)
        a32 = over(w_stage, [P, 2, D], at=after)
        a16 = over(w_stage, [P, 2, 2, KC, P], F16, at=after + 2 * D)
        e16 = over(w_stage, [P, 2, 2, 2, HPG * S], F16, at=after + 4 * D)
        den = sb("den", [P, 2, KC, P // HD])
        m16 = sb("m16", [P, 2, 2 * NG], F16)
        stat1 = sb("stat1", [P, TQ, 6])
        mv1 = sb("mv1", [P, TQ, 2])
        rstd1 = sb("rstd1", [P, TQ])
        std1 = sb("std1", [P, TQ])
        rec = sb("rec", [P, 2, 2 * NG])
        stat2 = sb("stat2", [P, TQ, 6])
        mv2 = sb("mv2", [P, TQ, 2])
        rstd2 = sb("rstd2", [P, TQ])
        std2 = sb("std2", [P, TQ])
        lg = sb("lg", [P, TQ, E + 1])
        lg_max = sb("lg_max", [P, TQ])
        shifted = sb("shifted", [P, TQ, E])
        ex = sb("ex", [P, TQ, E])
        sg_e = sb("sg_e", [P, TQ])
        sg_d = sb("sg_d", [P, TQ])
        sg = sb("sg", [P, TQ])
        ex_sum = sb("ex_sum", [P, TQ])
        ex_rec = sb("ex_rec", [P, TQ])
        prob = sb("prob", [P, TQ, E])
        top_v = sb("top_v", [P, TQ, 8])
        top_i = sb("top_i", [P, TQ, 8], U32)
        top_f = sb("top_f", [P, TQ, TOPK])
        mask16 = sb("mask16", [P, TQ + 1, E], F16)
        chosen = sb("chosen", [P, TQ, E])
        w_sum = sb("w_sum", [P, TQ])
        w_clip = sb("w_clip", [P, TQ])
        w_rec = sb("w_rec", [P, TQ])
        count = sb("count", [P, E])
        pos = sb("pos", [P, TQ, E])
        pos_f = sb("pos_f", [P, TQ * TOPK])
        pos_u = sb("pos_u", [P, TQ * TOPK], U32)
        token = sb("token", [P, TQ])
        zeros = sb("zeros", [P, D])
        pad_row = sb("pad_row", [P, ROW])
        more = over(queries_then_x2T, [P, E, E])
        tiles = sb("tiles", [P, E])
        tiles_to = over(queries_then_x2T, [P, E, E], at=E * E)
        cum = sb("cum", [P, E])
        evens_below = over(queries_then_x2T, [P, P // 2], at=2 * E * E)
        passed = sb("passed", [P, E])
        passed_t = sb("passed_t", [P, E])
        slot_f = sb("slot_f", [P, 8])
        TAB_ROW, TAB_PAD, TAB_LAPS, TAB_FOUR = P, 2 * P, 2 * P + E, 2 * P + E + 1
        tab = sb("tab", [1, TAB_FOUR + P // 2], I32)
        four = sb("four", [1, P])
        xg = over(xT[:, :, :].rearrange("p k n -> p (k n)"), [P, 2, ROW])
        xg16 = xg[:, :, 0:D].bitcast(F16)
        xgT = over(xT_then_x1T, [P, 2, 2 * KC, P], F16)
        ehT = over(xT_then_x1T, [P, 2, 2, KC, P], F16, at=2 * D)
        eh = over(queries_then_x2T, [P, 2, KC * P])
        ye = over(queries_then_x2T, [P, 2, D], at=2 * D)
        e_gate = over(w_stage, [P, 2, IM])
        meta = sb("meta", [P, 2, E + 1])
        ids = sb("ids", [P, 2], U32)
        fa = over(w_stage, [P, 2, 2, TQ, D], at=2 * IM)
        fsum = [x1, x2]
        fstat = sb("fstat", [P, 2, TQ, 6])
        fmv = sb("fmv", [P, 2, TQ, 2])
        fstd = sb("fstd", [P, 2, TQ])
        frstd = sb("frstd", [P, 2, TQ])

        bank = [ctx.enter_context(nc.psum_tensor(f"bank{k}", [P, 512], F32)) for k in range(8)]
        bP, bK, bN, bW, bT, bE = bank[0:2], bank[2:4], bank[4], bank[5], bank[6], bank[7]

        def half(b):
            return b[:, :].bitcast(F16)

        sems = {k: ctx.enter_context(nc.semaphore("s_" + k)) for k in (*PER, *ONCE_SEMS)}
        slot_sem = {k: [ctx.enter_context(nc.semaphore(f"s_{k}{p}")) for p in range(2)]
                    for k in (*SLOT_SEMS, *LAST_SEMS)}

        def need(eng, name, i, n=None):
            eng.wait_ge(sems[name], i * PER[name] + (PER[name] if n is None else n))

        def apart(eng, sem, value):
            eng.wait_ge(sem, value)
            eng.sem_inc(sems["waits_apart"], 1)

        def bc(ap, shape):
            return ap.broadcast_to(list(shape))

        def four_experts(eng, j):
            four_at = eng.value_load(tab[0:1, bass.ds(j + TAB_FOUR, 1)], min_val=0, max_val=E ** 4 - 1)
            return [(four_at // E ** n) % E for n in range(4)]

        block = ctx.enter_context(nc.Block())

        @block.sync
        def _(sp):
            def load_group(i, later):
                if later:
                    need(sp, "xT_hi", i, 0)
                    need(sp, "xT_lo", i, 0)
                sp.dma_start(xT[:, :, :], t["xT"][:, :, bass.ts(i, GT)].rearrange("k p n -> p k n")
                             ).then_inc(sems["ld_xT"], 16)
                if later:
                    apart(sp, sems["ctx_hi"], i * PER["ctx_hi"])
                    apart(sp, sems["ctx_lo"], i * PER["ctx_lo"])
                sp.dma_start(c_stage[:, :, :], t["ctxT"][:, bass.ts(i, GB), :]).then_inc(sems["ld_ctx"], 16)
                if later:
                    need(sp, "v_hi", i, 0)
                    need(sp, "v_lo", i, 0)
                for g in range(NG):
                    r, w = (g % 2) * S, (g % 2) * (HD + 1)
                    sp.dma_start(v_stage[r:r + S, :, g // 2, w:w + HD],
                                 t["ctx"][bass.ts(i, GB), :, g * HD:(g + 1) * HD].rearrange("b t d -> t b d")
                                 ).then_inc(sems["ld_v"], 16)
                if later:
                    need(sp, "ln2_sum", i, 0)
                sp.dma_start(x_in[:, :, :], t["x"][bass.ts(i, GT), :].rearrange("(q p) d -> p q d", p=P)
                             ).then_inc(sems["ld_x"], 16)

            def place_context(i):
                apart(sp, sems["ctx_hi"], (i + 1) * PER["ctx_hi"])
                apart(sp, sems["ctx_lo"], (i + 1) * PER["ctx_lo"])
                need(sp, "st_done", i, 0)
                for part in range(2):
                    for g in range(NG):
                        sp.dma_start(c16[g * HD:(g + 1) * HD, part, :, g * S:(g + 1) * S],
                                     c_parts[g * HD:(g + 1) * HD, part, :, :]).then_inc(sems["ctx_in"], 16)

            def load_experts(i, ns):
                for n in ns:
                    need(sp, "w_hi", i, n)
                    need(sp, "w_lo", i, n)
                    sp.dma_start(e_stage[:, :], t["e_w"][bass.ds(i * EPG + n, 1)].rearrange("a p c -> p (a c)")
                                 ).then_inc(sems["ld_exp"], 16)

            def store_group(i):
                need(sp, "acc_row", i)
                sp.dma_start(acc[0][bass.ts(i, GT), :].rearrange("(q p) d -> p q d", p=P), x2[:, :, :]
                             ).then_inc(sems["st_acc"], 16)

            sp.dma_start(cf[:, :], t["cf"]).then_inc(sems["ld_const"], 16)
            sp.dma_start(ch[:, :], t["ch"]).then_inc(sems["ld_const"], 16)
            sp.dma_start(bq_col[:, :], t["bq"]).then_inc(sems["ld_const"], 16)
            sp.dma_start(bias_rows[:, :, :].rearrange("p n d -> p (n d)"), t["biases"].partition_broadcast(P)
                         ).then_inc(sems["ld_const"], 16)
            def load_weights(n):
                a, b = W_PIECES[n]
                sp.dma_start(w_stage[:, a:b], t["w"][:, a:b]).then_inc(sems[f"ld_w{n}"], 16)

            load_weights(0)
            sp.wait_ge(sems["setup"], SETUP)
            load_group(0, False)
            for n in range(1, len(W_PIECES)):
                load_weights(n)
            sp.dma_start(c16[C:C + NG, 0, :, :], t["pick"]).then_inc(sems["ld_ind"], 16)
            sp.dma_start(acc[1].rearrange("(n p) d -> p n d", p=P),
                         bc(zeros[:, :].unsqueeze(1), [P, N // P, D])).then_inc(sems["st_zero"], 16)
            with sp.Fori(0, GROUPS - 1) as i:
                place_context(i)
                load_experts(i, range(EPG - 1))
                load_group(i + 1, True)
                load_experts(i, [EPG - 1])
                store_group(i)
            place_context(GROUPS - 1)
            load_experts(GROUPS - 1, range(EPG))
            store_group(GROUPS - 1)

            sp.wait_ge(sems["t_tab"], 1)
            sp.dma_start(xs[DUMP:DUMP + P, :], pad_row[:, :]).then_inc(sems["st_pad"], 16)
            for e in range(E):
                after = sp.value_load(tab[0:1, TAB_PAD + e:TAB_PAD + e + 1], min_val=0, max_val=DUMP - P)
                sp.dma_start(xs[bass.ds(after, P), :], pad_row[:, :]).then_inc(sems["st_pad"], 16)
            sp.wait_ge(sems["st_pad"], 16 * (E + 1))
            need(sp, "scattered", GROUPS - 1)
            laps = sp.value_load(tab[0:1, TAB_LAPS:TAB_LAPS + 1], min_val=0, max_val=P // 2 - 1)
            with sp.Fori(0, laps + 1) as j:
                for p in range(2):
                    first = sp.value_load(tab[0:1, bass.ds(TAB_ROW + 2 * j + p, 1)], min_val=0, max_val=DUMP)
                    sp.wait_ge(slot_sem["xg_T"][p], j)
                    sp.wait_ge(slot_sem["meta"][p], j)
                    sp.dma_start(xg[:, p, :], xs[bass.ds(first, P), :]).then_inc(slot_sem["xg_in"][p], 16)
            for p in range(2):
                apart(sp, slot_sem["e_add"][p], laps * 16 + 16)
            with sp.Fori(0, GROUPS // 2) as j:
                for p in range(2):
                    sp.wait_ge(slot_sem["f_sum"][p], j)
                    for a in range(2):
                        sp.dma_start(fa[:, p, a, :, :], acc[a][bass.ds((j * 2 + p) * GT, GT), :].rearrange(
                            "(q p) d -> p q d", p=P)).then_inc(slot_sem["f_in"][p], 16)
            for p in range(2):
                sp.wait_ge(slot_sem["f_st"][p], 16 * (GROUPS // 2))

        @block.tensor
        def _(pe):
            def three(out, lhs, rhs, chunks):
                steps = [(w, d, k) for k in range(chunks) for w, d in THREE]
                for n, (w, d, k) in enumerate(steps):
                    last = pe.matmul(out, lhs(w, d, k), rhs(w, d, k), start=n == 0, stop=n == len(steps) - 1)
                return last

            def q_projection(i):
                need(pe, "xT_hi", i)
                need(pe, "xT_lo", i)
                for c in range(KC):
                    if c == 0:
                        need(pe, "r_chain", i, 0)
                    else:
                        need(pe, "h_mul", i, 0)
                    three(bP[c][:, :], lambda w, d, k: weight("q", w, k, c * P, P),
                          lambda w, d, k: xT16[:, d, k, :], KC).then_inc(sems["q_proj"], 1)

            def kv_projection(i, q):
                if q < 2:
                    need(pe, "q_relu", i, q + 1)
                else:
                    need(pe, "kv_read", i, 2 * (q - 1))
                three(bP[q % 2][:, :], lambda w, d, k: xT16[:, d, k, q * P:(q + 1) * P],
                      lambda w, d, k: weight("kv", w, k, 0, 2 * D), KC).then_inc(sems["kv_proj"], 1)

            def kv_state(i, b):
                q, r = b // 2, (b % 2) * S
                need(pe, "k_relu", i, q + 1)
                need(pe, "kv_read", i, 2 * (q + 1))
                if b < 2:
                    need(pe, "h_mul", i, 0)
                else:
                    need(pe, "kv_masked", i, 2 * (b - 1))
                for c in range(KC):
                    last = pe.matmul(bK[b % 2][:, c * (P + 1):(c + 1) * (P + 1)], kb[r:r + S, q, c * P:(c + 1) * P],
                                     vb[r:r + S, q, c, :], start=True, stop=True)
                last.then_inc(sems["kv_state"], 1)

            def attention(i, b):
                q, r = b // 2, (b % 2) * S
                need(pe, "kv_masked", i, 2 * (b + 1))
                if b == 0:
                    need(pe, "q_relu", i)
                    need(pe, "h_mul", i, 0)
                    need(pe, "r_chain", i, 0)
                if b % 2 == 0 and b >= 4:
                    need(pe, "attn_div", i, q - 1)
                for c in range(KC):
                    last = pe.matmul((bN, bE)[q % 2][r:r + S, c * AW:(c + 1) * AW], qd[:, c, b * S:(b + 1) * S],
                                     kv_m[:, b % 2, c, :], start=True, stop=True)
                last.then_inc(sems["attn_nd"], 1)

            def attention_transposes(i, q):
                need(pe, "attn_div", i, q + 1)
                if q == 0:
                    need(pe, "kv_read", i)
                if q >= 2:
                    need(pe, "attn_lo", i, q - 1)
                for c in range(KC):
                    last = pe.transpose(bP[q % 2][:, c * P:(c + 1) * P], a32[:, q % 2, c * P:(c + 1) * P], ident)
                last.then_inc(sems["attn_T"], 1)

            def attention_out(i, q):
                need(pe, "attn_hi", i, q + 1)
                need(pe, "attn_lo", i, q + 1)
                if q == 0:
                    need(pe, "acc_row", i, 0)
                else:
                    need(pe, "ln1_sum", i, q)
                three(bW[:, 0:D], lambda w, d, k: a16[:, q % 2, d, k, :],
                      lambda w, d, k: weight("o", w, k, 0, D), KC).then_inc(sems["wo_done"], 1)

            def x1_transposes(i, q):
                if q == 0:
                    need(pe, "acc_row", i, 0)
                else:
                    need(pe, "x1T_lo", i, q)
                apart(pe, sems["x1_norm"], i * PER["x1_norm"] + q + 1)
                for h in range(HPG):
                    last = pe.transpose(bT[0:C, h * P:(h + 1) * P], x1[:, q, h * C:(h + 1) * C], ident)
                last.then_inc(sems["x1T"], 1)

            def scores(i, b):
                q = b // 2
                need(pe, "x1T_hi", i, q + 1)
                if b == 0:
                    need(pe, "ctx_in", i)
                if b < 2:
                    need(pe, "kv_masked", i)
                else:
                    need(pe, "s_max", i, b - 1)
                for hp in range(2):
                    last = pe.matmul(bK[b % 2][:, hp * NG * S:(hp + 1) * NG * S],
                                     xh[0:C, 0, q, b % 2, hp * P:(hp + 1) * P], c16[0:C, 0, b, :],
                                     start=True, stop=True)
                last.then_inc(sems["s_done"], 1)

            def max_transposes(i, b):
                need(pe, "s_max", i, b + 1)
                if b == 0:
                    need(pe, "attn_lo", i)
                else:
                    need(pe, "m_copied", i, b)
                for hp in range(2):
                    last = pe.transpose(half(bP[0])[0:NG, hp * P:(hp + 1) * P], m16[:, b % 2, hp * NG:(hp + 1) * NG], id16)
                last.then_inc(sems["m_T"], 1)

            def scores_T(i, b):
                q = b // 2
                need(pe, "m_copied", i, b + 1)
                need(pe, "x1T_lo", i, q + 1)
                if b == 0:
                    pe.wait_ge(sems["ld_ind"], 16)
                    need(pe, "attn_div", i)
                else:
                    need(pe, "exp_done", i, b)
                for gp in range(2):
                    last = three(bE[:, gp * HPG * S:(gp + 1) * HPG * S],
                                 lambda w, d, k: c16[0:C if w or d else C + NG, w, b, gp * P:(gp + 1) * P],
                                 lambda w, d, k: xh[0:C if w or d else C + NG, d, q, b % 2, :], 1)
                last.then_inc(sems["st_done"], 1)

            def values(i, b):
                need(pe, "e_hi", i, b + 1)
                need(pe, "e_lo", i, b + 1)
                if b == 0:
                    need(pe, "v_hi", i)
                    need(pe, "v_lo", i)
                    need(pe, "attn_div", i)
                    need(pe, "attn_lo", i)
                if b >= 2:
                    need(pe, "pv_norm", i, b - 1)
                for hp in range(2):
                    for gp in range(2):
                        a = (hp * 2 + gp) * VW
                        last = three((bN, bP[1])[b % 2][:, a:a + VW],
                                     lambda w, d, k: e16[:, b % 2, d, gp, hp * P:(hp + 1) * P],
                                     lambda w, d, k: v16[:, w, b, gp, :], 1)
                last.then_inc(sems["pv_done"], 1)

            def a_transposes(i, q):
                need(pe, "pv_norm", i, 2 * (q + 1))
                if q == 0:
                    need(pe, "x1T_lo", i)
                else:
                    need(pe, "aT_lo", i, q)
                for b in range(2):
                    last = pe.transpose(bT[:, b * P:(b + 1) * P], a2[:, 2 * q + b, :], ident)
                last.then_inc(sems["aT"], 1)

            def cross_out(i, q):
                need(pe, "aT_hi", i, q + 1)
                need(pe, "aT_lo", i, q + 1)
                if q == 0:
                    need(pe, "ln1_sum", i)
                else:
                    need(pe, "ln2_sum", i, q)
                three(bW[:, 0:D], lambda w, d, k: aT16[:, q % 2, d, k, :],
                      lambda w, d, k: weight("c", w, k, 0, D), KC).then_inc(sems["wc_done"], 1)

            def x2_transposes(i, q):
                need(pe, "row_hi", i, q + 1)
                need(pe, "row_lo", i, q + 1)
                if q < 2:
                    need(pe, "aT_lo", i)
                    need(pe, "ln2_sum", i)
                else:
                    need(pe, "x2T_read", i, q - 1)
                for a in range(2 * KC):
                    last = pe.transpose(half((bT, bW)[q % 2])[:, a * P:(a + 1) * P], row16[:, q, a * P:(a + 1) * P], id16)
                last.then_inc(sems["x2T"], 1)

            def router(i):
                need(pe, "m_copied", i)
                need(pe, "x2T_read", i)
                for q in range(TQ):
                    last = three(bP[0][:, q * (E + 1):(q + 1) * (E + 1)],
                                 lambda w, d, k: x2T16[:, d, k, q * P:(q + 1) * P],
                                 lambda w, d, k: weight("r", w, k, 0, E + 1), KC)
                last.then_inc(sems["router"], 1)

            def ranks(i):
                need(pe, "r_chain", i, R_MASK)
                need(pe, "exp_done", i)
                flat = mask16[:, :, :].rearrange("p q e -> p (q e)")
                pe.matmul(bE[:, 0:(TQ + 1) * E], tri16, flat, start=True, stop=False, skip_group_check=True)
                for q in range(TQ):
                    last = pe.matmul(bE[:, (q + 1) * E:(TQ + 1) * E].rearrange("p (q e) -> p q e", e=E), ones16,
                                     bc(mask16[:, q:q + 1, :], [P, TQ - q, E]), start=False, stop=q == TQ - 1,
                                     skip_group_check=True)
                last.then_inc(sems["rank"], 1)

            def shared_up(i, c):
                n, (bg, bu) = chunk_rows(c), ((bK[0], bK[1]), (bP[1], bN))[c % 2]
                if c < 2:
                    need(pe, "s_max", i)
                    need(pe, "pv_norm", i)
                else:
                    need(pe, "h_mul", i, c - 1)
                for half_, b_, name in ((0, bg, "g_done"), (1, bu, "u_done")):
                    three(b_[0:n, :], lambda w, d, k: weight("gu", w, k, half_ * IS + c * P, n),
                          lambda w, d, k: x2T16[:, d, k, :], KC).then_inc(sems[name], 1)

            def shared_down(i, q):
                if q == 0:
                    need(pe, "h_hi", i)
                    need(pe, "h_lo", i)
                    need(pe, "ln2_sum", i)
                    need(pe, "x2T_read", i)
                if q >= 2:
                    need(pe, "acc_row", i, q - 1)
                steps = [(w, d, c) for c in range(IC) for w, d in THREE]
                for n, (w, d, c) in enumerate(steps):
                    r = chunk_rows(c)
                    last = pe.matmul((bW, bT)[q % 2][:, 0:D], h16[0:r, d, c, q * P:(q + 1) * P],
                                     weight("dn", w, c, 0, D)[0:r], start=n == 0, stop=n == len(steps) - 1)
                last.then_inc(sems["down"], 1)

            pe.wait_ge(sems["ld_const"], 64)
            pe.wait_ge(sems["ws_hi"], len(W_PIECES))
            pe.wait_ge(sems["ws_lo"], len(W_PIECES))
            pe.wait_ge(sems["setup"], SETUP)
            with pe.Fori(0, GROUPS) as i:
                q_projection(i)
                for q in range(TQ):
                    kv_projection(i, q)
                for b in range(GB + 3):
                    if b < GB:
                        kv_state(i, b)
                    if 1 <= b <= GB:
                        attention(i, b - 1)
                    if b >= 3 and b % 2:
                        attention_transposes(i, (b - 3) // 2)
                    if b >= 4 and b % 2 == 0:
                        attention_out(i, b // 2 - 2)
                x1_transposes(i, 0)
                for step in range(GB + 6):
                    if step % 2 == 0 and step // 2 + 1 < TQ:
                        x1_transposes(i, step // 2 + 1)
                    if step < GB:
                        scores(i, step)
                    if 1 <= step <= GB:
                        max_transposes(i, step - 1)
                    if 2 <= step < GB + 2:
                        scores_T(i, step - 2)
                    if 3 <= step < GB + 3:
                        values(i, step - 3)
                    if step >= 5 and step % 2 and step < GB + 5:
                        a_transposes(i, (step - 5) // 2)
                    if step >= 6 and step % 2 == 0 and step < GB + 6:
                        cross_out(i, (step - 6) // 2)
                for q in range(TQ):
                    x2_transposes(i, q)
                router(i)
                for c in range(IC):
                    shared_up(i, c)
                    if c == 2:
                        ranks(i)
                for q in range(TQ):
                    shared_down(i, q)

            pe.wait_ge(sems["t_chain"], T_CHAIN)
            for n in range(2):
                last = pe.transpose(bP[0][0:1, n * P:(n + 1) * P], slot_f[:, n:n + 1], ident)
            last.then_inc(sems["t_rows"], 1)

            def slot_transposes(j, p):
                pe.wait_ge(slot_sem["xg_in"][p], 16 * (j + 1))
                pe.wait_ge(slot_sem["xg_read"][p], j)
                for a in range(2 * KC):
                    last = pe.transpose(half((bT, bE)[p])[:, a * P:(a + 1) * P], xg16[:, p, a * P:(a + 1) * P], id16)
                last.then_inc(slot_sem["xg_T"][p], 1)

            def slot_up(j, p, e):
                pe.wait_ge(slot_sem["xg_read"][p], j + 1)
                pe.wait_ge(slot_sem["e_mul"][p], j)
                three(bP[p][:, 0:2 * IM], lambda w, d, k: xgT[:, p, d * KC + k, :],
                      lambda w, d, k: e_w16[:, bass.ds(e, 1), w, k * 2 * IM:(k + 1) * 2 * IM].rearrange("p a n -> p (a n)"),
                      KC).then_inc(slot_sem["e_gu"][p], 1)

            def slot_h_transposes(j, p):
                pe.wait_ge(slot_sem["e_mul"][p], j + 1)
                pe.wait_ge(slot_sem["e_hlo"][p], j)
                for k in range(KC):
                    last = pe.transpose(bK[p][:, k * P:(k + 1) * P], eh[:, p, k * P:(k + 1) * P], ident)
                last.then_inc(slot_sem["e_hT"][p], 1)

            def slot_down(j, p, e):
                pe.wait_ge(slot_sem["e_hhi"][p], j + 1)
                pe.wait_ge(slot_sem["e_hlo"][p], j + 1)
                pe.wait_ge(slot_sem["e_yw"][p], j)
                three((bN, bW)[p][:, 0:D], lambda w, d, k: ehT[:, p, d, k, :],
                      lambda w, d, k: e_w16[:, bass.ds(e, 1), w, EG + k * D:EG + (k + 1) * D].rearrange("p a n -> p (a n)"),
                      KC).then_inc(slot_sem["e_y"][p], 1)

            pe.wait_ge(sems["t_tab"], 1)
            need(pe, "acc_row", GROUPS - 1)
            need(pe, "w_hi", GROUPS - 1)
            need(pe, "w_lo", GROUPS - 1)
            laps = pe.value_load(tab[0:1, TAB_LAPS:TAB_LAPS + 1], min_val=0, max_val=P // 2 - 1)
            e = [pe.value_load(tab[0:1, p:p + 1], min_val=0, max_val=E - 1) for p in range(2)]
            slot_transposes(0, 0)
            slot_up(0, 0, e[0])
            slot_transposes(0, 1)
            slot_h_transposes(0, 0)
            slot_up(0, 1, e[1])
            with pe.Fori(0, laps) as j:
                e = four_experts(pe, j + 1)
                slot_transposes(j + 1, 0)
                slot_down(j, 0, e[0])
                slot_h_transposes(j, 1)
                slot_up(j + 1, 0, e[2])
                slot_transposes(j + 1, 1)
                slot_down(j, 1, e[1])
                slot_h_transposes(j + 1, 0)
                slot_up(j + 1, 1, e[3])
            e = [pe.value_load(tab[0:1, bass.ds(2 * laps + p, 1)], min_val=0, max_val=E - 1) for p in range(2)]
            slot_down(laps, 0, e[0])
            slot_h_transposes(laps, 1)
            slot_down(laps, 1, e[1])

        @block.scalar
        def _(act):
            def split_expert(i, n):
                act.wait_ge(sems["ld_exp"], i * PER["ld_exp"] + 16 * (n + 1))
                act.activation(e_w16[:, bass.ds(i * EPG + n, 1), 0, :].rearrange("p a c -> p (a c)"),
                               e_stage[:, :], ACT.Copy, scale=W_SCALE).then_inc(sems["w_hi"], 1)

            act.wait_ge(sems["ld_const"], 64)
            for n, (a, b) in enumerate(W_PIECES):
                act.wait_ge(sems[f"ld_w{n}"], 16)
                act.activation(w16[:, 0, a:b], w_stage[:, a:b], ACT.Copy, scale=W_SCALE).then_inc(sems["ws_hi"], 1)
            with act.Fori(0, GROUPS) as i:
                need(act, "ld_xT", i)
                need(act, "kv_proj", i, 0)
                act.activation(xT16[:, 0, :, :], xT[:, :, :], ACT.Copy).then_inc(sems["xT_hi"], 1)
                for c in range(KC):
                    need(act, "q_proj", i, c + 1)
                    if c == 0:
                        need(act, "attn_nd", i, 0)
                    act.activation(qd[:, c, :], bP[c][:, :], ACT.Relu, bias=bq_col[:, c:c + 1], scale=W_BACK
                                   ).then_inc(sems["q_relu"], 1)
                need(act, "ld_ctx", i)
                need(act, "ctx_in", i, 0)
                act.activation(c_parts[:, 0, :, :], c_stage[:, :, :], ACT.Copy).then_inc(sems["ctx_hi"], 1)
                need(act, "ld_v", i)
                need(act, "pv_done", i, 0)
                act.activation(v16[:, 0, :, :, :], v_stage[:, :, :, :], ACT.Copy).then_inc(sems["v_hi"], 1)
                for q in range(TQ):
                    need(act, "kv_read", i, 2 * q + 1)
                    act.activation(kb[:, q, :], kb[:, q, :], ACT.Relu, scale=const("decay_col")
                                   ).then_inc(sems["k_relu"], 1)
                for step in range(TQ + 1):
                    if step < TQ:
                        q = step
                        need(act, "attn_T", i, q + 1)
                        need(act, "wo_done", i, max(q - 1, 0))
                        act.activation(a16[:, q % 2, 0, :, :], bP[q % 2][:, 0:D].rearrange("p (c n) -> p c n", c=KC),
                                       ACT.Copy).then_inc(sems["attn_hi"], 1)
                    if step >= 1:
                        q = step - 1
                        need(act, "ln1_mv", i, q + 1)
                        act.activation(std1[:, q:q + 1], mv1[:, q, 1:2], ACT.Sqrt, bias=const("ln_eps")
                                       ).then_inc(sems["ln1_std"], 1)
                split_expert(i, 0)

                def x1T_hi(q):
                    need(act, "x1T", i, q + 1)
                    if q == 0:
                        need(act, "st_done", i, 0)
                    act.activation(xh[0:C, 0, q, :, :].rearrange("p b (h s) -> p h b s", h=HPG),
                                   bT[0:C, :].rearrange("p (h b s) -> p h b s", h=HPG, b=2), ACT.Copy
                                   ).then_inc(sems["x1T_hi"], 1)

                x1T_hi(0)
                for step in range(GB + 6):
                    if step % 2 == 0 and step // 2 + 1 < TQ:
                        x1T_hi(step // 2 + 1)
                    if 1 <= step <= GB:
                        b = step - 1
                        need(act, "m_T", i, b + 1)
                        act.activation(xh[C:C + NG, 0, b // 2, b % 2, :], half(bP[0])[0:NG, 0:HPG * S], ACT.Copy,
                                       scale=-1.0).then_inc(sems["m_copied"], 1)
                    if 2 <= step < GB + 2:
                        b = step - 2
                        need(act, "st_done", i, b + 1)
                        if b >= 2:
                            need(act, "e_lo", i, b - 1)
                        act.activation(e32[:, b % 2, :, :], bE[:, :].rearrange("p (g n) -> p g n", g=2), ACT.Exp,
                                       scale=HD ** -0.5).then_inc(sems["exp_done"], 1)
                        need(act, "exp_done", i, b + 1)
                        if b >= 2:
                            need(act, "pv_done", i, b - 1)
                        act.activation(e16[:, b % 2, 0, :, :], e32[:, b % 2, :, :], ACT.Copy).then_inc(sems["e_hi"], 1)
                    if step >= 5 and step % 2 and step < GB + 5:
                        q = (step - 5) // 2
                        need(act, "aT", i, q + 1)
                        need(act, "wc_done", i, max(q - 1, 0))
                        act.activation(aT16[:, q % 2, 0, :, :].rearrange("p e (b s) -> p b e s", b=2),
                                       bT[:, 0:D].rearrange("p (b e s) -> p b e s", b=2, e=2), ACT.Copy
                                       ).then_inc(sems["aT_hi"], 1)
                need(act, "ln2_mv", i)
                act.activation(std2[:, :], mv2[:, :, 1], ACT.Sqrt, bias=const("ln_eps")).then_inc(sems["ln2_std"], 1)
                for q in range(TQ):
                    need(act, "x2_norm", i, q + 1)
                    if q == 0:
                        need(act, "scattered", i, 0)
                        need(act, "x2T", i, 0)
                    act.activation(row16[:, q, 0:D], x2[:, q, :], ACT.Copy).then_inc(sems["row_hi"], 1)
                split_expert(i, 1)
                need(act, "r_chain", i, R_SHIFT)
                act.activation(ex[:, :, :], shifted[:, :, :], ACT.Exp).then_inc(sems["r_exp"], 1)
                act.activation(sg_e[:, :], lg[:, :, E], ACT.Exp, scale=-1.0).then_inc(sems["r_exp"], 1)
                for c in range(IC + 1):
                    if c < IC:
                        n = chunk_rows(c)
                        need(act, "g_done", i, c + 1)
                        if c == 0:
                            need(act, "e_hi", i)
                            need(act, "e_lo", i)
                        if c >= 2:
                            need(act, "h_mul", i, c - 1)
                        act.activation(gate[0:n, c % 2, :], (bK[0], bP[1])[c % 2][0:n, :], ACT.Silu, scale=W_BACK
                                       ).then_inc(sems["silu"], 1)
                    if c >= 1:
                        n = chunk_rows(c - 1)
                        need(act, "h_mul", i, c)
                        if c == 1:
                            need(act, "down", i, 0)
                        act.activation(h16[0:n, 0, c - 1, :], h32[0:n, (c - 1) % 2, :], ACT.Copy
                                       ).then_inc(sems["h_hi"], 1)
                    if c == 2:
                        split_expert(i, 2)
                split_expert(i, 3)

            def slot_silu(j, p):
                act.wait_ge(slot_sem["e_gu"][p], j + 1)
                act.wait_ge(slot_sem["e_mul"][p], j)
                act.activation(e_gate[:, p, :], bP[p][:, 0:IM], ACT.Silu, scale=W_BACK).then_inc(slot_sem["e_silu"][p], 1)

            def slot_h_hi(j, p):
                act.wait_ge(slot_sem["e_hT"][p], j + 1)
                act.wait_ge(slot_sem["e_y"][p], j)
                act.activation(ehT[:, p, 0, :, :], bK[p][:, 0:KC * P].rearrange("p (k n) -> p k n", k=KC), ACT.Copy
                               ).then_inc(slot_sem["e_hhi"][p], 1)

            def slot_weighted(j, p, e):
                act.wait_ge(slot_sem["e_y"][p], j + 1)
                act.wait_ge(slot_sem["meta"][p], j + 1)
                act.wait_ge(slot_sem["e_add"][p], 16 * j)
                act.activation(ye[:, p, :], (bN, bW)[p][:, 0:D], ACT.Copy, scale=meta[:, p, bass.ds(e, 1)]
                               ).then_inc(slot_sem["e_yw"][p], 1)

            act.wait_ge(sems["t_tab"], 1)
            laps = act.value_load(tab[0:1, TAB_LAPS:TAB_LAPS + 1], min_val=0, max_val=P // 2 - 1)
            slot_silu(0, 0)
            slot_h_hi(0, 0)
            slot_silu(0, 1)
            with act.Fori(0, laps) as j:
                e = four_experts(act, j + 1)
                slot_weighted(j, 0, e[0])
                slot_h_hi(j, 1)
                slot_silu(j + 1, 0)
                slot_weighted(j, 1, e[1])
                slot_h_hi(j + 1, 0)
                slot_silu(j + 1, 1)
            e = [act.value_load(tab[0:1, bass.ds(2 * laps + p, 1)], min_val=0, max_val=E - 1) for p in range(2)]
            slot_weighted(laps, 0, e[0])
            slot_h_hi(laps, 1)
            slot_weighted(laps, 1, e[1])
            with act.Fori(0, GROUPS // 2) as j:
                for p in range(2):
                    act.wait_ge(slot_sem["f_mv"][p], TQ * (j + 1))
                    act.activation(fstd[:, p, :], fmv[:, p, :, 1], ACT.Sqrt, bias=const("ln_eps")
                                   ).then_inc(slot_sem["f_std"][p], 1)
                for p in range(2):
                    act.wait_ge(slot_sem["f_out"][p], TQ * (j + 1))
                    act.dma_start(out[bass.ds((j * 2 + p) * GT, GT), :].rearrange("(q p) d -> p q d", p=P),
                                  fsum[p][:, :, :]).then_inc(slot_sem["f_st"][p], 16)

        @block.vector
        def _(dve):
            dve.memset(vb[:, :, :, P:P + 1], 1.0).then_inc(sems["setup"], 1)
            dve.memset(mask16[:, TQ, :], 0.0).then_inc(sems["setup"], 1)
            dve.wait_ge(sems["ld_const"], 64)
            dve.tensor_copy(token[:, :], const("token")).then_inc(sems["setup"], 1)
            dve.tensor_copy(count[:, :], const("region")).then_inc(sems["setup"], 1)
            dve.wait_ge(sems["setup"], SETUP)
            for n, (a, b) in enumerate(W_PIECES):
                dve.wait_ge(sems["ws_hi"], n + 1)
                dve.scalar_tensor_tensor(w16[:, 1, a:b], w_stage[:, a:b], W_SCALE, w16[:, 0, a:b], ALU.mult,
                                         ALU.subtract).then_inc(sems["ws_lo"], 1)

            def split_expert(i, n):
                need(dve, "w_hi", i, n + 1)
                w = e_w16[:, bass.ds(i * EPG + n, 1), :, :].rearrange("p a s c -> p (a s) c")
                dve.scalar_tensor_tensor(w[:, 1, :], e_stage[:, :], W_SCALE, w[:, 0, :], ALU.mult,
                                         ALU.subtract).then_inc(sems["w_lo"], 1)

            def norm_stats(i, q, ln, total, stat, mv):
                need(dve, f"{ln}_sum", i, q + 1)
                dve.bn_stats(stat[:, q, :], total[:, q, :]).then_inc(sems[f"{ln}_stat"], 1)
                apart(dve, sems[f"{ln}_stat"], i * PER[f"{ln}_stat"] + q + 1)
                dve.bn_aggr(mv[:, q, :], stat[:, q, :]).then_inc(sems[f"{ln}_mv"], 1)

            with dve.Fori(0, GROUPS) as i:
                need(dve, "xT_hi", i)
                need(dve, "kv_proj", i, 0)
                dve.tensor_tensor(xT16[:, 1, :, :], xT[:, :, :], xT16[:, 0, :, :], ALU.subtract).then_inc(sems["xT_lo"], 1)
                for q in range(TQ):
                    need(dve, "kv_proj", i, q + 1)
                    if q == 0:
                        need(dve, "kv_state", i, 0)
                    keys, vals = bP[q % 2][:, 0:D], bP[q % 2][:, D:2 * D]
                    dve.scalar_tensor_tensor(kb[:, q, :], keys, W_BACK, bk_row, ALU.mult, ALU.add
                                             ).then_inc(sems["kv_read"], 1)
                    dve.scalar_tensor_tensor(vb[:, q, :, 0:P], vals.rearrange("p (c n) -> p c n", c=KC), W_BACK,
                                             bv_row.rearrange("p (c n) -> p c n", c=KC), ALU.mult, ALU.add
                                             ).then_inc(sems["kv_read"], 1)

                def state_masks(b):
                    need(dve, "kv_state", i, b + 1)
                    if b >= 2:
                        need(dve, "attn_nd", i, b - 1)
                    st = bK[b % 2][:, 0:KC * (P + 1)].rearrange("p (c n) -> p c n", c=KC)
                    blocks = bc(head_mask.unsqueeze(1), [P, KC, P])
                    dve.tensor_tensor(kv_m[:, b % 2, :, 0:P], st[:, :, 0:P], blocks, ALU.mult).then_inc(sems["kv_masked"], 1)
                    dve.tensor_tensor(kv_m[:, b % 2, :, P:AW], bc(st[:, :, P:P + 1], [P, KC, AW - P]),
                                      bc(const("head_pick").unsqueeze(1), [P, KC, AW - P]), ALU.mult
                                      ).then_inc(sems["kv_masked"], 1)

                def attention_rows(q):
                    both = (bN, bE)[q % 2][:, 0:KC * AW].rearrange("p (c n) -> p c n", c=KC)
                    need(dve, "attn_nd", i, 2 * (q + 1))
                    dve.tensor_scalar(den[:, q % 2, :, :], both[:, :, P:AW], const("attn_eps"), None, ALU.add
                                      ).then_inc(sems["attn_den"], 1)
                    need(dve, "attn_den", i, q + 1)
                    dve.reciprocal(den[:, q % 2, :, :], den[:, q % 2, :, :]).then_inc(sems["attn_rec"], 1)
                    need(dve, "attn_rec", i, q + 1)
                    if q >= 2:
                        need(dve, "attn_T", i, q - 1)
                    for c in range(KC):
                        last = dve.tensor_tensor(a32[:, q % 2, c * P:(c + 1) * P].rearrange("p (h d) -> p h d", d=HD),
                                                 both[:, c, 0:P].rearrange("p (h d) -> p h d", d=HD),
                                                 bc(den[:, q % 2, c, :].unsqueeze(2), [P, P // HD, HD]), ALU.mult)
                    last.then_inc(sems["attn_div"], 1)

                def attention_lo(q):
                    need(dve, "attn_hi", i, q + 1)
                    if q >= 2:
                        need(dve, "wo_done", i, q - 1)
                    dve.tensor_tensor(a16[:, q % 2, 1, :, :], bP[q % 2][:, 0:D].rearrange("p (c n) -> p c n", c=KC),
                                      a16[:, q % 2, 0, :, :], ALU.subtract).then_inc(sems["attn_lo"], 1)

                def first_norm(q):
                    need(dve, "wo_done", i, q + 1)
                    if q == 0:
                        need(dve, "x_bo", i)
                        need(dve, "x1T", i, 0)
                        need(dve, "x1_bc", i, 0)
                    dve.scalar_tensor_tensor(x1[:, q, :], bW[:, 0:D], W_BACK, x_in[:, q, :], ALU.mult, ALU.add
                                             ).then_inc(sems["ln1_sum"], 1)
                    norm_stats(i, q, "ln1", x1, stat1, mv1)

                def first_normed(q):
                    need(dve, "ln1_std", i, q + 1)
                    dve.reciprocal(rstd1[:, q:q + 1], std1[:, q:q + 1]).then_inc(sems["ln1_rstd"], 1)
                    need(dve, "ln1_rstd", i, q + 1)
                    dve.tensor_scalar(x1[:, q, :], x1[:, q, :], mv1[:, q, 0:1], rstd1[:, q:q + 1], ALU.subtract,
                                      ALU.mult).then_inc(sems["x1_norm"], 1)

                for step in range(GB + 7):
                    if step < GB:
                        state_masks(step)
                    if step >= 2 and step % 2 == 0 and step < GB + 2:
                        attention_rows(step // 2 - 1)
                    if step >= 3 and step % 2 and step < GB + 3:
                        attention_lo((step - 3) // 2)
                    if step >= 5 and step % 2 and step < GB + 5:
                        first_norm((step - 5) // 2)
                    if step >= 6 and step % 2 == 0 and step < GB + 6:
                        first_normed(step // 2 - 3)
                split_expert(i, 0)

                def x1T_lo(q):
                    need(dve, "x1T_hi", i, q + 1)
                    if q == 0:
                        need(dve, "st_done", i, 0)
                    dve.tensor_tensor(xh[0:C, 1, q, :, :].rearrange("p b (h s) -> p h b s", h=HPG),
                                      bT[0:C, :].rearrange("p (h b s) -> p h b s", h=HPG, b=2),
                                      xh[0:C, 0, q, :, :].rearrange("p b (h s) -> p h b s", h=HPG), ALU.subtract
                                      ).then_inc(sems["x1T_lo"], 1)

                def second_norm(q):
                    need(dve, "wc_done", i, q + 1)
                    need(dve, "x1_bc", i, q + 1)
                    if q == 0:
                        need(dve, "row_hi", i, 0)
                        need(dve, "row_lo", i, 0)
                        need(dve, "st_acc", i, 0)
                    dve.scalar_tensor_tensor(x2[:, q, :], bW[:, 0:D], W_BACK, x_in[:, q, :], ALU.mult, ALU.add
                                             ).then_inc(sems["ln2_sum"], 1)
                    norm_stats(i, q, "ln2", x2, stat2, mv2)

                def second_normed(q):
                    dve.tensor_scalar(x2[:, q, :], x2[:, q, :], mv2[:, q, 0:1], rstd2[:, q:q + 1], ALU.subtract,
                                      ALU.mult).then_inc(sems["x2_norm"], 1)

                x1T_lo(0)
                for step in range(GB + 6):
                    if step % 2 == 0 and step // 2 + 1 < TQ:
                        x1T_lo(step // 2 + 1)
                    if step < GB:
                        need(dve, "s_done", i, step + 1)
                        if step >= 2:
                            need(dve, "m_T", i, step - 1)
                        with nc.allow_low_precision("any value near the maximum guards the softmax"):
                            dve.tensor_reduce(m16[:, step % 2, :], bK[step % 2][:, :].rearrange("p (a t) -> p a t", t=S),
                                              AX, ALU.max).then_inc(sems["s_max"], 1)
                    if 3 <= step < GB + 3:
                        b = step - 3
                        o = (bN, bP[1])[b % 2][:, 0:2 * NG * (HD + 1)].rearrange("p (a n) -> p a n", n=HD + 1)
                        need(dve, "pv_done", i, b + 1)
                        if b >= 2:
                            need(dve, "pv_norm", i, b - 1)
                        if b == 0:
                            need(dve, "aT", i, 0)
                        dve.reciprocal(rec[:, b % 2, :], o[:, :, HD]).then_inc(sems["pv_rec"], 1)
                        need(dve, "pv_rec", i, b + 1)
                        dve.tensor_tensor(a2[:, b, :].rearrange("p (a d) -> p a d", d=HD), o[:, :, 0:HD],
                                          bc(rec[:, b % 2, :].unsqueeze(2), [P, 2 * NG, HD]), ALU.mult
                                          ).then_inc(sems["pv_norm"], 1)
                    if step >= 5 and step % 2 and step < GB + 5:
                        q = (step - 5) // 2
                        need(dve, "aT_hi", i, q + 1)
                        if q >= 2:
                            need(dve, "wc_done", i, q - 1)
                        dve.tensor_tensor(aT16[:, q % 2, 1, :, :].rearrange("p e (b s) -> p b e s", b=2),
                                          bT[:, 0:D].rearrange("p (b e s) -> p b e s", b=2, e=2),
                                          aT16[:, q % 2, 0, :, :].rearrange("p e (b s) -> p b e s", b=2), ALU.subtract
                                          ).then_inc(sems["aT_lo"], 1)
                    if step >= 6 and step % 2 == 0:
                        q = (step - 6) // 2
                        second_norm(q)
                need(dve, "ln2_std", i)
                dve.reciprocal(rstd2[:, :], std2[:, :]).then_inc(sems["ln2_rstd"], 1)
                need(dve, "ln2_rstd", i)
                for q in range(TQ):
                    second_normed(q)

                for q in range(TQ):
                    need(dve, "x2T", i, q + 1)
                    if q == 0:
                        need(dve, "u_done", i, 0)
                    dve.tensor_copy(x2T16[:, :, :, q * P:(q + 1) * P].rearrange("p s k n -> p (s k) n"),
                                    half((bT, bW)[q % 2])[:, 0:2 * KC * P].rearrange("p (a n) -> p a n", n=P)
                                    ).then_inc(sems["x2T_read"], 1)

                done = [0]

                def link(instruction, alone=False):
                    done[0] += 1
                    instruction.then_inc(sems["r_chain"], 1)
                    if not alone:
                        apart(dve, sems["r_chain"], i * R_CHAIN + done[0])

                def softmax_shift():
                    need(dve, "router", i)
                    link(dve.tensor_scalar(lg[:, :, :], bP[0][:, 0:TQ * (E + 1)].rearrange("p (q e) -> p q e", e=E + 1),
                                           W_BACK, None, ALU.mult))
                    logits = lg[:, :, 0:E]
                    link(dve.tensor_reduce(lg_max[:, :], logits, AX, ALU.max))
                    link(dve.tensor_tensor(shifted[:, :, :], logits, bc(lg_max[:, :].unsqueeze(2), [P, TQ, E]),
                                           ALU.subtract))
                    assert done[0] == R_SHIFT

                def top_experts():
                    need(dve, "r_exp", i, 1)
                    link(dve.tensor_reduce(ex_sum[:, :], ex[:, :, :], AX, ALU.add))
                    link(dve.reciprocal(ex_rec[:, :], ex_sum[:, :]))
                    link(dve.tensor_tensor(prob[:, :, :], ex[:, :, :], bc(ex_rec[:, :].unsqueeze(2), [P, TQ, E]), ALU.mult))
                    for q in range(TQ):
                        link(dve.max(top_v[:, q, :], prob[:, q, :]), alone=q < TQ - 1)
                    for q in range(TQ):
                        link(dve.max_index(top_i[:, q, :], top_v[:, q, :], prob[:, q, :]), alone=q < TQ - 1)
                    link(dve.tensor_copy(top_f[:, :, :], top_i[:, :, 0:TOPK]))
                    link(dve.tensor_tensor(onehot[:, :, :, :].rearrange("p q j e -> p (q j) e"),
                                           bc(top_f[:, :, :].rearrange("p q j -> p (q j)").unsqueeze(2), [P, TQ * TOPK, E]),
                                           bc(const("iota").unsqueeze(1), [P, TQ * TOPK, E]), ALU.is_equal))
                    with nc.allow_low_precision("zeros and ones"):
                        link(dve.tensor_reduce(mask16[:, 0:TQ, :], onehot[:, :, :, :].rearrange("p q j e -> p q e j"),
                                               AX, ALU.add))
                    assert done[0] == R_MASK

                def row_weights():
                    link(dve.tensor_reduce(w_sum[:, :], top_v[:, :, 0:TOPK], AX, ALU.add), alone=True)
                    link(dve.tensor_tensor(chosen[:, :, :], mask16[:, 0:TQ, :], prob[:, :, :], ALU.mult))
                    link(dve.tensor_scalar(w_clip[:, :], w_sum[:, :], TOP_MIN, None, ALU.max))
                    link(dve.reciprocal(w_rec[:, :], w_clip[:, :]))
                    need(dve, "scattered", i, 0)
                    link(dve.tensor_copy(row[:, :, ROW - 1:ROW].bitcast(U32), token[:, :].unsqueeze(2)), alone=True)
                    link(dve.scalar_tensor_tensor(row[:, :, D:D + E], chosen[:, :, :], W_BACK,
                                                  bc(w_rec[:, :].unsqueeze(2), [P, TQ, E]), ALU.mult, ALU.mult))
                    link(dve.tensor_scalar(token[:, :], token[:, :], float(GT), None, ALU.add), alone=True)

                def region_rows():
                    need(dve, "rank", i)
                    link(dve.tensor_tensor(pos[:, :, :], bE[:, 0:TQ * E].rearrange("p (q e) -> p q e", e=E),
                                           bc(count[:, :].unsqueeze(1), [P, TQ, E]), ALU.add))
                    link(dve.tensor_tensor(count[:, :], count[:, :], bE[:, TQ * E:(TQ + 1) * E], ALU.add), alone=True)
                    link(dve.tensor_tensor(pos_sel[:, :, :, :], onehot[:, :, :, :],
                                           bc(pos[:, :, :].unsqueeze(2), [P, TQ, TOPK, E]), ALU.mult))
                    link(dve.tensor_reduce(pos_f[:, :], pos_sel[:, :, :, :].rearrange("p q j e -> p (q j) e"),
                                           AX, ALU.add))
                    link(dve.tensor_copy(pos_u[:, :], pos_f[:, :]))

                def shared_gates():
                    need(dve, "r_exp", i)
                    link(dve.tensor_scalar(sg_d[:, :], sg_e[:, :], 1.0, W_SCALE, ALU.add, ALU.mult))
                    link(dve.reciprocal(sg[:, :], sg_d[:, :]))

                split_expert(i, 1)
                softmax_shift()
                top_experts()
                between = {0: row_weights, 2: region_rows, 4: shared_gates}
                for c in range(IC + 1):
                    if c < IC:
                        n, bu = chunk_rows(c), (bK[1], bN)[c % 2]
                        need(dve, "u_done", i, c + 1)
                        need(dve, "silu", i, c + 1)
                        if c >= 2:
                            need(dve, "h_hi", i, c - 1)
                            need(dve, "h_lo", i, c - 1)
                        dve.scalar_tensor_tensor(h32[0:n, c % 2, :], bu[0:n, :], W_BACK, gate[0:n, c % 2, :], ALU.mult,
                                                 ALU.mult).then_inc(sems["h_mul"], 1)
                    if c >= 1:
                        n = chunk_rows(c - 1)
                        need(dve, "h_hi", i, c)
                        if c == 1:
                            need(dve, "down", i, 0)
                        dve.tensor_tensor(h16[0:n, 1, c - 1, :], h32[0:n, (c - 1) % 2, :], h16[0:n, 0, c - 1, :],
                                          ALU.subtract).then_inc(sems["h_lo"], 1)
                    if c in between:
                        between[c]()
                    if c == 3:
                        split_expert(i, 2)
                assert done[0] == R_CHAIN, done[0]
                split_expert(i, 3)

                for q in range(TQ):
                    need(dve, "down", i, q + 1)
                    dve.scalar_tensor_tensor(x2[:, q, :], (bW, bT)[q % 2][:, 0:D], sg[:, q:q + 1], x2[:, q, :],
                                             ALU.mult, ALU.add).then_inc(sems["acc_row"], 1)

            tdone = [0]

            def tlink(instruction):
                tdone[0] += 1
                instruction.then_inc(sems["t_chain"], 1)
                dve.wait_ge(sems["t_chain"], tdone[0])

            tlink(dve.tensor_tensor(passed[:, :], count[:, :], const("region"), ALU.subtract))
            tlink(dve.tensor_tensor(more[:, :, :], bc(passed[:, :].unsqueeze(2), [P, E, E]),
                                    bc(const("steps").unsqueeze(1), [P, E, E]), ALU.is_gt))
            tlink(dve.tensor_reduce(tiles[:, :], more[:, :, :], AX, ALU.add))
            tlink(dve.tensor_tensor(tiles_to[:, :, :], bc(tiles[:, :].unsqueeze(1), [P, E, E]),
                                    const("upto").rearrange("p (a b) -> p a b", a=E), ALU.mult))
            tlink(dve.tensor_reduce(cum[:, :], tiles_to[:, :, :], AX, ALU.add))
            tlink(dve.tensor_scalar(passed[:, :], cum[:, :], const("slot"), None, ALU.is_le))
            tlink(dve.tensor_tensor(passed_t[:, :], passed[:, :], tiles[:, :], ALU.mult))
            tlink(dve.tensor_reduce(slot_f[:, 2:3], passed[:, :], AX, ALU.add))
            tlink(dve.tensor_reduce(slot_f[:, 3:4], passed_t[:, :], AX, ALU.add))
            tlink(dve.tensor_scalar(slot_f[:, 0:1], slot_f[:, 2:3], float(E - 1), None, ALU.min))
            tlink(dve.tensor_tensor(slot_f[:, 4:5], const("slot"), slot_f[:, 3:4], ALU.subtract))
            tlink(dve.tensor_scalar(slot_f[:, 5:6], slot_f[:, 4:5], float(P), None, ALU.mult))
            tlink(dve.scalar_tensor_tensor(slot_f[:, 1:2], slot_f[:, 2:3], float(REGION), slot_f[:, 5:6], ALU.mult,
                                           ALU.add))
            tlink(dve.tensor_scalar(evens_below[:, :], const("evens"), cum[:, E - 1:E], None, ALU.is_lt))
            tlink(dve.tensor_reduce(slot_f[:, 7:8], evens_below[:, :], AX, ALU.add))
            tlink(dve.tensor_copy(tab[0:1, TAB_PAD:TAB_PAD + E], count[0:1, :]))
            tlink(dve.tensor_copy(tab[0:1, TAB_LAPS:TAB_LAPS + 1], slot_f[0:1, 7:8]))
            tlink(dve.memset(eh[:, :, :], 0.0))
            assert tdone[0] == T_CHAIN
            dve.wait_ge(sems["t_rows"], 1)
            dve.tensor_copy(tab[0:1, 0:2 * P], bP[0][0:1, 0:2 * P]).then_inc(sems["t_four"], 1)
            dve.wait_ge(sems["t_four"], 1)
            experts = tab[0:1, 0:P].rearrange("a (j p) -> a j p", p=2)
            pair_row = four[0:1, 0:P // 2].unsqueeze(2)
            dve.scalar_tensor_tensor(pair_row, experts[:, :, 1:2], float(E), experts[:, :, 0:1], ALU.mult, ALU.add
                                     ).then_inc(sems["t_four"], 1)
            dve.wait_ge(sems["t_four"], 2)
            dve.scalar_tensor_tensor(tab[0:1, TAB_FOUR + 1:TAB_FOUR + P // 2], four[0:1, 1:P // 2], float(E * E),
                                     four[0:1, 0:P // 2 - 1], ALU.mult, ALU.add).then_inc(sems["t_tab"], 1)

            def slot_read(j, p):
                dve.wait_ge(slot_sem["xg_T"][p], j + 1)
                dve.wait_ge(slot_sem["e_gu"][p], j)
                dve.tensor_copy(xgT[:, p, :, :], half((bT, bE)[p])[:, 0:2 * KC * P].rearrange("p (a n) -> p a n", n=P)
                                ).then_inc(slot_sem["xg_read"][p], 1)

            def slot_product(j, p):
                dve.wait_ge(slot_sem["e_silu"][p], j + 1)
                dve.wait_ge(slot_sem["e_hT"][p], j)
                dve.scalar_tensor_tensor(eh[:, p, 0:IM], bP[p][:, IM:2 * IM], W_BACK, e_gate[:, p, :], ALU.mult, ALU.mult
                                         ).then_inc(slot_sem["e_mul"][p], 1)

            def slot_meta(j, p):
                dve.wait_ge(slot_sem["e_yw"][p], j)
                dve.wait_ge(slot_sem["e_id"][p], j)
                dve.tensor_copy(meta[:, p, :].bitcast(U32), xg[:, p, D:ROW].bitcast(U32)).then_inc(slot_sem["meta"][p], 1)

            def slot_h_lo(j, p):
                dve.wait_ge(slot_sem["e_hhi"][p], j + 1)
                dve.tensor_tensor(ehT[:, p, 1, :, :], bK[p][:, 0:KC * P].rearrange("p (k n) -> p k n", k=KC),
                                  ehT[:, p, 0, :, :], ALU.subtract).then_inc(slot_sem["e_hlo"][p], 1)

            dve.wait_ge(sems["t_tab"], 1)
            laps = dve.value_load(tab[0:1, TAB_LAPS:TAB_LAPS + 1], min_val=0, max_val=P // 2 - 1)
            slot_read(0, 0)
            slot_product(0, 0)
            slot_meta(0, 0)
            slot_read(0, 1)
            slot_h_lo(0, 0)
            slot_product(0, 1)
            slot_meta(0, 1)
            with dve.Fori(0, laps) as j:
                slot_read(j + 1, 0)
                slot_h_lo(j, 1)
                slot_product(j + 1, 0)
                slot_meta(j + 1, 0)
                slot_read(j + 1, 1)
                slot_h_lo(j + 1, 0)
                slot_product(j + 1, 1)
                slot_meta(j + 1, 1)
            slot_h_lo(laps, 1)

            with dve.Fori(0, GROUPS // 2) as j:
                for p in range(2):
                    dve.wait_ge(slot_sem["f_in"][p], 32 * (j + 1))
                    dve.wait_ge(slot_sem["f_st"][p], 16 * j)
                    dve.tensor_tensor(fsum[p][:, :, :], fa[:, p, 0, :, :], fa[:, p, 1, :, :], ALU.add
                                      ).then_inc(slot_sem["f_sum"][p], 1)
                    dve.wait_ge(slot_sem["f_sum"][p], j + 1)
                    for q in range(TQ):
                        dve.bn_stats(fstat[:, p, q, :], fsum[p][:, q, :]).then_inc(slot_sem["f_stat"][p], 1)
                    apart(dve, slot_sem["f_stat"][p], TQ * (j + 1))
                    for q in range(TQ):
                        dve.bn_aggr(fmv[:, p, q, :], fstat[:, p, q, :]).then_inc(slot_sem["f_mv"][p], 1)
                for p in range(2):
                    dve.wait_ge(slot_sem["f_std"][p], j + 1)
                    dve.reciprocal(frstd[:, p, :], fstd[:, p, :]).then_inc(slot_sem["f_rstd"][p], 1)
                    dve.wait_ge(slot_sem["f_rstd"][p], j + 1)
                    for q in range(TQ):
                        dve.tensor_scalar(fsum[p][:, q, :], fsum[p][:, q, :], fmv[:, p, q, 0:1], frstd[:, p, q:q + 1],
                                          ALU.subtract, ALU.mult).then_inc(slot_sem["f_out"][p], 1)

        @block.gpsimd
        def _(pool):
            pool.memset(c16[0:C, :, :, :], 0.0).then_inc(sems["setup"], 1)
            pool.memset(v_stage[:, :, :, :], 0.0).then_inc(sems["setup"], 1)
            pool.memset(zeros[:, :], 0.0).then_inc(sems["setup"], 1)
            pool.memset(pad_row[:, 0:ROW - 1], 0.0)
            pool.memset(pad_row[:, ROW - 1:ROW].bitcast(U32), NO_TOKEN).then_inc(sems["setup"], 1)
            for g in range(2):
                pool.wait_ge(sems["setup"], SETUP - 1)
                w = g * (HD + 1) + HD
                ones = pool.memset(v_stage[g * S:(g + 1) * S, :, :, w:w + 1], 1.0)
            ones.then_inc(sems["setup"], 1)

            with pool.Fori(0, GROUPS) as i:
                need(pool, "ld_x", i)
                pool.tensor_tensor(x_in[:, :, :], x_in[:, :, :], bc(bo_row.unsqueeze(1), [P, TQ, D]), ALU.add
                                   ).then_inc(sems["x_bo"], 1)
                need(pool, "ctx_hi", i)
                need(pool, "ctx_in", i, 0)
                pool.tensor_tensor(c_parts[:, 1, :, :], c_stage[:, :, :], c_parts[:, 0, :, :], ALU.subtract
                                   ).then_inc(sems["ctx_lo"], 1)
                need(pool, "v_hi", i)
                need(pool, "pv_done", i, 0)
                pool.tensor_tensor(v16[:, 1, :, :, :].rearrange("p b g n -> p (b g n)"),
                                   v_stage[:, :, :, :].rearrange("p b g n -> p (b g n)"),
                                   v16[:, 0, :, :, :].rearrange("p b g n -> p (b g n)"), ALU.subtract
                                   ).then_inc(sems["v_lo"], 1)
                for q in range(TQ):
                    need(pool, "x1_norm", i, q + 1)
                    need(pool, "ln1_sum", i, q + 1)
                    pool.tensor_tensor(x_in[:, q, :], x1[:, q, :], bc_row, ALU.add).then_inc(sems["x1_bc"], 1)
                for step in range(2, GB + 2):
                        b = step - 2
                        need(pool, "e_hi", i, b + 1)
                        need(pool, "exp_done", i, b + 1)
                        if b >= 2:
                            need(pool, "pv_done", i, b - 1)
                        pool.tensor_tensor(e16[:, b % 2, 1, :, :], e32[:, b % 2, :, :], e16[:, b % 2, 0, :, :],
                                           ALU.subtract).then_inc(sems["e_lo"], 1)
                for q in range(TQ):
                    need(pool, "row_hi", i, q + 1)
                    pool.tensor_tensor(row16[:, q, D:2 * D], x2[:, q, :], row16[:, q, 0:D], ALU.subtract
                                       ).then_inc(sems["row_lo"], 1)
                need(pool, "r_chain", i)
                apart(pool, sems["row_lo"], (i + 1) * PER["row_lo"])
                for q in range(TQ):
                    for k in range(TOPK):
                        a = q * TOPK + k
                        pool.indirect_dma_start(xs, bass.IndirectOffsetOnAxis(ap=pos_u[:, a:a + 1], axis=0),
                                                row[:, q, :], None).then_inc(sems["scattered"], 16)

            need(pool, "st_acc", GROUPS - 1)
            pool.wait_ge(sems["st_zero"], 16)
            pool.wait_ge(sems["t_tab"], 1)
            laps = pool.value_load(tab[0:1, TAB_LAPS:TAB_LAPS + 1], min_val=0, max_val=P // 2 - 1)
            with pool.Fori(0, laps + 1) as j:
                for p in range(2):
                    apart(pool, slot_sem["e_add"][p], 16 * j)
                    apart(pool, slot_sem["meta"][p], j + 1)
                    pool.tensor_copy(ids[:, p:p + 1], meta[:, p, E:E + 1].bitcast(U32)).then_inc(slot_sem["e_id"][p], 1)
                    apart(pool, slot_sem["e_yw"][p], j + 1)
                    apart(pool, slot_sem["e_id"][p], j + 1)
                    pool.indirect_dma_start(acc[p], bass.IndirectOffsetOnAxis(ap=ids[:, p:p + 1], axis=0), ye[:, p, :],
                                            None, bounds_check=N - 1, oob_is_err=False, compute_op=ALU.add
                                            ).then_inc(slot_sem["e_add"][p], 16)


R_SHIFT, R_MASK = 3, 17
T_CHAIN = 18


def constants():
    import numpy as np
    cf = {
        "ident": np.eye(P), "head_mask": np.kron(np.eye(P // HD), np.ones((HD, HD))),
        "attn_eps": (np.float32(ATTN_EPS) / np.exp(-(np.arange(P, dtype=np.float32) % S) / np.float32(S)))[:, None],
        "head_pick": np.kron(np.eye(P // HD), np.ones((HD, 1))),
        "decay_col": np.exp(-(np.arange(P, dtype=np.float32) % S) / np.float32(S))[:, None],
        "slot": np.arange(P)[:, None], "token": np.arange(P)[:, None] + P * np.arange(TQ),
        "ln_eps": np.full((P, 1), LN_EPS), "iota": np.broadcast_to(np.arange(E), (P, E)),
        "region": np.broadcast_to(REGION * np.arange(E), (P, E)),
        "steps": np.broadcast_to(P * np.arange(E), (P, E)),
        "evens": np.broadcast_to(2 + 2 * np.arange(P // 2), (P, P // 2)),
        "upto": np.broadcast_to(np.tri(E).reshape(-1), (P, E * E)),
    }
    cf = np.concatenate([cf[name].astype(np.float32) for name in CF_PARTS], axis=1)
    ch = np.concatenate([np.eye(P), np.tri(P, k=-1).T, np.ones((P, P))], axis=1).astype(np.float16)
    pick = np.kron(np.eye(NG), np.ones(S)).astype(np.float16)
    return {"cf": cf, "ch": ch, "pick": np.ascontiguousarray(np.broadcast_to(pick[:, None, :], (NG, GB, NG * S)))}


def kernel(**inputs):
    import numpy as np
    import concourse.bacc as bacc
    from concourse.bass_utils import run_bass_kernel_spmd

    a = {k: np.asarray(v) for k, v in inputs.items()}
    pre = "L0_"

    def chunks(w):
        n = -(-w.shape[0] // P)
        full = np.zeros((n * P, w.shape[1]), w.dtype)
        full[:w.shape[0]] = w
        return full.reshape(n, P, w.shape[1]).transpose(1, 0, 2).reshape(P, -1)

    def by_head(w, axis=-1):
        w = np.moveaxis(w, axis, 0)
        return np.moveaxis(w.reshape(NG, HPG, HD, -1).swapaxes(0, 1).reshape(w.shape), 0, axis)

    wc = by_head(a[pre + "xattn_Wc"].T).reshape(NG, 2, 2, HD, D)
    wc = wc.transpose(2, 1, 0, 3, 4).reshape(D, D)
    w = [
        chunks(a[pre + "attn_Wq"].T),
        chunks(np.concatenate([a[pre + "attn_Wk"].T, a[pre + "attn_Wv"].T], axis=1)),
        chunks(by_head(a[pre + "attn_Wo"].T)), chunks(wc),
        chunks(by_head(np.concatenate([a[pre + "ffn_router_w"].T, a[pre + "ffn_sh_gate_w"]], axis=1), 0)),
        chunks(by_head(np.concatenate([a[pre + "ffn_sh_gate"], a[pre + "ffn_sh_up"]], axis=1), 0)),
        chunks(by_head(a[pre + "ffn_sh_down"])),
    ]
    gu = by_head(np.concatenate([a[pre + "ffn_w_gate"], a[pre + "ffn_w_up"]], axis=2), 1)
    down = by_head(a[pre + "ffn_w_down"])
    x = a["x"].reshape(N, D)
    data = {
        "x": by_head(x), "xT": np.ascontiguousarray(x.T).reshape(KC, P, N),
        "ctx": a["ctx_512"], "ctxT": np.ascontiguousarray(a["ctx_512"].transpose(2, 0, 1)),
        "bq": np.ascontiguousarray(a[pre + "attn_bq"].reshape(KC, P).T),
        "biases": np.concatenate([a[pre + "attn_bk"], a[pre + "attn_bv"], by_head(a[pre + "attn_bo"]),
                                  by_head(a[pre + "xattn_bc"])]),
        "w": np.concatenate(w, axis=1),
        "e_w": np.stack([np.concatenate([chunks(gu[e]), chunks(down[e])], axis=1) for e in range(E)]),
        **constants(),
    }
    nc = bacc.Bacc("TRN2", target_bir_lowering=False, num_devices=1)
    args = {k: nc.dram_tensor(f"in_{k}", v.shape, mybir.dt.from_np(v.dtype), kind="ExternalInput").ap()
            for k, v in data.items()}
    out = nc.dram_tensor("out_0", (N, D), F32, kind="ExternalOutput").ap()
    decoder_layer_program(nc, args, out)
    r = run_bass_kernel_spmd(nc, [{f"in_{k}": v for k, v in data.items()}], core_ids=[0])
    by_group = r.results[0]["out_0"].reshape(N, HPG, NG, HD).swapaxes(1, 2)
    return np.ascontiguousarray(by_group).reshape(B, S, D)
```

```python
from contextlib import ExitStack

import concourse.bass as bass
from concourse import mybir

F32, F16 = mybir.dt.float32, mybir.dt.float16
U32, I32 = mybir.dt.uint32, mybir.dt.int32
ALU = mybir.AluOpType
ACT = mybir.ActivationFunctionType
AX = mybir.AxisListType.X

P = 128
B, S, D = 32, 64, 256
N = B * S
KC = D // P
HD = 16
NG, HPG = 4, 4
C = NG * HD
AW = P + P // HD
VW = 2 * (HD + 1)
E, TOPK = 16, 4
IM, IS = 176, 704
IC = -(-IS // P)
FULL = (IC - 1) * P
assert IS - FULL == P // 2
W_SCALE = 64.0
W_BACK = 1.0 / W_SCALE
ATTN_EPS, LN_EPS, TOP_MIN = 1e-6, 1e-5, 1e-9

GROUPS = 4
GT = N // GROUPS
TQ = GT // P
GB = GT // S
EPG = E // GROUPS

ROW = D + E + 1
REGION = N + P
DUMP = E * REGION
ROUND = 4
NO_TOKEN = 1 << 20

W_PARTS = dict(q=KC * D, kv=KC * 2 * D, o=KC * D, c=KC * D, r=KC * (E + 1), gu=KC * 2 * IS, dn=IC * D)
W_AT, _n = {}, 0
for _name, _cols in W_PARTS.items():
    W_AT[_name] = _n
    _n += _cols
W_COLS = _n
_cuts = [0, W_AT["o"], W_AT["gu"], W_AT["gu"] + 2 * IS, W_AT["dn"], W_COLS]
W_PIECES = list(zip(_cuts, _cuts[1:]))
EG = KC * 2 * IM
EW = EG + KC * D

CF_PARTS = dict(ident=P, head_mask=P, head_pick=P // HD, attn_eps=1, decay_col=1, slot=1, token=TQ, ln_eps=1, iota=E,
                region=E, steps=E, upto=E * E, rounds=P // ROUND)
CF_AT, _n = {}, 0
for _name, _cols in CF_PARTS.items():
    CF_AT[_name] = _n
    _n += _cols
CF_COLS = _n
R_CHAIN = 31

PER = dict(
    ld_xT=16, ld_x=16, ld_ctx=16, ctx_in=16 * 3 * NG, ld_v=16 * NG, ld_exp=16 * EPG, st_acc=16,
    scattered=16 * TQ * TOPK,
    xT_hi=1, xT_lo=1, ctx_hi=1, ctx_lo=1, v_hi=1, v_lo=1, x_bo=1,
    q_proj=KC, q_relu=KC, kv_proj=TQ, kv_read=2 * TQ, k_relu=TQ,
    kv_state=GB, kv_masked=2 * GB, attn_nd=GB, attn_den=TQ, attn_rec=TQ, attn_div=TQ, attn_T=TQ, attn_hi=TQ, attn_lo=TQ,
    wo_done=TQ, ln1_sum=TQ, ln1_stat=TQ, ln1_mv=TQ, ln1_std=TQ, ln1_rstd=TQ, x1_norm=TQ, x1_bc=TQ,
    x1T=TQ, x1T_hi=TQ, x1T_lo=TQ, x1T_again=TQ, s_done=GB, s_max=GB, m_T=GB, m_copied=GB, st_done=GB,
    exp_done=GB, e_hi=GB, e_lo=GB, pv_done=GB, pv_rec=GB, pv_norm=GB, aT=TQ, aT_hi=TQ, aT_lo=TQ,
    wc_done=TQ, ln2_sum=TQ, ln2_stat=TQ, ln2_mv=TQ, ln2_std=3, ln2_rstd=3, x2_norm=TQ,
    row_hi=TQ, row_lo=TQ, x2T=TQ, x2T_read=TQ, router=1, r_chain=R_CHAIN, r_exp=2, rank=1,
    g_done=IC, u_done=IC - 1, silu=IC, h_mul=IC, h_hi=IC, h_lo=IC, down=TQ, acc_row=TQ,
    w_hi=EPG, w_lo=EPG,
)
SLOT_SEMS = ("xg_in", "xg_T", "xg_read", "meta", "e_gu", "e_silu", "e_mul", "e_hT", "e_hhi", "e_hlo",
             "e_y", "e_yw", "e_id", "e_add")
LAST = N // P // 2
LAST_SEMS = (*(f"f_in{g}" for g in range(LAST)), "f_sum0", "f_sum1", "f_stat", "f_mv", "f_std", "f_rstd", "f_out", "f_st")
ONCE_SEMS = ("ld_const", *(f"ld_w{n}" for n in range(len(W_PIECES))), "ld_ind", "setup", "ws_hi", "ws_lo", "st_zero", "t_pad",
             "t_chain", "t_rows", "t_packed", "t_tab", "st_pad", "waits_apart")
SETUP = 9

THREE = ((0, 0), (1, 0), (0, 1))


def chunk_rows(c):
    return min(P, IS - c * P)


def decoder_layer_program(nc, t, out):
    xs = nc.dram_tensor("xs_rows", [DUMP + (ROUND - 1) * P, ROW], F32, kind="Internal").ap()
    acc = [nc.dram_tensor(f"acc{p}", [N, D], F32, kind="Internal").ap() for p in range(2)]

    with ExitStack() as ctx:
        def sb(name, shape, dt=F32):
            return ctx.enter_context(nc.sbuf_tensor(name, shape, dt))

        def over(buffer, shape, dt=F32, at=0):
            cols = 1
            for n in shape[1:]:
                cols *= n
            cols = cols if dt != F16 else cols // 2
            view = buffer[0:shape[0], at:at + cols]
            if dt != F32:
                view = view.bitcast(dt)
            names = "abcde"[:len(shape) - 1]
            return view.rearrange(f"p ({' '.join(names)}) -> p {' '.join(names)}", **dict(zip(names, shape[1:])))

        w_stage = sb("w_stage", [P, W_COLS])
        w16 = sb("w16", [P, 2, W_COLS], F16)
        e_stage = sb("e_stage", [P, EW])
        e_w16 = sb("e_w16", [P, E, 2, EW], F16)
        cf = sb("cf", [P, CF_COLS])
        ch = sb("ch", [P, 3 * P], F16)
        bq_col = sb("bq_col", [P, KC])
        bias_rows = sb("bias_rows", [P, 4, D])
        bk_row, bv_row, bo_row, bc_row = (bias_rows[:, n, :] for n in range(4))

        def const(name):
            return cf[:, CF_AT[name]:CF_AT[name] + CF_PARTS[name]]

        ident, head_mask = const("ident"), const("head_mask")
        id16, tri16, ones16 = ch[:, 0:P], ch[:, P:2 * P], ch[:, 2 * P:3 * P]

        def weight(name, part, chunk, lo, n):
            width = {"q": D, "kv": 2 * D, "o": D, "c": D, "r": E + 1, "gu": 2 * IS, "dn": D}[name]
            a = W_AT[name] + chunk * width + lo
            return w16[:, part, a:a + n]

        xT = sb("xT", [P, KC, GT])
        x_in = sb("x_in", [P, TQ, D])
        c_stage = sb("c_stage", [C, GB, S])
        c_parts = sb("c_parts", [C, 2, GB, S], F16)
        c16 = sb("c16", [P, 2, GB, NG * S], F16)
        v_stage = sb("v_stage", [P, GB, 2, VW])
        v16 = sb("v16", [P, 2, GB, 2, VW], F16)
        vb = sb("vb", [P, TQ, KC, P + 1])
        x1 = sb("x1", [P, TQ, D])
        x2 = sb("x2", [P, TQ, D])
        row = sb("row", [P, TQ, ROW])
        row16 = row[:, :, 0:D].bitcast(F16)
        queries_then_x2T = sb("queries_then_x2T", [P, KC * GT])
        qd = over(queries_then_x2T, [P, KC, GT])
        x2T16 = over(queries_then_x2T, [P, 2, KC, GT], F16)
        xT_then_x1T = sb("xT_then_x1T", [P, 2 * TQ * HPG * S])
        xT16 = over(xT_then_x1T, [P, 2, KC, GT], F16)
        xh = over(xT_then_x1T, [P, 2, TQ, 2, HPG * S], F16)
        state_then_rows = sb("state_then_rows", [P, 4 * D])
        kv_m = over(state_then_rows, [P, 3, KC, AW])
        aT16 = over(state_then_rows, [P, 2, 2, 2, P], F16)
        onehot = over(state_then_rows, [P, TQ, TOPK, E], at=2 * D)
        pos_sel = over(state_then_rows, [P, TQ, TOPK, E], at=3 * D)
        kb = over(w_stage, [P, TQ, D])
        e32 = over(w_stage, [P, 2, 2, HPG * S])
        gate = over(w_stage, [P, 2, GT])
        h32 = over(w_stage, [P, 2, GT], at=2 * GT)
        a2 = over(w_stage, [P, GB, P], at=4 * GT)
        after = 4 * GT + GB * P
        h16 = over(w_stage, [P, 2, IC, GT], F16, at=after)
        a32 = over(w_stage, [P, 2, D], at=2 * GT)
        a16 = over(w_stage, [P, 2, 2, KC, P], F16, at=2 * GT + 2 * D)
        e16 = over(w_stage, [P, 2, 2, 2, HPG * S], F16, at=after + 4 * D)
        den = sb("den", [P, 2, KC, P // HD])
        m16 = sb("m16", [P, 2, 2 * NG], F16)
        stat1 = sb("stat1", [P, TQ, 6])
        mv1 = sb("mv1", [P, TQ, 2])
        rstd1 = sb("rstd1", [P, TQ])
        std1 = sb("std1", [P, TQ])
        rec = sb("rec", [P, 2, 2 * NG])
        stat2 = sb("stat2", [P, TQ, 6])
        mv2 = sb("mv2", [P, TQ, 2])
        rstd2 = sb("rstd2", [P, TQ])
        std2 = sb("std2", [P, TQ])
        lg = sb("lg", [P, TQ, E + 1])
        lg_max = sb("lg_max", [P, TQ])
        shifted = sb("shifted", [P, TQ, E])
        ex = sb("ex", [P, TQ, E])
        sg_e = sb("sg_e", [P, TQ])
        sg_d = sb("sg_d", [P, TQ])
        sg = sb("sg", [P, TQ])
        ex_sum = sb("ex_sum", [P, TQ])
        ex_rec = sb("ex_rec", [P, TQ])
        prob = sb("prob", [P, TQ, E])
        top_v = sb("top_v", [P, TQ, 8])
        top_i = sb("top_i", [P, TQ, 8], U32)
        top_f = sb("top_f", [P, TQ, TOPK])
        mask16 = sb("mask16", [P, TQ + 1, E], F16)
        chosen = sb("chosen", [P, TQ, E])
        w_sum = sb("w_sum", [P, TQ])
        w_clip = sb("w_clip", [P, TQ])
        w_rec = sb("w_rec", [P, TQ])
        count = sb("count", [P, E])
        pos = sb("pos", [P, TQ, E])
        pos_f = sb("pos_f", [P, TQ * TOPK])
        pos_u = sb("pos_u", [P, TQ * TOPK], U32)
        token = sb("token", [P, TQ])
        zeros = sb("zeros", [P, D])
        pad_row = sb("pad_row", [P, ROW])
        more = over(state_then_rows, [P, E, E])
        tiles = sb("tiles", [P, E])
        tiles_to = over(state_then_rows, [P, E, E], at=E * E)
        cum = sb("cum", [P, E])
        more_rounds = over(state_then_rows, [P, P // ROUND], at=3 * D)
        passed = sb("passed", [P, E])
        passed_t = sb("passed_t", [P, E])
        slot_f = sb("slot_f", [P, 8])
        TAB_ROW, TAB_PAD, TAB_LAPS, TAB_SIX = P, 2 * P, 2 * P + E, 2 * P + E + 1
        tab = sb("tab", [1, TAB_SIX + P // ROUND], I32)
        packed = sb("packed", [1, P])
        xg = over(xT[:, :, :].rearrange("p k n -> p (k n)"), [P, 2, ROW])
        xg16 = xg[:, :, 0:D].bitcast(F16)
        xgT = over(xT_then_x1T, [P, 2, 2 * KC, P], F16)
        ehT = over(xT_then_x1T, [P, 2, 2, KC, P], F16, at=2 * D)
        eh = over(queries_then_x2T, [P, 2, KC * P])
        ye = over(queries_then_x2T, [P, 2, D], at=2 * D)
        e_gate = over(w_stage, [P, 2, IM])
        meta = sb("meta", [P, 2, 2 * (E + 1)])
        ids = sb("ids", [P, 2], U32)
        fa = over(e_w16[:, :, :, :].rearrange("p e a c -> p (e a c)").bitcast(F32), [P, LAST, 2, 2, D])
        fstat = sb("fstat", [P, LAST, 2, 6])
        fmv = sb("fmv", [P, LAST, 2, 2])
        fstd = sb("fstd", [P, LAST, 2])
        frstd = sb("frstd", [P, LAST, 2])
        fshift = sb("fshift", [P, LAST, 2])

        bank = [ctx.enter_context(nc.psum_tensor(f"bank{k}", [P, 512], F32)) for k in range(8)]
        bP, bK, bN, bW, bT, bE = bank[0:2], bank[2:4], bank[4], bank[5], bank[6], bank[7]

        bKV = (bW, bN)
        bS = (bK[0], bK[1], bT)
        bX1 = (bT, bP[1], bT, bT)

        def half(b):
            return b[:, :].bitcast(F16)

        sems = {k: ctx.enter_context(nc.semaphore("s_" + k)) for k in (*PER, *ONCE_SEMS, *LAST_SEMS)}
        slot_sem = {k: [ctx.enter_context(nc.semaphore(f"s_{k}{p}")) for p in range(2)]
                    for k in SLOT_SEMS}

        def need(eng, name, i, n=None):
            eng.wait_ge(sems[name], i * PER[name] + (PER[name] if n is None else n))

        def apart(eng, sem, value):
            eng.wait_ge(sem, value)
            eng.sem_inc(sems["waits_apart"], 1)

        def bc(ap, shape):
            return ap.broadcast_to(list(shape))

        def last_sum(eng, g):
            eng.wait_ge(sems[f"f_in{g}"], 32)
            eng.tensor_tensor(fa[:, g, 0, :, :], fa[:, g, 0, :, :], fa[:, g, 1, :, :], ALU.add
                              ).then_inc(sems[f"f_sum{g % 2}"], 1)

        def pad_regions(eng, experts):
            for e in experts:
                after = eng.value_load(tab[0:1, TAB_PAD + e:TAB_PAD + e + 1], min_val=0, max_val=DUMP - P)
                eng.dma_start(xs[bass.ds(after, P), :], pad_row[:, :]).then_inc(sems["st_pad"], 16)

        def store_group(eng, i):
            need(eng, "acc_row", i)
            eng.dma_start(acc[0][bass.ts(i, GT), :].rearrange("(q p) d -> p q d", p=P), x2[:, :, :]
                          ).then_inc(sems["st_acc"], 16)

        def slot_turns(eng):
            return eng.value_load(tab[0:1, TAB_LAPS:TAB_LAPS + 1], min_val=0, max_val=P // ROUND - 1)

        def six_experts(eng, t):
            six = eng.value_load(tab[0:1, bass.ds(t + TAB_SIX, 1)], min_val=0, max_val=E ** 6 - 1)
            return [(six // E ** n) % E for n in range(6)]

        def last_experts(eng, laps):
            return [eng.value_load(tab[0:1, bass.ds(ROUND * laps + n, 1)], min_val=0, max_val=E - 1) for n in range(ROUND)]

        block = ctx.enter_context(nc.Block())

        @block.sync
        def _(sp):
            def load_xT(i):
                sp.dma_start(xT[:, :, :], t["xT"][:, :, bass.ts(i, GT)].rearrange("k p n -> p k n")
                             ).then_inc(sems["ld_xT"], 16)

            def load_group(i, later):
                if later:
                    need(sp, "xT_hi", i, 0)
                    need(sp, "xT_lo", i, 0)
                    load_xT(i)
                if later:
                    apart(sp, sems["ctx_hi"], i * PER["ctx_hi"])
                    apart(sp, sems["ctx_lo"], i * PER["ctx_lo"])
                sp.dma_start(c_stage[:, :, :], t["ctxT"][:, bass.ts(i, GB), :]).then_inc(sems["ld_ctx"], 16)
                if later:
                    need(sp, "v_hi", i, 0)
                    need(sp, "v_lo", i, 0)
                for g in range(NG):
                    r, w = (g % 2) * S, (g % 2) * (HD + 1)
                    sp.dma_start(v_stage[r:r + S, :, g // 2, w:w + HD],
                                 t["ctx"][bass.ts(i, GB), :, g * HD:(g + 1) * HD].rearrange("b t d -> t b d")
                                 ).then_inc(sems["ld_v"], 16)
                if later:
                    need(sp, "ln2_sum", i, 0)
                sp.dma_start(x_in[:, :, :], t["x"][bass.ts(i, GT), :].rearrange("(q p) d -> p q d", p=P)
                             ).then_inc(sems["ld_x"], 16)

            def place_context(i):
                apart(sp, sems["ctx_hi"], (i + 1) * PER["ctx_hi"])
                apart(sp, sems["ctx_lo"], (i + 1) * PER["ctx_lo"])
                need(sp, "st_done", i, 0)
                for to, part in ((0, 0), (C, 0), (0, 1)):
                    for g in range(NG):
                        sp.dma_start(c16[to + g * HD:to + (g + 1) * HD, part, :, g * S:(g + 1) * S],
                                     c_parts[g * HD:(g + 1) * HD, part, :, :]).then_inc(sems["ctx_in"], 16)

            def load_experts(i, ns):
                for n in ns:
                    need(sp, "w_hi", i, n)
                    need(sp, "w_lo", i, n)
                    sp.dma_start(e_stage[:, :], t["e_w"][bass.ds(i * EPG + n, 1)].rearrange("a p c -> p (a c)")
                                 ).then_inc(sems["ld_exp"], 16)

            def load_weights(n):
                a, b = W_PIECES[n]
                sp.dma_start(w_stage[:, a:b], t["w"][:, a:b]).then_inc(sems[f"ld_w{n}"], 16)

            load_xT(0)
            load_weights(0)
            sp.dma_start(cf[:, :], t["cf"]).then_inc(sems["ld_const"], 16)
            sp.dma_start(ch[:, :], t["ch"]).then_inc(sems["ld_const"], 16)
            sp.dma_start(bq_col[:, :], t["bq"]).then_inc(sems["ld_const"], 16)
            sp.dma_start(bias_rows[:, :, :].rearrange("p n d -> p (n d)"), t["biases"].partition_broadcast(P)
                         ).then_inc(sems["ld_const"], 16)
            for n in range(1, len(W_PIECES)):
                load_weights(n)
            sp.wait_ge(sems["setup"], SETUP)
            load_group(0, False)
            sp.dma_start(c16[C:C + NG, 1, :, :], t["pick"]).then_inc(sems["ld_ind"], 16)
            sp.dma_start(acc[1].rearrange("(n p) d -> p n d", p=P),
                         bc(zeros[:, :].unsqueeze(1), [P, N // P, D])).then_inc(sems["st_zero"], 16)
            with sp.Fori(0, GROUPS - 1) as i:
                load_experts(i, [0])
                place_context(i)
                load_group(i + 1, True)
                load_experts(i, range(1, EPG))
                store_group(sp, i)
            load_experts(GROUPS - 1, [0])
            place_context(GROUPS - 1)
            load_experts(GROUPS - 1, range(1, EPG - 1))
            sp.wait_ge(sems["t_pad"], 1)
            pad_regions(sp, range(0, E, 2))
            for n in range(ROUND - 1):
                sp.dma_start(xs[DUMP + n * P:DUMP + (n + 1) * P, :], pad_row[:, :]).then_inc(sems["st_pad"], 16)
            load_experts(GROUPS - 1, [EPG - 1])

            sp.wait_ge(sems["t_tab"], 1)
            laps = slot_turns(sp)
            sp.wait_ge(sems["st_pad"], 16 * (E + ROUND - 1))
            need(sp, "scattered", GROUPS - 1)
            with sp.Fori(0, 2 * laps + 2) as j:
                for p in range(2):
                    first = sp.value_load(tab[0:1, bass.ds(TAB_ROW + 2 * j + p, 1)], min_val=0,
                                          max_val=DUMP + (ROUND - 2) * P)
                    sp.wait_ge(slot_sem["xg_T"][p], j)
                    sp.wait_ge(slot_sem["meta"][p], j)
                    sp.dma_start(xg[:, p, :], xs[bass.ds(first, P), :]).then_inc(slot_sem["xg_in"][p], 16)
            def load_sums(a, pairs):
                for g in pairs:
                    sp.dma_start(fa[:, g, a, :, :], acc[a][g * 2 * P:(g + 1) * 2 * P, :].rearrange(
                        "(q p) d -> p q d", p=P)).then_inc(sems[f"f_in{g}"], 16)

            apart(sp, slot_sem["e_y"][1], 2 * laps + 2)
            apart(sp, slot_sem["e_add"][0], laps * 32 + 32)
            load_sums(0, range(2))
            apart(sp, slot_sem["e_add"][1], laps * 32 + 32)
            load_sums(1, range(2))
            for g in range(2, LAST):
                for a in range(2):
                    load_sums(a, [g])
            for g in range(LAST):
                sp.wait_ge(sems["f_out"], 2 * (g + 1))
                sp.dma_start(out[g * 2 * P:(g + 1) * 2 * P, :].rearrange("(q p) d -> p q d", p=P), fa[:, g, 0, :, :]
                             ).then_inc(sems["f_st"], 16)
            sp.wait_ge(sems["f_st"], 16 * LAST)

        @block.tensor
        def _(pe):
            def three(out, lhs, rhs, chunks):
                steps = [(w, d, k) for k in range(chunks) for w, d in THREE]
                for n, (w, d, k) in enumerate(steps):
                    last = pe.matmul(out, lhs(w, d, k), rhs(w, d, k), start=n == 0, stop=n == len(steps) - 1)
                return last

            def q_projection(i):
                need(pe, "xT_hi", i)
                need(pe, "xT_lo", i)
                for c in range(KC):
                    if c == 0:
                        need(pe, "r_chain", i, 0)
                    else:
                        need(pe, "h_mul", i, 0)
                    three(bP[c][:, :], lambda w, d, k: weight("q", w, k, c * P, P),
                          lambda w, d, k: xT16[:, d, k, :], KC).then_inc(sems["q_proj"], 1)

            def kv_projection(i, q):
                if q == 0:
                    need(pe, "acc_row", i, 0)
                elif q == 1:
                    need(pe, "h_mul", i, 0)
                else:
                    need(pe, "kv_read", i, 2 * (q - 1))
                three(bKV[q % 2][:, :], lambda w, d, k: xT16[:, d, k, q * P:(q + 1) * P],
                      lambda w, d, k: weight("kv", w, k, 0, 2 * D), KC).then_inc(sems["kv_proj"], 1)

            def kv_state(i, b):
                if b == 0:
                    pe.wait_ge(sems["ws_hi"], len(W_PIECES))
                    pe.wait_ge(sems["ws_lo"], len(W_PIECES))
                q, r = b // 2, (b % 2) * S
                need(pe, "k_relu", i, q + 1)
                need(pe, "kv_read", i, 2 * (q + 1))
                if b < 2:
                    need(pe, "h_mul", i, 0)
                elif b == 2:
                    need(pe, "acc_row", i, 0)
                else:
                    need(pe, "kv_masked", i, 2 * (b - 2))
                for c in range(KC):
                    last = pe.matmul(bS[b % 3][:, c * (P + 1):(c + 1) * (P + 1)], kb[r:r + S, q, c * P:(c + 1) * P],
                                     vb[r:r + S, q, c, :], start=True, stop=True)
                last.then_inc(sems["kv_state"], 1)

            def attention(i, b):
                q, r = b // 2, (b % 2) * S
                need(pe, "kv_masked", i, 2 * (b + 1))
                if b == 0:
                    need(pe, "q_relu", i)
                    need(pe, "kv_read", i)
                    need(pe, "r_chain", i, 0)
                if b % 2 == 0 and b >= 4:
                    need(pe, "attn_div", i, q - 1)
                for c in range(KC):
                    last = pe.matmul((bN, bE)[q % 2][r:r + S, c * AW:(c + 1) * AW], qd[:, c, b * S:(b + 1) * S],
                                     kv_m[:, b % 3, c, :], start=True, stop=True)
                last.then_inc(sems["attn_nd"], 1)

            def attention_transposes(i, q):
                need(pe, "attn_div", i, q + 1)
                if q == 0:
                    need(pe, "q_relu", i)
                if q >= 2:
                    need(pe, "attn_lo", i, q - 1)
                for c in range(KC):
                    last = pe.transpose(bP[q % 2][:, c * P:(c + 1) * P], a32[:, q % 2, c * P:(c + 1) * P], ident)
                last.then_inc(sems["attn_T"], 1)

            def attention_out(i, q):
                need(pe, "attn_hi", i, q + 1)
                need(pe, "attn_lo", i, q + 1)
                if q == 0:
                    need(pe, "kv_read", i)
                else:
                    need(pe, "ln1_sum", i, q)
                three(bW[:, 0:D], lambda w, d, k: a16[:, q % 2, d, k, :],
                      lambda w, d, k: weight("o", w, k, 0, D), KC).then_inc(sems["wo_done"], 1)

            def x1_transposes(i, q):
                if q == 0:
                    need(pe, "acc_row", i, 0)
                elif q == 1:
                    need(pe, "attn_lo", i)
                else:
                    need(pe, "x1T_lo", i, 2 * q - 3)
                apart(pe, sems["x1_norm"], i * PER["x1_norm"] + q + 1)
                for h in range(HPG):
                    last = pe.transpose(bX1[q][0:C, h * P:(h + 1) * P], x1[:, q, h * C:(h + 1) * C], ident)
                last.then_inc(sems["x1T"], 1)

            def scores(i, b):
                q = b // 2
                need(pe, "x1T_hi", i, q + 1)
                if b == 0:
                    need(pe, "ctx_in", i)
                if b < 2:
                    need(pe, "kv_masked", i)
                else:
                    need(pe, "s_max", i, b - 1)
                for hp in range(2):
                    last = pe.matmul(bK[b % 2][:, hp * NG * S:(hp + 1) * NG * S],
                                     xh[0:C, 0, q, b % 2, hp * P:(hp + 1) * P], c16[0:C, 0, b, :],
                                     start=True, stop=True)
                last.then_inc(sems["s_done"], 1)

            def max_transposes(i, b):
                need(pe, "s_max", i, b + 1)
                if b == 0:
                    need(pe, "attn_lo", i)
                else:
                    need(pe, "m_copied", i, b)
                for hp in range(2):
                    last = pe.transpose(half(bP[0])[0:NG, hp * P:(hp + 1) * P], m16[:, b % 2, hp * NG:(hp + 1) * NG], id16)
                last.then_inc(sems["m_T"], 1)

            def scores_T(i, b):
                q = b // 2
                need(pe, "m_copied", i, b + 1)
                need(pe, "x1T_lo", i, q + 1)
                need(pe, "x1T_again", i, q + 1)
                if b == 0:
                    pe.wait_ge(sems["ld_ind"], 16)
                    need(pe, "attn_div", i)
                else:
                    need(pe, "exp_done", i, b)
                for gp in range(2):
                    for part, rows in ((0, P), (1, C + NG)):
                        last = pe.matmul(bE[:, gp * HPG * S:(gp + 1) * HPG * S], c16[0:rows, part, b, gp * P:(gp + 1) * P],
                                         xh[0:rows, part, q, b % 2, :], start=part == 0, stop=part == 1)
                last.then_inc(sems["st_done"], 1)

            def values(i, b):
                need(pe, "e_hi", i, b + 1)
                need(pe, "e_lo", i, b + 1)
                if b == 0:
                    need(pe, "v_hi", i)
                    need(pe, "v_lo", i)
                    need(pe, "attn_div", i)
                    need(pe, "attn_lo", i)
                if b >= 2:
                    need(pe, "pv_norm", i, b - 1)
                for hp in range(2):
                    for gp in range(2):
                        a = (hp * 2 + gp) * VW
                        last = three((bN, bP[1])[b % 2][:, a:a + VW],
                                     lambda w, d, k: e16[:, b % 2, d, gp, hp * P:(hp + 1) * P],
                                     lambda w, d, k: v16[:, w, b, gp, :], 1)
                last.then_inc(sems["pv_done"], 1)

            def a_transposes(i, q):
                need(pe, "pv_norm", i, 2 * (q + 1))
                if q == 0:
                    need(pe, "x1T_lo", i)
                else:
                    need(pe, "aT_lo", i, q)
                for b in range(2):
                    last = pe.transpose(bT[:, b * P:(b + 1) * P], a2[:, 2 * q + b, :], ident)
                last.then_inc(sems["aT"], 1)

            def cross_out(i, q):
                need(pe, "aT_hi", i, q + 1)
                need(pe, "aT_lo", i, q + 1)
                if q == 0:
                    need(pe, "ln1_sum", i)
                else:
                    need(pe, "ln2_sum", i, q)
                three(bW[:, 0:D], lambda w, d, k: aT16[:, q % 2, d, k, :],
                      lambda w, d, k: weight("c", w, k, 0, D), KC).then_inc(sems["wc_done"], 1)

            def x2_transposes(i, q):
                need(pe, "row_hi", i, q + 1)
                need(pe, "row_lo", i, q + 1)
                if q < 2:
                    need(pe, "aT_lo", i)
                    need(pe, "ln2_sum", i)
                else:
                    need(pe, "x2T_read", i, q - 1)
                for a in range(2 * KC):
                    last = pe.transpose(half((bT, bW)[q % 2])[:, a * P:(a + 1) * P], row16[:, q, a * P:(a + 1) * P], id16)
                last.then_inc(sems["x2T"], 1)

            def router(i):
                need(pe, "m_copied", i)
                need(pe, "x2T_read", i)
                for q in range(TQ):
                    last = three(bP[0][:, q * (E + 1):(q + 1) * (E + 1)],
                                 lambda w, d, k: x2T16[:, d, k, q * P:(q + 1) * P],
                                 lambda w, d, k: weight("r", w, k, 0, E + 1), KC)
                last.then_inc(sems["router"], 1)

            def ranks(i):
                need(pe, "r_chain", i, R_MASK)
                need(pe, "exp_done", i)
                flat = mask16[:, :, :].rearrange("p q e -> p (q e)")
                pe.matmul(bE[:, 0:(TQ + 1) * E], tri16, flat, start=True, stop=False, skip_group_check=True)
                for q in range(TQ):
                    last = pe.matmul(bE[:, (q + 1) * E:(TQ + 1) * E].rearrange("p (q e) -> p q e", e=E), ones16,
                                     bc(mask16[:, q:q + 1, :], [P, TQ - q, E]), start=False, stop=q == TQ - 1,
                                     skip_group_check=True)
                last.then_inc(sems["rank"], 1)

            def shared_up(i, c):
                bg, bu = ((bK[0], bK[1]), (bP[1], bN))[c % 2]
                if c < 2:
                    need(pe, "s_max", i)
                    need(pe, "pv_norm", i)
                else:
                    need(pe, "h_mul", i, c - 1)
                if c < IC - 1:
                    for half_, b_, name in ((0, bg, "g_done"), (1, bu, "u_done")):
                        three(b_[:, :], lambda w, d, k: weight("gu", w, k, half_ * FULL + c * P, P),
                              lambda w, d, k: x2T16[:, d, k, :], KC).then_inc(sems[name], 1)
                else:
                    three(bg[:, :], lambda w, d, k: weight("gu", w, k, 2 * FULL, P),
                          lambda w, d, k: x2T16[:, d, k, :], KC).then_inc(sems["g_done"], 1)

            def shared_down(i, q, chunks=range(IC)):
                if chunks[0] == 0 and q < 2:
                    need(pe, "ln2_sum", i)
                    need(pe, "x2T_read", i)
                elif chunks[0] == 0:
                    need(pe, "acc_row", i, q - 1)
                need(pe, "h_hi", i, chunks[-1] + 1)
                need(pe, "h_lo", i, chunks[-1] + 1)
                for c in chunks:
                    for w, d in THREE:
                        r = chunk_rows(c)
                        last = pe.matmul((bW, bT)[q % 2][:, 0:D], h16[0:r, d, c, q * P:(q + 1) * P],
                                         weight("dn", w, c, 0, D)[0:r], start=c == 0 and (w, d) == THREE[0],
                                         stop=c == IC - 1 and (w, d) == THREE[-1])
                if chunks[-1] == IC - 1:
                    last.then_inc(sems["down"], 1)

            pe.wait_ge(sems["ld_const"], 64)
            pe.wait_ge(sems["ws_hi"], 1)
            pe.wait_ge(sems["ws_lo"], 1)
            pe.wait_ge(sems["setup"], SETUP)
            def group_pass(i, last):
                q_projection(i)
                for q in range(TQ):
                    kv_projection(i, q)
                for b in range(GB + 3):
                    if b == 0:
                        kv_state(i, 0)
                    if b < GB - 1:
                        kv_state(i, b + 1)
                    if 1 <= b <= GB:
                        attention(i, b - 1)
                    if b == GB:
                        x1_transposes(i, 0)
                    if b >= 3 and b % 2:
                        attention_transposes(i, (b - 3) // 2)
                    if b >= 4 and b % 2 == 0:
                        attention_out(i, b // 2 - 2)
                    if b == GB + 1:
                        scores(i, 0)
                        scores(i, 1)
                x1_transposes(i, 1)
                max_transposes(i, 0)
                x1_transposes(i, 2)
                for step in range(2, GB + 6):
                    if step == 3:
                        x1_transposes(i, 3)
                    if step < GB:
                        scores(i, step)
                    if 1 <= step <= GB:
                        max_transposes(i, step - 1)
                    if 2 <= step < GB + 2:
                        scores_T(i, step - 2)
                    if 4 <= step < GB + 4:
                        values(i, step - 4)
                    if step >= 6 and step % 2 == 0:
                        a_transposes(i, (step - 6) // 2)
                    if step >= 7 and step % 2:
                        cross_out(i, (step - 7) // 2)
                for q in range(TQ):
                    x2_transposes(i, q)
                router(i)
                for c in range(IC):
                    shared_up(i, c)
                    if c == 1:
                        ranks(i)
                for chunks in (range(IC - 2), range(IC - 2, IC)):
                    for q in range(2):
                        shared_down(i, q, chunks)
                if last:
                    pe.wait_ge(sems["t_chain"], T_CHAIN)
                    for n in range(2):
                        turned = pe.transpose(bP[0][0:1, n * P:(n + 1) * P], slot_f[:, n:n + 1], ident)
                    turned.then_inc(sems["t_rows"], 1)
                for q in range(2, TQ):
                    shared_down(i, q)

            with pe.Fori(0, GROUPS - 1) as i:
                group_pass(i, False)
            group_pass(GROUPS - 1, True)

            def slot_transposes(j, p):
                pe.wait_ge(slot_sem["xg_in"][p], 16 * (j + 1))
                pe.wait_ge(slot_sem["xg_read"][p], j)
                for a in range(2 * KC):
                    last = pe.transpose(half((bT, bE)[p])[:, a * P:(a + 1) * P], xg16[:, p, a * P:(a + 1) * P], id16)
                last.then_inc(slot_sem["xg_T"][p], 1)

            def slot_up(j, p, e):
                pe.wait_ge(slot_sem["xg_read"][p], j + 1)
                pe.wait_ge(slot_sem["e_mul"][p], j)
                three(bP[p][:, 0:2 * IM], lambda w, d, k: xgT[:, p, d * KC + k, :],
                      lambda w, d, k: e_w16[:, bass.ds(e, 1), w, k * 2 * IM:(k + 1) * 2 * IM].rearrange("p a n -> p (a n)"),
                      KC).then_inc(slot_sem["e_gu"][p], 1)

            def slot_h_transposes(j, p):
                pe.wait_ge(slot_sem["e_mul"][p], j + 1)
                pe.wait_ge(slot_sem["e_hlo"][p], j)
                for k in range(KC):
                    last = pe.transpose(bK[p][:, k * P:(k + 1) * P], eh[:, p, k * P:(k + 1) * P], ident)
                last.then_inc(slot_sem["e_hT"][p], 1)

            def slot_down(j, p, e):
                pe.wait_ge(slot_sem["e_hhi"][p], j + 1)
                pe.wait_ge(slot_sem["e_hlo"][p], j + 1)
                pe.wait_ge(slot_sem["e_yw"][p], j)
                three((bN, bW)[p][:, 0:D], lambda w, d, k: ehT[:, p, d, k, :],
                      lambda w, d, k: e_w16[:, bass.ds(e, 1), w, EG + k * D:EG + (k + 1) * D].rearrange("p a n -> p (a n)"),
                      KC).then_inc(slot_sem["e_y"][p], 1)

            pe.wait_ge(sems["t_tab"], 1)
            need(pe, "acc_row", GROUPS - 1)
            need(pe, "w_hi", GROUPS - 1)
            need(pe, "w_lo", GROUPS - 1)
            laps = slot_turns(pe)
            e = [pe.value_load(tab[0:1, p:p + 1], min_val=0, max_val=E - 1) for p in range(2)]
            slot_transposes(0, 0)
            slot_up(0, 0, e[0])
            slot_transposes(0, 1)
            slot_h_transposes(0, 0)
            slot_up(0, 1, e[1])

            def next_pair(j, e):
                slot_down(j, 0, e[0])
                slot_h_transposes(j, 1)
                slot_up(j + 1, 0, e[2])
                slot_transposes(j + 1, 1)
                slot_down(j, 1, e[1])
                slot_h_transposes(j + 1, 0)
                slot_up(j + 1, 1, e[3])

            with pe.Fori(0, laps) as turn:
                slot_transposes(2 * turn + 1, 0)
                e = six_experts(pe, turn)
                next_pair(2 * turn, e[0:4])
                slot_transposes(2 * turn + 2, 0)
                next_pair(2 * turn + 1, e[2:6])
            slot_transposes(2 * laps + 1, 0)
            e = last_experts(pe, laps)
            next_pair(2 * laps, e)
            slot_down(2 * laps + 1, 0, e[2])
            slot_h_transposes(2 * laps + 1, 1)
            slot_down(2 * laps + 1, 1, e[3])

        @block.scalar
        def _(act):
            def split_expert(i, n):
                act.wait_ge(sems["ld_exp"], i * PER["ld_exp"] + 16 * (n + 1))
                act.activation(e_w16[:, bass.ds(i * EPG + n, 1), 0, :].rearrange("p a c -> p (a c)"),
                               e_stage[:, :], ACT.Copy, scale=W_SCALE).then_inc(sems["w_hi"], 1)

            def input_hi(i):
                need(act, "ld_xT", i)
                need(act, "st_done", i, 0)
                act.activation(xT16[:, 0, :, :], xT[:, :, :], ACT.Copy).then_inc(sems["xT_hi"], 1)

            def context_hi(i):
                need(act, "ld_ctx", i)
                need(act, "ctx_in", i, 0)
                act.activation(c_parts[:, 0, :, :], c_stage[:, :, :], ACT.Copy).then_inc(sems["ctx_hi"], 1)
                need(act, "ld_v", i)
                need(act, "pv_done", i, 0)
                act.activation(v16[:, 0, :, :, :], v_stage[:, :, :, :], ACT.Copy).then_inc(sems["v_hi"], 1)

            input_hi(0)
            for n, (a, b) in enumerate(W_PIECES):
                act.wait_ge(sems[f"ld_w{n}"], 16)
                act.activation(w16[:, 0, a:b], w_stage[:, a:b], ACT.Copy, scale=W_SCALE).then_inc(sems["ws_hi"], 1)
            context_hi(0)
            act.wait_ge(sems["ld_const"], 64)

            def group_pass(i, last):
                for c in range(KC):
                    need(act, "q_proj", i, c + 1)
                    if c == 0:
                        need(act, "attn_nd", i, 0)
                    act.activation(qd[:, c, :], bP[c][:, :], ACT.Relu, bias=bq_col[:, c:c + 1], scale=W_BACK
                                   ).then_inc(sems["q_relu"], 1)
                for q in range(TQ):
                    need(act, "kv_read", i, 2 * q + 1)
                    act.activation(kb[:, q, :], kb[:, q, :], ACT.Relu, scale=const("decay_col")
                                   ).then_inc(sems["k_relu"], 1)
                def attention_hi(q):
                    need(act, "attn_T", i, q + 1)
                    need(act, "wo_done", i, max(q - 1, 0))
                    act.activation(a16[:, q % 2, 0, :, :], bP[q % 2][:, 0:D].rearrange("p (c n) -> p c n", c=KC),
                                   ACT.Copy).then_inc(sems["attn_hi"], 1)

                def first_deviation(q):
                    need(act, "ln1_mv", i, q + 1)
                    act.activation(std1[:, q:q + 1], mv1[:, q, 1:2], ACT.Sqrt, bias=const("ln_eps")
                                   ).then_inc(sems["ln1_std"], 1)

                def maxima(b):
                    need(act, "m_T", i, b + 1)
                    act.activation(xh[C:C + NG, 1, b // 2, b % 2, :], half(bP[0])[0:NG, 0:HPG * S], ACT.Copy,
                                   scale=-1.0).then_inc(sems["m_copied"], 1)

                def x1T_hi(q):
                    need(act, "x1T", i, q + 1)
                    if q == 0:
                        need(act, "st_done", i, 0)
                    act.activation(xh[0:C, 0, q, :, :].rearrange("p b (h s) -> p h b s", h=HPG),
                                   bX1[q][0:C, :].rearrange("p (h b s) -> p h b s", h=HPG, b=2), ACT.Copy
                                   ).then_inc(sems["x1T_hi"], 1)

                def deviation(a, b):
                    need(act, "ln2_mv", i, b)
                    act.activation(std2[:, a:b], mv2[:, a:b, 1], ACT.Sqrt, bias=const("ln_eps")
                                   ).then_inc(sems["ln2_std"], 1)

                def row_hi(q):
                    need(act, "x2_norm", i, q + 1)
                    if q == 0:
                        need(act, "scattered", i, 0)
                        need(act, "x2T", i, 0)
                    act.activation(row16[:, q, 0:D], x2[:, q, :], ACT.Copy).then_inc(sems["row_hi"], 1)

                attention_hi(0)
                attention_hi(1)
                first_deviation(0)
                attention_hi(2)
                first_deviation(1)
                x1T_hi(0)
                attention_hi(3)
                first_deviation(2)
                x1T_hi(1)
                maxima(0)
                first_deviation(3)
                x1T_hi(2)
                for step in range(2, GB + 6):
                    if step == 3:
                        x1T_hi(3)
                    if step <= GB:
                        maxima(step - 1)
                    if 2 <= step < GB + 2:
                        b = step - 2
                        need(act, "st_done", i, b + 1)
                        if b >= 2:
                            need(act, "e_lo", i, b - 1)
                        act.activation(e32[:, b % 2, :, :], bE[:, :].rearrange("p (g n) -> p g n", g=2), ACT.Exp,
                                       scale=HD ** -0.5).then_inc(sems["exp_done"], 1)
                        need(act, "exp_done", i, b + 1)
                        if b >= 2:
                            need(act, "pv_done", i, b - 1)
                        act.activation(e16[:, b % 2, 0, :, :], e32[:, b % 2, :, :], ACT.Copy).then_inc(sems["e_hi"], 1)
                    if step >= 6 and step % 2 == 0:
                        q = (step - 6) // 2
                        need(act, "aT", i, q + 1)
                        need(act, "wc_done", i, max(q - 1, 0))
                        act.activation(aT16[:, q % 2, 0, :, :].rearrange("p e (b s) -> p b e s", b=2),
                                       bT[:, 0:D].rearrange("p (b e s) -> p b e s", b=2, e=2), ACT.Copy
                                       ).then_inc(sems["aT_hi"], 1)
                    if step == 10:
                        deviation(0, 2)
                    if step == 12:
                        deviation(2, 3)
                        row_hi(0)
                        row_hi(1)
                deviation(TQ - 1, TQ)
                for q in range(2, TQ):
                    row_hi(q)
                split_expert(i, 0)
                need(act, "r_chain", i, R_SHIFT)
                act.activation(ex[:, :, :], shifted[:, :, :], ACT.Exp).then_inc(sems["r_exp"], 1)
                act.activation(sg_e[:, :], lg[:, :, E], ACT.Exp, scale=-1.0).then_inc(sems["r_exp"], 1)
                for c in range(IC + 1):
                    if c < IC:
                        n = chunk_rows(c)
                        need(act, "g_done", i, c + 1)
                        if c == 0:
                            need(act, "e_hi", i)
                            need(act, "e_lo", i)
                        if c >= 2:
                            need(act, "h_mul", i, c - 1)
                        to = slice(0, n) if c < IC - 1 else slice(n, 2 * n)
                        act.activation(gate[to, c % 2, :], (bK[0], bP[1])[c % 2][0:n, :], ACT.Silu, scale=W_BACK
                                       ).then_inc(sems["silu"], 1)
                        if c == 0 and not last:
                            context_hi(i + 1)
                    if c >= 1:
                        n = chunk_rows(c - 1)
                        need(act, "h_mul", i, c)
                        if c == 1:
                            need(act, "down", i, 0)
                        act.activation(h16[0:n, 0, c - 1, :], h32[0:n, (c - 1) % 2, :], ACT.Copy
                                       ).then_inc(sems["h_hi"], 1)
                    if c == 1:
                        split_expert(i, 1)
                    if c == 3 and not last:
                        input_hi(i + 1)
                    if 3 <= c and last:
                        if c == 3:
                            act.wait_ge(sems["t_pad"], 1)
                        pad_regions(act, range(4 * (c - 3) + 1, 4 * (c - 2), 2))
                split_expert(i, 2)
                split_expert(i, 3)
                if last:
                    store_group(act, i)

            with act.Fori(0, GROUPS - 1) as i:
                group_pass(i, False)
            group_pass(GROUPS - 1, True)

            def slot_silu(j, p):
                act.wait_ge(slot_sem["e_gu"][p], j + 1)
                act.wait_ge(slot_sem["e_mul"][p], j)
                act.activation(e_gate[:, p, :], bP[p][:, 0:IM], ACT.Silu, scale=W_BACK).then_inc(slot_sem["e_silu"][p], 1)

            def slot_h_hi(j, p):
                act.wait_ge(slot_sem["e_hT"][p], j + 1)
                act.wait_ge(slot_sem["e_y"][p], j)
                act.activation(ehT[:, p, 0, :, :], bK[p][:, 0:KC * P].rearrange("p (k n) -> p k n", k=KC), ACT.Copy
                               ).then_inc(slot_sem["e_hhi"][p], 1)

            def slot_weighted(j, p, e, place):
                act.wait_ge(slot_sem["e_y"][p], j + 1)
                act.wait_ge(slot_sem["meta"][p], j + 1)
                act.wait_ge(slot_sem["e_add"][p], 16 * j)
                act.activation(ye[:, p, :], (bN, bW)[p][:, 0:D], ACT.Copy,
                               scale=meta[:, p, bass.ds(place * (E + 1) + e, 1)]
                               ).then_inc(slot_sem["e_yw"][p], 1)

            act.wait_ge(sems["t_tab"], 1)
            laps = slot_turns(act)
            slot_silu(0, 0)
            slot_h_hi(0, 0)
            slot_silu(0, 1)

            def next_pair(j, e, place):
                slot_h_hi(j, 1)
                slot_weighted(j, 0, e[0], place)
                slot_silu(j + 1, 0)
                slot_h_hi(j + 1, 0)
                slot_weighted(j, 1, e[1], place)
                slot_silu(j + 1, 1)

            with act.Fori(0, laps) as turn:
                e = six_experts(act, turn)
                next_pair(2 * turn, e[0:2], 0)
                next_pair(2 * turn + 1, e[2:4], 1)
            e = last_experts(act, laps)
            next_pair(2 * laps, e[0:2], 0)
            slot_h_hi(2 * laps + 1, 1)
            slot_weighted(2 * laps + 1, 0, e[2], 1)
            slot_weighted(2 * laps + 1, 1, e[3], 1)
            for g in range(LAST + 1):
                if g < LAST:
                    act.wait_ge(sems["f_mv"], 2 * (g + 1))
                    act.activation(fstd[:, g, :], fmv[:, g, :, 1], ACT.Sqrt, bias=const("ln_eps")
                                   ).then_inc(sems["f_std"], 1)
                if g >= 1:
                    act.wait_ge(sems["f_rstd"], 2 * g)
                    for q in range(2):
                        act.activation(fa[:, g - 1, 0, q, :], fa[:, g - 1, 0, q, :], ACT.Identity,
                                       bias=fshift[:, g - 1, q:q + 1], scale=frstd[:, g - 1, q:q + 1]
                                       ).then_inc(sems["f_out"], 1)

        @block.vector
        def _(dve):
            def input_lo(i):
                need(dve, "xT_hi", i)
                dve.tensor_tensor(xT16[:, 1, :, :], xT[:, :, :], xT16[:, 0, :, :], ALU.subtract).then_inc(sems["xT_lo"], 1)

            def split_weights(n):
                a, b = W_PIECES[n]
                dve.wait_ge(sems["ws_hi"], n + 1)
                dve.scalar_tensor_tensor(w16[:, 1, a:b], w_stage[:, a:b], W_SCALE, w16[:, 0, a:b], ALU.mult,
                                         ALU.subtract).then_inc(sems["ws_lo"], 1)

            dve.memset(vb[:, :, :, P:P + 1], 1.0).then_inc(sems["setup"], 1)
            dve.memset(mask16[:, TQ, :], 0.0).then_inc(sems["setup"], 1)
            input_lo(0)
            split_weights(0)
            dve.wait_ge(sems["ld_const"], 64)
            dve.tensor_copy(token[:, :], const("token")).then_inc(sems["setup"], 1)
            dve.tensor_copy(count[:, :], const("region")).then_inc(sems["setup"], 1)
            dve.wait_ge(sems["setup"], SETUP)
            for n in range(1, len(W_PIECES)):
                split_weights(n)

            def split_expert(i, n):
                need(dve, "w_hi", i, n + 1)
                w = e_w16[:, bass.ds(i * EPG + n, 1), :, :].rearrange("p a s c -> p (a s) c")
                dve.scalar_tensor_tensor(w[:, 1, :], e_stage[:, :], W_SCALE, w[:, 0, :], ALU.mult,
                                         ALU.subtract).then_inc(sems["w_lo"], 1)

            def norm_stats(i, q, ln, total, stat, mv):
                need(dve, f"{ln}_sum", i, q + 1)
                dve.bn_stats(stat[:, q, :], total[:, q, :]).then_inc(sems[f"{ln}_stat"], 1)
                apart(dve, sems[f"{ln}_stat"], i * PER[f"{ln}_stat"] + q + 1)
                dve.bn_aggr(mv[:, q, :], stat[:, q, :]).then_inc(sems[f"{ln}_mv"], 1)

            tdone = [0]

            def tlink(instruction):
                tdone[0] += 1
                instruction.then_inc(sems["t_chain"], 1)
                dve.wait_ge(sems["t_chain"], tdone[0])

            def expert_tiles():
                tlink(dve.tensor_tensor(passed[:, :], count[:, :], const("region"), ALU.subtract))
                tlink(dve.tensor_tensor(more[:, :, :], bc(passed[:, :].unsqueeze(2), [P, E, E]),
                                        bc(const("steps").unsqueeze(1), [P, E, E]), ALU.is_gt))
                tlink(dve.tensor_reduce(tiles[:, :], more[:, :, :], AX, ALU.add))
                tlink(dve.tensor_tensor(tiles_to[:, :, :], bc(tiles[:, :].unsqueeze(1), [P, E, E]),
                                        const("upto").rearrange("p (a b) -> p a b", a=E), ALU.mult))
                tlink(dve.tensor_reduce(cum[:, :], tiles_to[:, :, :], AX, ALU.add))

            def slot_experts():
                tlink(dve.tensor_scalar(passed[:, :], cum[:, :], const("slot"), None, ALU.is_le))
                tlink(dve.tensor_tensor(passed_t[:, :], passed[:, :], tiles[:, :], ALU.mult))
                tlink(dve.tensor_reduce(slot_f[:, 2:3], passed[:, :], AX, ALU.add))
                tlink(dve.tensor_reduce(slot_f[:, 3:4], passed_t[:, :], AX, ALU.add))
                tlink(dve.tensor_scalar(slot_f[:, 0:1], slot_f[:, 2:3], float(E - 1), None, ALU.min))

            def slot_rows():
                tlink(dve.tensor_tensor(slot_f[:, 4:5], const("slot"), slot_f[:, 3:4], ALU.subtract))
                tlink(dve.tensor_scalar(slot_f[:, 5:6], slot_f[:, 4:5], float(P), None, ALU.mult))
                tlink(dve.scalar_tensor_tensor(slot_f[:, 1:2], slot_f[:, 2:3], float(REGION), slot_f[:, 5:6], ALU.mult,
                                               ALU.add))
                tlink(dve.tensor_scalar(more_rounds[:, :], const("rounds"), cum[:, E - 1:E], None, ALU.is_lt))
                tlink(dve.tensor_reduce(slot_f[:, 7:8], more_rounds[:, :], AX, ALU.add))
                tlink(dve.tensor_copy(tab[0:1, TAB_LAPS:TAB_LAPS + 1], slot_f[0:1, 7:8]))
                assert tdone[0] == T_CHAIN

            def slot_table():
                dve.wait_ge(sems["t_rows"], 1)
                dve.tensor_copy(tab[0:1, 0:2 * P], bP[0][0:1, 0:2 * P]).then_inc(sems["t_packed"], 1)
                dve.wait_ge(sems["t_packed"], 1)
                experts = tab[0:1, 0:P].rearrange("a (j p) -> a j p", p=2)
                pairs = packed[0:1, 0:P // 2].rearrange("a (t p) -> a t p", p=2)
                fours = packed[0:1, P // 2:P // 2 + P // ROUND].unsqueeze(2)
                dve.scalar_tensor_tensor(packed[0:1, 0:P // 2].unsqueeze(2), experts[:, :, 1:2], float(E),
                                         experts[:, :, 0:1], ALU.mult, ALU.add).then_inc(sems["t_packed"], 1)
                dve.wait_ge(sems["t_packed"], 2)
                dve.scalar_tensor_tensor(fours, pairs[:, :, 1:2], float(E ** 2), pairs[:, :, 0:1], ALU.mult, ALU.add
                                         ).then_inc(sems["t_packed"], 1)
                dve.wait_ge(sems["t_packed"], 3)
                turns = P // ROUND - 1
                dve.scalar_tensor_tensor(tab[0:1, TAB_SIX:TAB_SIX + turns].unsqueeze(2), pairs[:, 1:turns + 1, 0:1],
                                         float(E ** 4), fours[:, 0:turns], ALU.mult, ALU.add).then_inc(sems["t_tab"], 1)

            def group_pass(i, last):
                for q in range(TQ):
                    need(dve, "kv_proj", i, q + 1)
                    if q == 0:
                        need(dve, "kv_state", i, 0)
                    keys, vals = bKV[q % 2][:, 0:D], bKV[q % 2][:, D:2 * D]
                    dve.scalar_tensor_tensor(kb[:, q, :], keys, W_BACK, bk_row, ALU.mult, ALU.add
                                             ).then_inc(sems["kv_read"], 1)
                    dve.scalar_tensor_tensor(vb[:, q, :, 0:P], vals.rearrange("p (c n) -> p c n", c=KC), W_BACK,
                                             bv_row.rearrange("p (c n) -> p c n", c=KC), ALU.mult, ALU.add
                                             ).then_inc(sems["kv_read"], 1)

                def state_masks(b):
                    need(dve, "kv_state", i, b + 1)
                    if b >= 3:
                        need(dve, "attn_nd", i, b - 2)
                    st = bS[b % 3][:, 0:KC * (P + 1)].rearrange("p (c n) -> p c n", c=KC)
                    blocks = bc(head_mask.unsqueeze(1), [P, KC, P])
                    dve.tensor_tensor(kv_m[:, b % 3, :, 0:P], st[:, :, 0:P], blocks, ALU.mult
                                      ).then_inc(sems["kv_masked"], 1)
                    dve.tensor_tensor(kv_m[:, b % 3, :, P:AW], bc(st[:, :, P:P + 1], [P, KC, AW - P]),
                                      bc(const("head_pick").unsqueeze(1), [P, KC, AW - P]), ALU.mult
                                      ).then_inc(sems["kv_masked"], 1)

                def attention_rows(q):
                    both = (bN, bE)[q % 2][:, 0:KC * AW].rearrange("p (c n) -> p c n", c=KC)
                    need(dve, "attn_nd", i, 2 * (q + 1))
                    dve.tensor_scalar(den[:, q % 2, :, :], both[:, :, P:AW], const("attn_eps"), None, ALU.add
                                      ).then_inc(sems["attn_den"], 1)
                    need(dve, "attn_den", i, q + 1)
                    dve.reciprocal(den[:, q % 2, :, :], den[:, q % 2, :, :]).then_inc(sems["attn_rec"], 1)
                    need(dve, "attn_rec", i, q + 1)
                    if q >= 2:
                        need(dve, "attn_T", i, q - 1)
                    for c in range(KC):
                        last = dve.tensor_tensor(a32[:, q % 2, c * P:(c + 1) * P].rearrange("p (h d) -> p h d", d=HD),
                                                 both[:, c, 0:P].rearrange("p (h d) -> p h d", d=HD),
                                                 bc(den[:, q % 2, c, :].unsqueeze(2), [P, P // HD, HD]), ALU.mult)
                    last.then_inc(sems["attn_div"], 1)

                def attention_lo(q):
                    need(dve, "attn_hi", i, q + 1)
                    if q >= 2:
                        need(dve, "wo_done", i, q - 1)
                    dve.tensor_tensor(a16[:, q % 2, 1, :, :], bP[q % 2][:, 0:D].rearrange("p (c n) -> p c n", c=KC),
                                      a16[:, q % 2, 0, :, :], ALU.subtract).then_inc(sems["attn_lo"], 1)

                def first_norm(q):
                    need(dve, "wo_done", i, q + 1)
                    if q == 0:
                        need(dve, "x_bo", i)
                        need(dve, "x1T", i, 0)
                        need(dve, "x1_bc", i, 0)
                    dve.scalar_tensor_tensor(x1[:, q, :], bW[:, 0:D], W_BACK, x_in[:, q, :], ALU.mult, ALU.add
                                             ).then_inc(sems["ln1_sum"], 1)
                    norm_stats(i, q, "ln1", x1, stat1, mv1)

                def first_normed(q):
                    need(dve, "ln1_std", i, q + 1)
                    dve.reciprocal(rstd1[:, q:q + 1], std1[:, q:q + 1]).then_inc(sems["ln1_rstd"], 1)
                    need(dve, "ln1_rstd", i, q + 1)
                    dve.tensor_scalar(x1[:, q, :], x1[:, q, :], mv1[:, q, 0:1], rstd1[:, q:q + 1], ALU.subtract,
                                      ALU.mult).then_inc(sems["x1_norm"], 1)

                def x1T_lo(q):
                    need(dve, "x1T_hi", i, q + 1)
                    if q == 0:
                        need(dve, "st_done", i, 0)
                    dve.tensor_tensor(xh[C:P, 0, q, :, :].rearrange("p b (h s) -> p h b s", h=HPG),
                                      bX1[q][0:C, :].rearrange("p (h b s) -> p h b s", h=HPG, b=2),
                                      xh[0:C, 0, q, :, :].rearrange("p b (h s) -> p h b s", h=HPG), ALU.subtract
                                      ).then_inc(sems["x1T_lo"], 1)
                    dve.tensor_copy(xh[0:C, 1, q, :, :], xh[0:C, 0, q, :, :]).then_inc(sems["x1T_again"], 1)

                def score_maxima(b):
                    need(dve, "s_done", i, b + 1)
                    if b >= 2:
                        need(dve, "m_T", i, b - 1)
                    with nc.allow_low_precision("any value near the maximum guards the softmax"):
                        dve.tensor_reduce(m16[:, b % 2, :], bK[b % 2][:, :].rearrange("p (a t) -> p a t", t=S),
                                          AX, ALU.max).then_inc(sems["s_max"], 1)

                def second_norm(q):
                    need(dve, "wc_done", i, q + 1)
                    need(dve, "x1_bc", i, q + 1)
                    if q == 0:
                        need(dve, "row_hi", i, 0)
                        need(dve, "row_lo", i, 0)
                        need(dve, "st_acc", i, 0)
                    dve.scalar_tensor_tensor(x2[:, q, :], bW[:, 0:D], W_BACK, x_in[:, q, :], ALU.mult, ALU.add
                                             ).then_inc(sems["ln2_sum"], 1)
                    norm_stats(i, q, "ln2", x2, stat2, mv2)

                def second_normed(a, b):
                    n = {0: 1, 2: 2, 3: 3}[a]
                    need(dve, "ln2_std", i, n)
                    dve.reciprocal(rstd2[:, a:b], std2[:, a:b]).then_inc(sems["ln2_rstd"], 1)
                    need(dve, "ln2_rstd", i, n)
                    for q in range(a, b):
                        dve.tensor_scalar(x2[:, q, :], x2[:, q, :], mv2[:, q, 0:1], rstd2[:, q:q + 1], ALU.subtract,
                                          ALU.mult).then_inc(sems["x2_norm"], 1)

                for step in range(GB + 1):
                    if step == 0:
                        state_masks(0)
                    if step < GB - 1:
                        state_masks(step + 1)
                    if step >= 2 and step % 2 == 0:
                        attention_rows(step // 2 - 1)
                    if step >= 3 and step % 2:
                        attention_lo((step - 3) // 2)
                    if step >= 5 and step % 2:
                        first_norm((step - 5) // 2)
                    if step >= 6 and step % 2 == 0:
                        first_normed(step // 2 - 3)
                x1T_lo(0)
                attention_lo(3)
                first_norm(2)
                score_maxima(0)
                first_normed(2)
                first_norm(3)
                score_maxima(1)
                x1T_lo(1)
                first_normed(3)
                x1T_lo(2)
                for step in range(2, GB + 6):
                    if step == 3:
                        x1T_lo(3)
                    if step < GB:
                        score_maxima(step)
                    if 4 <= step < GB + 4:
                        b = step - 4
                        o = (bN, bP[1])[b % 2][:, 0:2 * NG * (HD + 1)].rearrange("p (a n) -> p a n", n=HD + 1)
                        need(dve, "pv_done", i, b + 1)
                        if b >= 2:
                            need(dve, "pv_norm", i, b - 1)
                        if b == 0:
                            need(dve, "aT", i, 0)
                        dve.reciprocal(rec[:, b % 2, :], o[:, :, HD]).then_inc(sems["pv_rec"], 1)
                        need(dve, "pv_rec", i, b + 1)
                        dve.tensor_tensor(a2[:, b, :].rearrange("p (a d) -> p a d", d=HD), o[:, :, 0:HD],
                                          bc(rec[:, b % 2, :].unsqueeze(2), [P, 2 * NG, HD]), ALU.mult
                                          ).then_inc(sems["pv_norm"], 1)
                    if step >= 6 and step % 2 == 0:
                        q = (step - 6) // 2
                        need(dve, "aT_hi", i, q + 1)
                        if q >= 2:
                            need(dve, "wc_done", i, q - 1)
                        dve.tensor_tensor(aT16[:, q % 2, 1, :, :].rearrange("p e (b s) -> p b e s", b=2),
                                          bT[:, 0:D].rearrange("p (b e s) -> p b e s", b=2, e=2),
                                          aT16[:, q % 2, 0, :, :].rearrange("p e (b s) -> p b e s", b=2), ALU.subtract
                                          ).then_inc(sems["aT_lo"], 1)
                    if step >= 7 and step % 2:
                        second_norm((step - 7) // 2)
                    if step == 12:
                        second_normed(0, 2)
                        second_normed(2, 3)
                second_normed(TQ - 1, TQ)

                for q in range(TQ):
                    need(dve, "x2T", i, q + 1)
                    if q == 0:
                        need(dve, "g_done", i, 0)
                    dve.tensor_copy(x2T16[:, :, :, q * P:(q + 1) * P].rearrange("p s k n -> p (s k) n"),
                                    half((bT, bW)[q % 2])[:, 0:2 * KC * P].rearrange("p (a n) -> p a n", n=P)
                                    ).then_inc(sems["x2T_read"], 1)

                done = [0]

                def link(instruction, alone=False):
                    done[0] += 1
                    instruction.then_inc(sems["r_chain"], 1)
                    if not alone:
                        apart(dve, sems["r_chain"], i * R_CHAIN + done[0])

                def softmax_shift():
                    need(dve, "router", i)
                    link(dve.tensor_scalar(lg[:, :, :], bP[0][:, 0:TQ * (E + 1)].rearrange("p (q e) -> p q e", e=E + 1),
                                           W_BACK, None, ALU.mult))
                    logits = lg[:, :, 0:E]
                    link(dve.tensor_reduce(lg_max[:, :], logits, AX, ALU.max))
                    link(dve.tensor_tensor(shifted[:, :, :], logits, bc(lg_max[:, :].unsqueeze(2), [P, TQ, E]),
                                           ALU.subtract))
                    assert done[0] == R_SHIFT

                def top_experts():
                    need(dve, "r_exp", i, 1)
                    link(dve.tensor_reduce(ex_sum[:, :], ex[:, :, :], AX, ALU.add))
                    link(dve.reciprocal(ex_rec[:, :], ex_sum[:, :]))
                    link(dve.tensor_tensor(prob[:, :, :], ex[:, :, :], bc(ex_rec[:, :].unsqueeze(2), [P, TQ, E]), ALU.mult))
                    for q in range(TQ):
                        link(dve.max(top_v[:, q, :], prob[:, q, :]), alone=q < TQ - 1)
                    for q in range(TQ):
                        link(dve.max_index(top_i[:, q, :], top_v[:, q, :], prob[:, q, :]), alone=q < TQ - 1)
                    link(dve.tensor_copy(top_f[:, :, :], top_i[:, :, 0:TOPK]))
                    link(dve.tensor_tensor(onehot[:, :, :, :].rearrange("p q j e -> p (q j) e"),
                                           bc(top_f[:, :, :].rearrange("p q j -> p (q j)").unsqueeze(2), [P, TQ * TOPK, E]),
                                           bc(const("iota").unsqueeze(1), [P, TQ * TOPK, E]), ALU.is_equal))
                    with nc.allow_low_precision("zeros and ones"):
                        link(dve.tensor_reduce(mask16[:, 0:TQ, :], onehot[:, :, :, :].rearrange("p q j e -> p q e j"),
                                               AX, ALU.add))
                    assert done[0] == R_MASK

                def row_weights():
                    link(dve.tensor_reduce(w_sum[:, :], top_v[:, :, 0:TOPK], AX, ALU.add), alone=True)
                    link(dve.tensor_tensor(chosen[:, :, :], mask16[:, 0:TQ, :], prob[:, :, :], ALU.mult))
                    link(dve.tensor_scalar(w_clip[:, :], w_sum[:, :], TOP_MIN, None, ALU.max))
                    link(dve.reciprocal(w_rec[:, :], w_clip[:, :]))
                    need(dve, "scattered", i, 0)
                    link(dve.tensor_copy(row[:, :, ROW - 1:ROW].bitcast(U32), token[:, :].unsqueeze(2)), alone=True)
                    link(dve.scalar_tensor_tensor(row[:, :, D:D + E], chosen[:, :, :], W_BACK,
                                                  bc(w_rec[:, :].unsqueeze(2), [P, TQ, E]), ALU.mult, ALU.mult))
                    link(dve.tensor_scalar(token[:, :], token[:, :], float(GT), None, ALU.add), alone=True)

                def region_rows():
                    need(dve, "rank", i)
                    link(dve.tensor_tensor(pos[:, :, :], bE[:, 0:TQ * E].rearrange("p (q e) -> p q e", e=E),
                                           bc(count[:, :].unsqueeze(1), [P, TQ, E]), ALU.add))
                    link(dve.tensor_tensor(count[:, :], count[:, :], bE[:, TQ * E:(TQ + 1) * E], ALU.add), alone=True)
                    link(dve.tensor_tensor(pos_sel[:, :, :, :], onehot[:, :, :, :],
                                           bc(pos[:, :, :].unsqueeze(2), [P, TQ, TOPK, E]), ALU.mult))
                    link(dve.tensor_reduce(pos_f[:, :], pos_sel[:, :, :, :].rearrange("p q j e -> p (q j) e"),
                                           AX, ALU.add))
                    link(dve.tensor_copy(pos_u[:, :], pos_f[:, :]))
                    assert done[0] == R_ROWS

                def shared_gates():
                    need(dve, "r_exp", i)
                    link(dve.tensor_scalar(sg_d[:, :], sg_e[:, :], 1.0, W_SCALE, ALU.add, ALU.mult))
                    link(dve.reciprocal(sg[:, :], sg_d[:, :]))

                def padding_places():
                    need(dve, "r_chain", i, R_ROWS)
                    dve.tensor_copy(tab[0:1, TAB_PAD:TAB_PAD + E], count[0:1, :]).then_inc(sems["t_pad"], 1)

                split_expert(i, 0)
                softmax_shift()
                top_experts()
                for c in range(IC + 1):
                    if c < IC:
                        n = chunk_rows(c)
                        if c < IC - 1:
                            up = (bK[1], bN)[c % 2][:, :]
                            need(dve, "u_done", i, c + 1)
                        else:
                            up = (bK[0], bP[1])[c % 2][n:2 * n, :]
                            need(dve, "g_done", i, c + 1)
                        to = slice(0, n) if c < IC - 1 else slice(n, 2 * n)
                        need(dve, "silu", i, c + 1)
                        if c >= 2:
                            need(dve, "h_hi", i, c - 1)
                            need(dve, "h_lo", i, c - 1)
                        dve.scalar_tensor_tensor(h32[0:n, c % 2, :], up, W_BACK, gate[to, c % 2, :], ALU.mult,
                                                 ALU.mult).then_inc(sems["h_mul"], 1)
                    if c >= 1:
                        n = chunk_rows(c - 1)
                        need(dve, "h_hi", i, c)
                        if c == 1:
                            need(dve, "down", i, 0)
                        dve.tensor_tensor(h16[0:n, 1, c - 1, :], h32[0:n, (c - 1) % 2, :], h16[0:n, 0, c - 1, :],
                                          ALU.subtract).then_inc(sems["h_lo"], 1)
                    if c == 0:
                        row_weights()
                    if c == 1:
                        region_rows()
                        if last:
                            padding_places()
                    if c == 2:
                        split_expert(i, 1)
                    if c == 3 and last:
                        expert_tiles()
                    if c == 4:
                        shared_gates()
                    if c == 5 and last:
                        slot_experts()
                if last:
                    slot_rows()
                assert done[0] == R_CHAIN, done[0]
                for q in range(TQ):
                    need(dve, "down", i, q + 1)
                    dve.scalar_tensor_tensor(x2[:, q, :], (bW, bT)[q % 2][:, 0:D], sg[:, q:q + 1], x2[:, q, :],
                                             ALU.mult, ALU.add).then_inc(sems["acc_row"], 1)
                    if q == 0:
                        split_expert(i, 2)
                    if q == 1 and not last:
                        input_lo(i + 1)
                    if q == 1 and last:
                        slot_table()
                split_expert(i, 3)

            with dve.Fori(0, GROUPS - 1) as i:
                group_pass(i, False)
            group_pass(GROUPS - 1, True)

            dve.memset(eh[:, :, :], 0.0)
            def slot_read(j, p):
                dve.wait_ge(slot_sem["xg_T"][p], j + 1)
                dve.wait_ge(slot_sem["e_gu"][p], j)
                dve.tensor_copy(xgT[:, p, :, :], half((bT, bE)[p])[:, 0:2 * KC * P].rearrange("p (a n) -> p a n", n=P)
                                ).then_inc(slot_sem["xg_read"][p], 1)

            def slot_product(j, p):
                dve.wait_ge(slot_sem["e_silu"][p], j + 1)
                dve.wait_ge(slot_sem["e_hT"][p], j)
                dve.scalar_tensor_tensor(eh[:, p, 0:IM], bP[p][:, IM:2 * IM], W_BACK, e_gate[:, p, :], ALU.mult, ALU.mult
                                         ).then_inc(slot_sem["e_mul"][p], 1)

            def slot_meta(j, p, place, first=False):
                if not first:
                    apart(dve, slot_sem["e_yw"][p], j - 1)
                    apart(dve, slot_sem["e_id"][p], j - 1)
                dve.tensor_copy(meta[:, p, place * (E + 1):(place + 1) * (E + 1)].bitcast(U32), xg[:, p, D:ROW].bitcast(U32)
                                ).then_inc(slot_sem["meta"][p], 1)

            def slot_h_lo(j, p):
                dve.wait_ge(slot_sem["e_hhi"][p], j + 1)
                dve.tensor_tensor(ehT[:, p, 1, :, :], bK[p][:, 0:KC * P].rearrange("p (k n) -> p k n", k=KC),
                                  ehT[:, p, 0, :, :], ALU.subtract).then_inc(slot_sem["e_hlo"][p], 1)

            dve.wait_ge(sems["t_tab"], 1)
            laps = slot_turns(dve)
            slot_read(0, 0)
            slot_meta(0, 0, 0, first=True)
            slot_product(0, 0)
            slot_read(0, 1)
            slot_meta(0, 1, 0, first=True)
            slot_h_lo(0, 0)
            slot_product(0, 1)

            def next_pair(j, place):
                slot_read(j + 1, 0)
                slot_meta(j + 1, 0, place)
                slot_h_lo(j, 1)
                slot_product(j + 1, 0)
                slot_read(j + 1, 1)
                slot_meta(j + 1, 1, place)
                slot_h_lo(j + 1, 0)
                slot_product(j + 1, 1)

            with dve.Fori(0, laps) as turn:
                next_pair(2 * turn, 1)
                next_pair(2 * turn + 1, 0)
            next_pair(2 * laps, 1)
            slot_h_lo(2 * laps + 1, 1)

            for g in range(LAST + 2):
                if g < LAST and g % 2 == 0:
                    last_sum(dve, g)
                if 1 <= g <= LAST:
                    dve.wait_ge(sems[f"f_sum{(g - 1) % 2}"], (g + 1) // 2)
                    for q in range(2):
                        dve.bn_stats(fstat[:, g - 1, q, :], fa[:, g - 1, 0, q, :]).then_inc(sems["f_stat"], 1)
                if g >= 2:
                    dve.wait_ge(sems["f_std"], g - 1)
                    dve.reciprocal(frstd[:, g - 2, :], fstd[:, g - 2, :]).then_inc(sems["f_rstd"], 1)
                    dve.wait_ge(sems["f_rstd"], 2 * (g - 2) + 1)
                    dve.scalar_tensor_tensor(fshift[:, g - 2, :], fmv[:, g - 2, :, 0], -1.0, frstd[:, g - 2, :],
                                             ALU.mult, ALU.mult).then_inc(sems["f_rstd"], 1)
                if 1 <= g <= LAST:
                    dve.wait_ge(sems["f_stat"], 2 * g)
                    for q in range(2):
                        dve.bn_aggr(fmv[:, g - 1, q, :], fstat[:, g - 1, q, :]).then_inc(sems["f_mv"], 1)

        @block.gpsimd
        def _(pool):
            pool.memset(c16[:, 0, :, :], 0.0)
            pool.memset(c16[0:C, 1, :, :], 0.0).then_inc(sems["setup"], 1)
            pool.memset(v_stage[:, :, :, :], 0.0).then_inc(sems["setup"], 1)
            pool.memset(zeros[:, :], 0.0).then_inc(sems["setup"], 1)
            pool.memset(pad_row[:, 0:ROW - 1], 0.0)
            pool.memset(pad_row[:, ROW - 1:ROW].bitcast(U32), NO_TOKEN).then_inc(sems["setup"], 1)
            for g in range(2):
                pool.wait_ge(sems["setup"], SETUP - 1)
                w = g * (HD + 1) + HD
                ones = pool.memset(v_stage[g * S:(g + 1) * S, :, :, w:w + 1], 1.0)
            ones.then_inc(sems["setup"], 1)

            def prepare(i):
                need(pool, "ld_x", i)
                pool.tensor_tensor(x_in[:, :, :], x_in[:, :, :], bc(bo_row.unsqueeze(1), [P, TQ, D]), ALU.add
                                   ).then_inc(sems["x_bo"], 1)
                need(pool, "ctx_hi", i)
                need(pool, "ctx_in", i, 0)
                pool.tensor_tensor(c_parts[:, 1, :, :], c_stage[:, :, :], c_parts[:, 0, :, :], ALU.subtract
                                   ).then_inc(sems["ctx_lo"], 1)
                need(pool, "v_hi", i)
                need(pool, "pv_done", i, 0)
                pool.tensor_tensor(v16[:, 1, :, :, :].rearrange("p b g n -> p (b g n)"),
                                   v_stage[:, :, :, :].rearrange("p b g n -> p (b g n)"),
                                   v16[:, 0, :, :, :].rearrange("p b g n -> p (b g n)"), ALU.subtract
                                   ).then_inc(sems["v_lo"], 1)

            prepare(0)

            def group_pass(i, last):
                for q in range(TQ):
                    need(pool, "x1_norm", i, q + 1)
                    need(pool, "ln1_sum", i, q + 1)
                    pool.tensor_tensor(x_in[:, q, :], x1[:, q, :], bc_row, ALU.add).then_inc(sems["x1_bc"], 1)
                for b in range(GB):
                    need(pool, "e_hi", i, b + 1)
                    need(pool, "exp_done", i, b + 1)
                    if b >= 2:
                        need(pool, "pv_done", i, b - 1)
                    pool.tensor_tensor(e16[:, b % 2, 1, :, :], e32[:, b % 2, :, :], e16[:, b % 2, 0, :, :],
                                       ALU.subtract).then_inc(sems["e_lo"], 1)
                for q in range(TQ):
                    need(pool, "row_hi", i, q + 1)
                    pool.tensor_tensor(row16[:, q, D:2 * D], x2[:, q, :], row16[:, q, 0:D], ALU.subtract
                                       ).then_inc(sems["row_lo"], 1)
                if not last:
                    prepare(i + 1)
                need(pool, "r_chain", i, R_ROWS)
                apart(pool, sems["row_lo"], (i + 1) * PER["row_lo"])
                for q in range(TQ):
                    for k in range(TOPK):
                        a = q * TOPK + k
                        pool.indirect_dma_start(xs, bass.IndirectOffsetOnAxis(ap=pos_u[:, a:a + 1], axis=0),
                                                row[:, q, :], None).then_inc(sems["scattered"], 16)

            with pool.Fori(0, GROUPS - 1) as i:
                group_pass(i, False)
            group_pass(GROUPS - 1, True)

            need(pool, "st_acc", GROUPS - 1)
            pool.wait_ge(sems["st_zero"], 16)
            pool.wait_ge(sems["t_tab"], 1)
            laps = slot_turns(pool)
            with pool.Fori(0, 2 * laps + 2) as j:
                for p in range(2):
                    apart(pool, slot_sem["e_add"][p], 16 * j)
                    apart(pool, slot_sem["meta"][p], j + 1)
                    pool.tensor_copy(ids[:, p:p + 1], meta[:, p, bass.ds((j % 2) * (E + 1) + E, 1)].bitcast(U32)
                                     ).then_inc(slot_sem["e_id"][p], 1)
                    apart(pool, slot_sem["e_yw"][p], j + 1)
                    apart(pool, slot_sem["e_id"][p], j + 1)
                    pool.indirect_dma_start(acc[p], bass.IndirectOffsetOnAxis(ap=ids[:, p:p + 1], axis=0), ye[:, p, :],
                                            None, bounds_check=N - 1, oob_is_err=False, compute_op=ALU.add
                                            ).then_inc(slot_sem["e_add"][p], 16)
            for g in range(1, LAST, 2):
                last_sum(pool, g)


R_SHIFT, R_MASK, R_ROWS = 3, 17, 29
T_CHAIN = 16


def constants():
    import numpy as np
    cf = {
        "ident": np.eye(P), "head_mask": np.kron(np.eye(P // HD), np.ones((HD, HD))),
        "attn_eps": (np.float32(ATTN_EPS) / np.exp(-(np.arange(P, dtype=np.float32) % S) / np.float32(S)))[:, None],
        "head_pick": np.kron(np.eye(P // HD), np.ones((HD, 1))),
        "decay_col": np.exp(-(np.arange(P, dtype=np.float32) % S) / np.float32(S))[:, None],
        "slot": np.arange(P)[:, None], "token": np.arange(P)[:, None] + P * np.arange(TQ),
        "ln_eps": np.full((P, 1), LN_EPS), "iota": np.broadcast_to(np.arange(E), (P, E)),
        "region": np.broadcast_to(REGION * np.arange(E), (P, E)),
        "steps": np.broadcast_to(P * np.arange(E), (P, E)),
        "rounds": np.broadcast_to(ROUND + ROUND * np.arange(P // ROUND), (P, P // ROUND)),
        "upto": np.broadcast_to(np.tri(E).reshape(-1), (P, E * E)),
    }
    cf = np.concatenate([cf[name].astype(np.float32) for name in CF_PARTS], axis=1)
    ch = np.concatenate([np.eye(P), np.tri(P, k=-1).T, np.ones((P, P))], axis=1).astype(np.float16)
    pick = np.kron(np.eye(NG), np.ones(S)).astype(np.float16)
    return {"cf": cf, "ch": ch, "pick": np.ascontiguousarray(np.broadcast_to(pick[:, None, :], (NG, GB, NG * S)))}


def kernel(**inputs):
    import numpy as np
    import concourse.bacc as bacc
    from concourse.bass_utils import run_bass_kernel_spmd

    a = {k: np.asarray(v) for k, v in inputs.items()}
    pre = "L0_"

    def chunks(w):
        n = -(-w.shape[0] // P)
        full = np.zeros((n * P, w.shape[1]), w.dtype)
        full[:w.shape[0]] = w
        return full.reshape(n, P, w.shape[1]).transpose(1, 0, 2).reshape(P, -1)

    def by_head(w, axis=-1):
        w = np.moveaxis(w, axis, 0)
        return np.moveaxis(w.reshape(NG, HPG, HD, -1).swapaxes(0, 1).reshape(w.shape), 0, axis)

    wc = by_head(a[pre + "xattn_Wc"].T).reshape(NG, 2, 2, HD, D)
    wc = wc.transpose(2, 1, 0, 3, 4).reshape(D, D)
    sh_gate, sh_up = a[pre + "ffn_sh_gate"], a[pre + "ffn_sh_up"]
    w = [
        chunks(a[pre + "attn_Wq"].T),
        chunks(np.concatenate([a[pre + "attn_Wk"].T, a[pre + "attn_Wv"].T], axis=1)),
        chunks(by_head(a[pre + "attn_Wo"].T)), chunks(wc),
        chunks(by_head(np.concatenate([a[pre + "ffn_router_w"].T, a[pre + "ffn_sh_gate_w"]], axis=1), 0)),
        chunks(by_head(np.concatenate([sh_gate[:, :FULL], sh_up[:, :FULL], sh_gate[:, FULL:], sh_up[:, FULL:]], axis=1),
                       0)),
        chunks(by_head(a[pre + "ffn_sh_down"])),
    ]
    gu = by_head(np.concatenate([a[pre + "ffn_w_gate"], a[pre + "ffn_w_up"]], axis=2), 1)
    down = by_head(a[pre + "ffn_w_down"])
    x = a["x"].reshape(N, D)
    data = {
        "x": by_head(x), "xT": np.ascontiguousarray(x.T).reshape(KC, P, N),
        "ctx": a["ctx_512"], "ctxT": np.ascontiguousarray(a["ctx_512"].transpose(2, 0, 1)),
        "bq": np.ascontiguousarray(a[pre + "attn_bq"].reshape(KC, P).T),
        "biases": np.concatenate([a[pre + "attn_bk"], a[pre + "attn_bv"], by_head(a[pre + "attn_bo"]),
                                  by_head(a[pre + "xattn_bc"])]),
        "w": np.concatenate(w, axis=1),
        "e_w": np.stack([np.concatenate([chunks(gu[e]), chunks(down[e])], axis=1) for e in range(E)]),
        **constants(),
    }
    nc = bacc.Bacc("TRN2", target_bir_lowering=False, num_devices=1)
    args = {k: nc.dram_tensor(f"in_{k}", v.shape, mybir.dt.from_np(v.dtype), kind="ExternalInput").ap()
            for k, v in data.items()}
    out = nc.dram_tensor("out_0", (N, D), F32, kind="ExternalOutput").ap()
    decoder_layer_program(nc, args, out)
    r = run_bass_kernel_spmd(nc, [{f"in_{k}": v for k, v in data.items()}], core_ids=[0])
    by_group = r.results[0]["out_0"].reshape(N, HPG, NG, HD).swapaxes(1, 2)
    return np.ascontiguousarray(by_group).reshape(B, S, D)
```
